# Optimizing a Trainium2 kernel written in Bass

```python
import numpy as np
import jax
import jax.numpy as jnp

def _softmax(x, axis=-1):
    return jax.nn.softmax(x, axis=axis)

def _gelu(x):
    return jax.nn.gelu(x, approximate=True)

def _silu(x):
    return jax.nn.silu(x)

def _sigmoid(x):
    return jax.nn.sigmoid(x)

def _layernorm(x, axis=-1, eps=1e-05):
    m = jnp.mean(x, axis=axis, keepdims=True)
    v = jnp.var(x, axis=axis, keepdims=True)
    return (x - m) / jnp.sqrt(v + eps)

def _scatter_add(tgt, idx, src, axis=0):
    return tgt.at[idx].add(src)

def _segment_sum(src, seg, n):
    return jax.ops.segment_sum(src, seg, n)
kernel_name = 'mk_prb_d2_jaxref_r8_2960ca'

def setup_inputs(seed: int=0):
    np.random.seed(seed)
    _w = jnp.asarray

    def _L0_attn_setup():
        import jax, jax.numpy as jnp
        import numpy as np
        BATCH, SEQ, HIDDEN = (2, 512, 512)
        HEADS, HEAD_DIM, BLOCK = (32, 128, 32)
        LAYER_IDX, N_LAYERS = (1, 32)
        EPS = 1e-05

        def _decays():
            base = 1.0 / 2.0 ** (8.0 / HEADS)
            exponent = jnp.arange(HEADS, dtype=jnp.float32) + 1.0
            factor = 1.0 - LAYER_IDX / (N_LAYERS - 1 + 1e-05) + 1e-05
            slope = (base ** exponent * factor)[:, None, None]
            r = jnp.arange(BLOCK, dtype=jnp.float32) + 1.0
            q_decay = jnp.exp(-slope * r[:, None])
            k_decay = jnp.exp(-slope * (BLOCK - r)[:, None])
            diff = r[:, None] - r[None, :]
            diag = slope[None] * diff[None, None]
            diag = jnp.where(diag >= 0, -diag, -jnp.inf)
            diag_decay = jnp.exp(diag)
            block_decay = jnp.exp(-slope * BLOCK)
            return (q_decay, k_decay, diag_decay, block_decay)
        key = jax.random.key(seed)
        ks = jax.random.split(key, 5)
        s = 0.02
        return {'hidden_states': jax.random.normal(ks[0], (BATCH, SEQ, HIDDEN), jnp.float32), 'qkv_w': jax.random.normal(ks[1], (3 * HEADS * HEAD_DIM, HIDDEN), jnp.float32) * s, 'out_w': jax.random.normal(ks[2], (HIDDEN, HEADS * HEAD_DIM), jnp.float32) * s, 'gate_w': jax.random.normal(ks[3], (HEADS * HEAD_DIM, HIDDEN), jnp.float32) * s, 'norm_w': jnp.ones((HEADS * HEAD_DIM,), jnp.float32)}
    _L0_attn_in = _L0_attn_setup()

    def _L0_ffn_setup():
        import jax, jax.numpy as jnp
        import numpy as np
        DIM = 512
        INTER = 128
        E = 16
        GROUPS = 4
        LIM = 2
        K = 2
        SHARED_INTER = 2 * INTER
        SCALE = 1.0
        key = jax.random.key(seed)
        ks = jax.random.split(key, 16)

        def n(k, shape, s=0.02):
            return jax.random.normal(k, shape, jnp.float32) * s
        return {'x': jax.random.normal(ks[0], (1, 256, DIM), jnp.float32), 'router_w': n(ks[1], (DIM, E)), 'router_b': n(ks[2], (E,)), 'router_bias': n(ks[3], (E,), 1.0), 'ew1': n(ks[4], (E, DIM, INTER)), 'eb1': n(ks[5], (E, INTER)), 'ew2': n(ks[6], (E, DIM, INTER)), 'eb2': n(ks[7], (E, INTER)), 'ew3': n(ks[8], (E, INTER, DIM)), 'eb3': n(ks[9], (E, DIM)), 'sw1': n(ks[10], (DIM, SHARED_INTER)), 'sb1': n(ks[11], (SHARED_INTER,)), 'sw2': n(ks[12], (DIM, SHARED_INTER)), 'sb2': n(ks[13], (SHARED_INTER,)), 'sw3': n(ks[14], (SHARED_INTER, DIM)), 'sb3': n(ks[15], (DIM,))}
    _L0_ffn_in = _L0_ffn_setup()

    def _L1_attn_setup():
        import jax, jax.numpy as jnp
        import numpy as np
        H = 512
        D = H // 4
        key = jax.random.key(seed)
        k1, k2, k3, k4, k5 = jax.random.split(key, 5)
        x = jax.random.normal(k1, (4, 512, H), dtype=jnp.float32)
        s_in = 1.0 / np.sqrt(H)
        Wqkv = jax.random.normal(k2, (H, 3 * D), dtype=jnp.float32) * s_in
        bqkv = jax.random.normal(k3, (3 * D,), dtype=jnp.float32) * 0.01
        Wo = jax.random.normal(k4, (D, H), dtype=jnp.float32) * (1.0 / np.sqrt(D))
        bo = jax.random.normal(k5, (H,), dtype=jnp.float32) * 0.01
        return {'x': x, 'Wqkv': Wqkv, 'bqkv': bqkv, 'Wo': Wo, 'bo': bo}
    _L1_attn_in = _L1_attn_setup()

    def _L1_ffn_setup():
        import jax, jax.numpy as jnp
        import numpy as np
        BATCH, SEQ, D = (2, 256, 512)
        K, TOPK, RANK = (64, 16, 16)
        ALPHA = 32.0
        SCALING = ALPHA / RANK
        key = jax.random.key(seed)
        k1, k2, k3, k4 = jax.random.split(key, 4)
        x = jax.random.normal(k1, (BATCH, SEQ, D), dtype=jnp.float32)
        A = jax.random.normal(k2, (K, RANK, D), dtype=jnp.float32) * 0.02
        B = jax.random.normal(k3, (K, D, RANK), dtype=jnp.float32) * 0.02
        Wr = jax.random.normal(k4, (K, D), dtype=jnp.float32) * 0.02
        return {'x': x, 'A': A, 'B': B, 'Wr': Wr}
    _L1_ffn_in = _L1_ffn_setup()
    _d = {'L0_attn_hidden_states': _L0_attn_in['hidden_states'], 'L0_attn_qkv_w': _L0_attn_in['qkv_w'], 'L0_attn_out_w': _L0_attn_in['out_w'], 'L0_attn_gate_w': _L0_attn_in['gate_w'], 'L0_attn_norm_w': _L0_attn_in['norm_w'], 'L0_ffn_router_w': _L0_ffn_in['router_w'], 'L0_ffn_router_b': _L0_ffn_in['router_b'], 'L0_ffn_router_bias': _L0_ffn_in['router_bias'], 'L0_ffn_ew1': _L0_ffn_in['ew1'], 'L0_ffn_eb1': _L0_ffn_in['eb1'], 'L0_ffn_ew2': _L0_ffn_in['ew2'], 'L0_ffn_eb2': _L0_ffn_in['eb2'], 'L0_ffn_ew3': _L0_ffn_in['ew3'], 'L0_ffn_eb3': _L0_ffn_in['eb3'], 'L0_ffn_sw1': _L0_ffn_in['sw1'], 'L0_ffn_sb1': _L0_ffn_in['sb1'], 'L0_ffn_sw2': _L0_ffn_in['sw2'], 'L0_ffn_sb2': _L0_ffn_in['sb2'], 'L0_ffn_sw3': _L0_ffn_in['sw3'], 'L0_ffn_sb3': _L0_ffn_in['sb3'], 'L1_attn_Wqkv': _L1_attn_in['Wqkv'], 'L1_attn_bqkv': _L1_attn_in['bqkv'], 'L1_attn_Wo': _L1_attn_in['Wo'], 'L1_attn_bo': _L1_attn_in['bo'], 'L1_ffn_A': _L1_ffn_in['A'], 'L1_ffn_B': _L1_ffn_in['B'], 'L1_ffn_Wr': _L1_ffn_in['Wr']}
    _x0 = _d['L0_attn_hidden_states']
    _d['L0_attn_hidden_states'] = jax.random.normal(jax.random.fold_in(jax.random.key(seed), 1), (8, 256, 512), dtype=_x0.dtype)
    del _x0
    return _d

def reference(L0_attn_hidden_states, L0_attn_qkv_w, L0_attn_out_w, L0_attn_gate_w, L0_attn_norm_w, L0_ffn_router_w, L0_ffn_router_b, L0_ffn_router_bias, L0_ffn_ew1, L0_ffn_eb1, L0_ffn_ew2, L0_ffn_eb2, L0_ffn_ew3, L0_ffn_eb3, L0_ffn_sw1, L0_ffn_sb1, L0_ffn_sw2, L0_ffn_sb2, L0_ffn_sw3, L0_ffn_sb3, L1_attn_Wqkv, L1_attn_bqkv, L1_attn_Wo, L1_attn_bo, L1_ffn_A, L1_ffn_B, L1_ffn_Wr):

    def _L0_attn_ref(hidden_states, qkv_w, out_w, gate_w, norm_w):
        import jax, jax.numpy as jnp
        import numpy as np
        BATCH, SEQ, HIDDEN = (2, 512, 512)
        HEADS, HEAD_DIM, BLOCK = (32, 128, 32)
        LAYER_IDX, N_LAYERS = (1, 32)
        EPS = 1e-05

        def _decays():
            base = 1.0 / 2.0 ** (8.0 / HEADS)
            exponent = jnp.arange(HEADS, dtype=jnp.float32) + 1.0
            factor = 1.0 - LAYER_IDX / (N_LAYERS - 1 + 1e-05) + 1e-05
            slope = (base ** exponent * factor)[:, None, None]
            r = jnp.arange(BLOCK, dtype=jnp.float32) + 1.0
            q_decay = jnp.exp(-slope * r[:, None])
            k_decay = jnp.exp(-slope * (BLOCK - r)[:, None])
            diff = r[:, None] - r[None, :]
            diag = slope[None] * diff[None, None]
            diag = jnp.where(diag >= 0, -diag, -jnp.inf)
            diag_decay = jnp.exp(diag)
            block_decay = jnp.exp(-slope * BLOCK)
            return (q_decay, k_decay, diag_decay, block_decay)
        b, s, _ = hidden_states.shape
        h, d, bs = (HEADS, HEAD_DIM, BLOCK)
        nb = s // bs
        q_decay, k_decay, diag_decay, block_decay = _decays()
        qkv = jax.nn.silu(hidden_states @ qkv_w.T)
        qkv = qkv.reshape(b, s, h, 3, d)
        q = jnp.moveaxis(qkv[:, :, :, 0], 2, 1)
        k = jnp.moveaxis(qkv[:, :, :, 1], 2, 1)
        v = jnp.moveaxis(qkv[:, :, :, 2], 2, 1)

        def to_blocks(x):
            return jnp.moveaxis(x.reshape(b, h, nb, bs, d), 2, 0)
        qb, kb, vb = (to_blocks(q), to_blocks(k), to_blocks(v))

        def step(kv, blk):
            cq, ck, cv = blk
            scores = jnp.einsum('bhnd,bhmd->bhnm', cq, ck) * diag_decay
            intra = jnp.einsum('bhnm,bhmd->bhnd', scores, cv)
            inter = jnp.einsum('bhnd,bhde->bhne', cq * q_decay, kv)
            kv_next = kv * block_decay + jnp.einsum('bhnd,bhne->bhde', ck * k_decay, cv)
            return (kv_next, intra + inter)
        kv0 = jnp.zeros((b, h, d, d), hidden_states.dtype)
        _, out_blocks = jax.lax.scan(step, kv0, (qb, kb, vb))
        attn = jnp.moveaxis(out_blocks, 0, 2)
        attn = attn.reshape(b, h, s, d).transpose(0, 2, 1, 3).reshape(b, s, h * d)
        xf = attn.astype(jnp.float32)
        xf = xf * jax.lax.rsqrt(jnp.mean(xf * xf, axis=-1, keepdims=True) + EPS)
        normed = norm_w * xf.astype(attn.dtype)
        gate = jax.nn.sigmoid(hidden_states @ gate_w.T)
        return gate * normed @ out_w.T

    def _L0_ffn_ref(x, router_w, router_b, router_bias, ew1, eb1, ew2, eb2, ew3, eb3, sw1, sb1, sw2, sb2, sw3, sb3):
        import jax, jax.numpy as jnp
        import numpy as np
        DIM = 512
        INTER = 128
        E = 16
        GROUPS = 4
        LIM = 2
        K = 2
        SHARED_INTER = 2 * INTER
        SCALE = 1.0
        shape = x.shape
        xt = x.reshape(-1, DIM)
        T = xt.shape[0]
        logits = xt @ router_w + router_b
        scores = jax.nn.softmax(logits.astype(jnp.float32), axis=-1) + router_bias
        g = scores.reshape(T, GROUPS, E // GROUPS)
        _, gidx = jax.lax.top_k(g.max(axis=-1), LIM)
        keep = jnp.zeros((T, GROUPS), bool).at[jnp.arange(T)[:, None], gidx].set(True)
        masked = jnp.where(keep[:, :, None], g, -jnp.inf).reshape(T, E)
        _, idx = jax.lax.top_k(masked, K)
        vals = (jnp.take_along_axis(scores, idx, axis=1) * SCALE).astype(x.dtype)
        gate = jnp.zeros((T, E), x.dtype).at[jnp.arange(T)[:, None], idx].add(vals)

        def step(y, p):
            w1, b1, w2, b2, w3, b3, ge = p
            h = jax.nn.silu(xt @ w1 + b1) * (xt @ w2 + b2)
            return (y + ge[:, None] * (h @ w3 + b3), None)
        y, _ = jax.lax.scan(step, jnp.zeros_like(xt), (ew1, eb1, ew2, eb2, ew3, eb3, gate.T))
        z = jax.nn.silu(xt @ sw1 + sb1) * (xt @ sw2 + sb2) @ sw3 + sb3
        return (y + z).reshape(shape)

    def _L1_attn_ref(x, Wqkv, bqkv, Wo, bo):
        import jax, jax.numpy as jnp
        import numpy as np
        H = 512
        D = H // 4
        B, S, C = x.shape
        d = C // 4
        qkv = jnp.einsum('bsc,cf->bsf', x, Wqkv) + bqkv
        qkv = qkv.reshape(B, S, 3, d)
        q, k, v = (qkv[:, :, 0], qkv[:, :, 1], qkv[:, :, 2])
        scale = 1.0 / jnp.sqrt(jnp.float32(d)).astype(x.dtype)
        attn = jnp.einsum('bqd,bkd->bqk', q, k) * scale
        attn = jax.nn.softmax(attn, axis=-1)
        out = jnp.einsum('bqk,bkd->bqd', attn, v)
        return jnp.einsum('bqd,dc->bqc', out, Wo) + bo

    def _L1_ffn_ref(x, A, B, Wr):
        import jax, jax.numpy as jnp
        import numpy as np
        BATCH, SEQ, D = (2, 256, 512)
        K, TOPK, RANK = (64, 16, 16)
        ALPHA = 32.0
        SCALING = ALPHA / RANK
        prefix = x.shape[:-1]
        xf = x.reshape(-1, x.shape[-1])
        N = xf.shape[0]
        scores = xf @ Wr.T
        top_vals, top_idx = jax.lax.top_k(scores, TOPK)
        gates = jax.nn.softmax(top_vals, axis=-1)
        G = jnp.zeros((N, K), xf.dtype).at[jnp.arange(N)[:, None], top_idx].set(gates)
        h = jnp.einsum('nd,krd->nkr', xf, A)
        out = jnp.einsum('nkr,kdr->nd', h * G[:, :, None], B)
        return (out * SCALING).reshape(*prefix, -1)
    x = L0_attn_hidden_states
    xn = _layernorm(x, axis=-1)
    x = x + _L0_attn_ref(xn, L0_attn_qkv_w, L0_attn_out_w, L0_attn_gate_w, L0_attn_norm_w) + _L0_ffn_ref(xn, L0_ffn_router_w, L0_ffn_router_b, L0_ffn_router_bias, L0_ffn_ew1, L0_ffn_eb1, L0_ffn_ew2, L0_ffn_eb2, L0_ffn_ew3, L0_ffn_eb3, L0_ffn_sw1, L0_ffn_sb1, L0_ffn_sw2, L0_ffn_sb2, L0_ffn_sw3, L0_ffn_sb3)
    xn = _layernorm(x, axis=-1)
    x = x + _L1_attn_ref(xn, L1_attn_Wqkv, L1_attn_bqkv, L1_attn_Wo, L1_attn_bo) + _L1_ffn_ref(xn, L1_ffn_A, L1_ffn_B, L1_ffn_Wr)
    return x

_drawn_inputs = setup_inputs


def setup_inputs(seed=0):
    import zlib

    import numpy as np

    out = dict(_drawn_inputs(seed))
    spreads = {'L0_attn_norm_w': (1.0, 0.2)}
    factors = {'L0_ffn_router_w': 8.0,
     'L0_ffn_router_b': 188.473,
     'L0_ffn_eb1': 8.0,
     'L0_ffn_eb2': 8.0,
     'L0_ffn_sb1': 34.896,
     'L0_ffn_sb2': 34.097,
     'L0_ffn_sb3': 2.806,
     'L1_attn_bqkv': 6.473,
     'L1_attn_bo': 7.254,
     'L1_ffn_A': 3.648,
     'L1_ffn_B': 3.499,
     'L1_ffn_Wr': 4.041}
    for name, (base, spread) in spreads.items():
        noise = np.random.default_rng([zlib.crc32(name.encode()), seed]).standard_normal(out[name].shape)
        drawn = base * np.exp(spread * noise) if base else spread * noise
        out[name] = jnp.asarray(drawn.astype(out[name].dtype))
    for name, factor in factors.items():
        out[name] = (out[name] * factor).astype(out[name].dtype)
    return out
```

```python
from contextlib import ExitStack

import numpy as np

import concourse.bass as bass
from concourse import mybir

F32 = mybir.dt.float32
F32R = mybir.dt.float32r
ALU = mybir.AluOpType
ACT = mybir.ActivationFunctionType
AX_X = mybir.AxisListType.X

P = 128
B, S, D = 8, 256, 512
T = B * S
NT = T // P
KC = D // P
GT = 512
NG = T // GT
TPG = GT // P
EPS = 1e-5
H, DH, BLOCK = 32, 128, 32
NP_ = H // 2
SEC = KC * P
NSEC = 6
WCOLS = NSEC * SEC + 2 * SEC
OCOLS = 2 * D
FILLS = 8
MC = S + P
E, INTER, GROUPS = 16, 128, 4
NE = E + 2
XCOLS = 3 * SEC + 2
K1, RANK, TOPK = 64, 16, 16
NR = K1 * RANK // P
NEG = -3.0e38


class Chain:

    def __init__(self, eng, sem):
        self.eng, self.sem, self.n = eng, sem, 0

    def link(self, ins):
        self.n += 1
        ins.then_inc(self.sem, 1)
        self.eng.wait_ge(self.sem, self.n)


def layernorm_transposed(nc, name, x_at, xn_at, x_ready, xh, xl, ident, extra_sync=None, extra_pool=None):
    with ExitStack() as ctx:
        def sem(n):
            return ctx.enter_context(nc.semaphore(f"{name}_{n}"))

        stat = ctx.enter_context(nc.sbuf_tensor(f"{name}_stat", [P, TPG, 6], F32))
        mv = ctx.enter_context(nc.sbuf_tensor(f"{name}_mv", [P, NG, TPG, 2], F32))
        var = ctx.enter_context(nc.sbuf_tensor(f"{name}_var", [P, NG, TPG], F32))
        root = ctx.enter_context(nc.sbuf_tensor(f"{name}_root", [P, NG, TPG], F32))
        rstd = ctx.enter_context(nc.sbuf_tensor(f"{name}_rstd", [P, NG, TPG], F32))
        ps = [ctx.enter_context(nc.psum_tensor(f"{name}_ps{i}", [P, GT], F32)) for i in range(8)]
        v_chain, v_var, a_root, v_xn, pe_xt, a_hi, v_lo = (
            sem(n) for n in ("v_chain", "v_var", "a_root", "v_xn", "pe_xt", "a_hi", "v_lo"))
        block = ctx.enter_context(nc.Block())

        if extra_sync:
            block.sync(extra_sync)
        if extra_pool:
            block.gpsimd(extra_pool)

        @block.vector
        def _(v):
            c = Chain(v, v_chain)

            def normalise(g):
                x_ready(v, g)
                for t in range(TPG):
                    ins = v.bn_stats(stat[:, t, :], x_at(g * TPG + t))
                c.link(ins)
                for t in range(TPG):
                    ins = v.bn_aggr(mv[:, g, t, :], stat[:, t, :])
                c.link(ins)
                v.tensor_scalar(var[:, g, :], mv[:, g, :, 1], EPS, None, ALU.add).then_inc(v_var, 1)
                v.wait_ge(a_root, g + 1)
                c.link(v.reciprocal(rstd[:, g, :], root[:, g, :]))
                c.link(v.tensor_tensor(rstd[:, g, :], rstd[:, g, :], var[:, g, :], ALU.mult))
                c.link(v.tensor_tensor(root[:, g, :], root[:, g, :], rstd[:, g, :], ALU.add))
                c.link(v.tensor_scalar(root[:, g, :], root[:, g, :], 0.5, None, ALU.mult))
                c.link(v.reciprocal(rstd[:, g, :], root[:, g, :]))
                if g >= 2:
                    v.wait_ge(pe_xt, KC * (g - 1))
                for t in range(TPG):
                    ins = v.tensor_scalar(xn_at(g * TPG + t), x_at(g * TPG + t), mv[:, g, t, 0:1],
                                          rstd[:, g, t:t + 1], ALU.subtract, ALU.mult)
                ins.then_inc(v_xn, 1)

            def low(g):
                for k in range(KC):
                    n = g * KC + k
                    v.wait_ge(a_hi, n + 1)
                    v.tensor_tensor(xl[:, k, g * GT:(g + 1) * GT], ps[n % 8][:],
                                    xh[:, k, g * GT:(g + 1) * GT].bitcast(F32), ALU.subtract).then_inc(v_lo, 1)

            for g in range(NG):
                normalise(g)
                if g:
                    low(g - 1)
            low(NG - 1)

        @block.scalar
        def _(a):
            def roots(g):
                a.wait_ge(v_var, g + 1)
                a.activation(root[:, g, :], var[:, g, :], ACT.Sqrt).then_inc(a_root, 1)

            roots(0)
            for g in range(NG):
                if g + 1 < NG:
                    roots(g + 1)
                for k in range(KC):
                    a.wait_ge(pe_xt, g * KC + k + 1)
                    a.copy(xh[:, k, g * GT:(g + 1) * GT], ps[(g * KC + k) % 8][:]).then_inc(a_hi, 1)

        @block.tensor
        def _(pe):
            for g in range(NG):
                pe.wait_ge(v_xn, g + 1)
                for k in range(KC):
                    n = g * KC + k
                    if n >= 8:
                        pe.wait_ge(v_lo, n - 7)
                    for t in range(TPG):
                        ins = pe.transpose(ps[n % 8][:, t * P:(t + 1) * P],
                                           xn_at(g * TPG + t)[:, k * P:(k + 1) * P], ident[:])
                    ins.then_inc(pe_xt, 1)


def three_passes(pe, out, parts, start, stop):
    n = len(parts)
    for i, (wh, wl, mh, ml) in enumerate(parts):
        pe.matmul(out, wh, mh, start=start and i == 0, stop=False)
        pe.matmul(out, wh, ml, start=False, stop=False)
        ins = pe.matmul(out, wl, mh, start=False, stop=stop and i == n - 1)
    return ins


def two_layers(nc, x, w_pairs, o_pairs, decay, norm_w, router_w, router_b, router_bias, earlier, ex, b3, w_qkv,
               b_qkv, w_o, b_o, w_r, w_a, w_b, sel, ident_in, out):
    x_tiles = x.rearrange("b (s p) d -> (b s) p d", p=P)
    out_tiles = out.rearrange("b (s p) d -> (b s) p d", p=P)
    with ExitStack() as top:
        ident = top.enter_context(nc.sbuf_tensor("ident", [P, P], F32))
        acc = top.enter_context(nc.sbuf_tensor("acc", [P, NT, D], F32))
        with ExitStack() as layer0:
            xh = layer0.enter_context(nc.sbuf_tensor("xh", [P, KC, T], F32R))
            xl = layer0.enter_context(nc.sbuf_tensor("xl", [P, KC, T], F32R))
            sqacc = layer0.enter_context(nc.sbuf_tensor("sqacc", [P, T], F32))
            with ExitStack() as ctx:
                lightning_attention(nc, ctx, x_tiles, w_pairs, o_pairs, decay, norm_w, ident_in, ident, xh, xl, acc,
                                    sqacc)
            with ExitStack() as ctx:
                experts(nc, ctx, x_tiles, router_w, router_b, router_bias, earlier, ex, b3, ident, xh, xl, acc, sqacc)
        with ExitStack() as ctx:
            layer_one(nc, ctx, w_qkv, b_qkv, w_o, b_o, w_r, w_a, w_b, sel, ident, acc, out_tiles)


def lightning_attention(nc, ctx, x_tiles, w_pairs, o_pairs, decay, norm_w, ident_in, ident, xh, xl, acc, sqacc):
    def sb(name, shape, dt=F32):
        return ctx.enter_context(nc.sbuf_tensor(name, shape, dt))

    def sem(name):
        return ctx.enter_context(nc.semaphore(name))

    wh = sb("wh", [P, WCOLS], F32R)
    wl = sb("wl", [P, WCOLS], F32R)
    oh = sb("oh", [P, OCOLS], F32R)
    ol = sb("ol", [P, OCOLS], F32R)
    wraw = sb("wraw", [P, WCOLS])
    oraw = sb("oraw", [P, OCOLS])
    draw = sb("draw", [P, 2, MC])
    dcur = sb("dcur", [P, 2, MC])
    nw = sb("nw", [P, H])
    nwcur = sb("nwcur", [P, 2])
    qT = sb("qT", [P, 2, GT])
    kT = sb("kT", [P, 2, GT])
    gT = sb("gT", [P, 2, GT])
    vt = sb("vt", [P, TPG, 2 * DH])
    ms = [sb(f"ms{i}", [P, MC]) for i in range(2)]
    yf = [sb(f"yf{i}", [P, GT]) for i in range(2)]
    yh = [sb(f"yh{i}", [P, GT], F32R) for i in range(2)]
    yl = [sb(f"yl{i}", [P, GT], F32R) for i in range(2)]
    sq = [sb(f"sq{i}", [P, GT]) for i in range(2)]

    s_x = [sem(f"dma_x{g}") for g in range(NG)]
    s_c = sem("dma_consts")
    dma_w, dma_o, dma_d = sem("dma_w"), sem("dma_o"), sem("dma_d")
    w_hi, w_lo, o_hi, o_lo = sem("w_hi"), sem("w_lo"), sem("o_hi"), sem("o_lo")
    nw_ready = sem("nw_ready")

    def section(j):
        return slice(j * SEC, (j + 1) * SEC)

    def load_pair(sp, p):
        sp.dma_start(wraw[:], w_pairs[p]).then_inc(dma_w, 16)
        sp.dma_start(oraw[:], o_pairs[p]).then_inc(dma_o, 16)
        sp.dma_start(draw[:], decay[p]).then_inc(dma_d, 16)

    def load_first(sp):
        sp.dma_start(ident[:], ident_in).then_inc(s_c, 16)
        sp.dma_start(nw[:], norm_w).then_inc(s_c, 16)
        for g in range(NG):
            for t in range(TPG):
                sp.dma_start(acc[:, g * TPG + t, :], x_tiles[g * TPG + t]).then_inc(s_x[g], 16)
        load_pair(sp, 0)

    def split_first(pool):
        pool.wait_ge(s_c, 32)
        pool.tensor_scalar(nw[:], nw[:], 0.5, None, ALU.mult).then_inc(nw_ready, 1)
        pool.wait_ge(dma_w, 16)
        for j in range(FILLS):
            c = section(j)
            pool.tensor_copy(wh[:, c], wraw[:, c]).then_inc(w_hi, 1)
            pool.wait_ge(w_hi, j + 1)
            pool.tensor_tensor(wl[:, c], wraw[:, c], wh[:, c].bitcast(F32), ALU.subtract).then_inc(w_lo, 1)
        pool.wait_ge(dma_o, 16)
        for j in range(2):
            c = slice(j * D, (j + 1) * D)
            pool.tensor_copy(oh[:, c], oraw[:, c]).then_inc(o_hi, 1)
            pool.wait_ge(o_hi, j + 1)
            pool.tensor_tensor(ol[:, c], oraw[:, c], oh[:, c].bitcast(F32), ALU.subtract).then_inc(o_lo, 1)

    def x_ready(v, g):
        if g == 0:
            v.wait_ge(s_c, 32)
        v.wait_ge(s_x[g], 16 * TPG)

    layernorm_transposed(nc, "ln0", lambda t: acc[:, t, :], lambda t: acc[:, t, :], x_ready, xh, xl, ident,
                         load_first, split_first)

    with ExitStack() as inner:
        def ps(name):
            return inner.enter_context(nc.psum_tensor(name, [P, GT], F32))

        pj = [ps(f"proj{i}") for i in range(2)]
        sc = [ps(f"score{i}") for i in range(2)]
        ot = [ps(f"attnout{i}") for i in range(2)]
        op = [ps(f"outproj{i}") for i in range(2)]
        pe_proj, pe_s, pe_av, pe_out = sem("pe_proj"), sem("pe_s"), sem("pe_av"), sem("pe_out")
        a_ev, a_sq, a_yh = sem("a_ev"), sem("a_sq"), sem("a_yh")
        v_dec, v_mask, v_y, v_yl, v_acc, p_zero, p_sq = (
            sem(n) for n in ("v_dec", "v_mask", "v_y", "v_yl", "v_acc", "p_zero", "p_sq"))
        block = inner.enter_context(nc.Block())

        def all_steps(eng, run):
            run(-1, NG - 1, False, True, False)
            with eng.Fori(0, NP_ - 1) as p:
                for g in range(NG):
                    run(p, g, True, True, True)
            for g in range(NG):
                run(NP_ - 1, g, True, g + 1 < NG, False)

        @block.sync
        def _(sp):
            with sp.Fori(1, NP_) as p:
                sp.wait_ge(w_lo, p * FILLS)
                sp.dma_start(wraw[:], w_pairs[p]).then_inc(dma_w, 16)
                sp.wait_ge(v_dec, p)
                sp.dma_start(draw[:], decay[p]).then_inc(dma_d, 16)
                sp.wait_ge(o_lo, p * 2)
                sp.dma_start(oraw[:], o_pairs[p]).then_inc(dma_o, 16)

        @block.tensor
        def _(pe):
            def project_head(pn, gn, fill, j):
                if gn == 0:
                    pe.wait_ge(w_lo, pn * FILLS + j + 1)
                if not isinstance(fill, int) or fill > 1:
                    pe.wait_ge(a_ev, fill - 1)
                parts = []
                m = slice(gn * GT, (gn + 1) * GT)
                for k in range(KC):
                    c = slice(j * SEC + k * P, j * SEC + (k + 1) * P)
                    parts.append((wh[:, c], wl[:, c], xh[:, k, m], xl[:, k, m]))
                three_passes(pe, pj[j % 2][:], parts, True, True).then_inc(pe_proj, 1)

            def project_v(pn, gn, fill, j):
                if gn == 0:
                    pe.wait_ge(w_lo, pn * FILLS + FILLS)
                pe.wait_ge(a_ev, fill - 1)
                for i in range(2):
                    tok = gn * GT + ((j - NSEC) * 2 + i) * P
                    parts = []
                    for k in range(KC):
                        c = slice(NSEC * SEC + k * 2 * P, NSEC * SEC + (k + 1) * 2 * P)
                        parts.append((xh[:, k, tok:tok + P], xl[:, k, tok:tok + P], wh[:, c], wl[:, c]))
                    ins = three_passes(pe, pj[j % 2][:, i * 2 * P:(i + 1) * 2 * P], parts, True, True)
                ins.then_inc(pe_proj, 1)

            def scores(u, i):
                h, s0 = i // 2, (i % 2) * S
                if i == 0:
                    pe.wait_ge(a_ev, u * FILLS + FILLS)
                pe.matmul(sc[i % 2][:, 0:S], kT[:, h, s0:s0 + P], qT[:, h, s0:s0 + S], start=True, stop=True)
                pe.matmul(sc[i % 2][:, S:MC], kT[:, h, s0 + P:s0 + S], qT[:, h, s0 + P:s0 + S],
                          start=True, stop=True).then_inc(pe_s, 1)

            def values(u, i):
                h, b = i // 2, i % 2
                pe.wait_ge(v_mask, u * 4 + i + 1)
                c = slice(h * DH, (h + 1) * DH)
                pe.matmul(ot[h][:, b * S:(b + 1) * S], vt[:, 2 * b, c], ms[i % 2][:, 0:S], start=True, stop=False)
                pe.matmul(ot[h][:, b * S + P:(b + 1) * S], vt[:, 2 * b + 1, c], ms[i % 2][:, S:MC],
                          start=False, stop=True).then_inc(pe_av, 1)

            def project_out(p, g, u):
                if g == 0:
                    pe.wait_ge(o_lo, p * 2 + 2)
                pe.wait_ge(v_yl, u * 2 + 2)
                for t in range(TPG):
                    if t >= 2:
                        pe.wait_ge(v_acc, u * TPG + t - 1)
                    m = slice(t * P, (t + 1) * P)
                    parts = [(yh[h][:, m], yl[h][:, m], oh[:, h * D:(h + 1) * D], ol[:, h * D:(h + 1) * D])
                             for h in range(2)]
                    three_passes(pe, op[t % 2][:], parts, True, True).then_inc(pe_out, 1)

            def run(p, g, attend, project, more):
                u = p * NG + g
                pn, gn = (p, g + 1) if g + 1 < NG else (p + 1, 0)
                for what, i in (("s", 0), ("s", 1), ("p", 0), ("a", 0), ("a", 1), ("p", 1), ("s", 2), ("s", 3),
                                ("p", 2), ("a", 2), ("a", 3), ("p", 3), ("p", 4), ("p", 5), ("v", 6), ("v", 7)):
                    if what == "s" and attend:
                        scores(u, i)
                    if what == "a" and attend:
                        values(u, i)
                    if what == "p" and project:
                        project_head(pn, gn, (u + 1) * FILLS + i, i)
                    if what == "v" and project:
                        project_v(pn, gn, (u + 1) * FILLS + i, i)
                if attend:
                    project_out(p, g, u)

            all_steps(pe, run)

        @block.scalar
        def _(a):
            dst = [qT[:, 0, :], kT[:, 0, :], gT[:, 0, :], qT[:, 1, :], kT[:, 1, :], gT[:, 1, :],
                   vt[:, 0:2, :].rearrange("p t c -> p (t c)"), vt[:, 2:4, :].rearrange("p t c -> p (t c)")]

            def evacuate(u, j, attend):
                a.wait_ge(pe_proj, (u + 1) * FILLS + j + 1)
                gate = j in (2, 5)
                if gate and attend:
                    a.wait_ge(v_y, u * 2 + j // 3 + 1)
                a.activation(dst[j], pj[j % 2][:], ACT.Tanh if gate else ACT.Silu,
                             scale=0.5 if gate else 1.0).then_inc(a_ev, 1)

            def square(u, h):
                a.wait_ge(v_y, u * 2 + h + 1)
                a.wait_ge(p_sq, u * 2 + h + 1)
                a.activation(sq[h][:], ot[h][:], ACT.Square).then_inc(a_sq, 1)

            def y_high(u, h):
                a.wait_ge(v_y, u * 2 + h + 1)
                a.activation(yh[h][:], yf[h][:], ACT.Identity, scale=nwcur[:, h:h + 1]).then_inc(a_yh, 1)

            def split_high(pn, j):
                a.wait_ge(dma_w, pn * 16 + 16)
                a.copy(wh[:, section(j)], wraw[:, section(j)]).then_inc(w_hi, 1)

            def run(p, g, attend, project, more):
                u = p * NG + g
                split = more and g == 2
                for j in range(FILLS):
                    if project:
                        evacuate(u, j, attend)
                        if split and j < NSEC:
                            split_high(p + 1, j)
                    if attend and j in (0, 2):
                        square(u, j // 2)
                    if attend and j in (1, 3):
                        y_high(u, j // 2)
                if split:
                    split_high(p + 1, 6)
                    split_high(p + 1, 7)
                if more and g == NG - 1:
                    a.wait_ge(dma_o, p * 16 + 32)
                    a.wait_ge(pe_out, u * TPG + TPG)
                    for h in range(2):
                        a.copy(oh[:, h * D:(h + 1) * D], oraw[:, h * D:(h + 1) * D]).then_inc(o_hi, 1)

            all_steps(a, run)

        @block.vector
        def _(v):
            def decays(p):
                v.wait_ge(dma_d, p * 16 + 16)
                v.tensor_copy(dcur[:], draw[:])
                v.tensor_copy(nwcur[:], nw[:, bass.ds(p * 2, 2)]).then_inc(v_dec, 1)

            def mask(p, u, i):
                v.wait_ge(pe_s, u * 4 + i + 1)
                if i == 0:
                    v.wait_ge(v_dec, p + 1)
                v.tensor_tensor(ms[i % 2][:], sc[i % 2][:, 0:MC], dcur[:, i // 2, :], ALU.mult).then_inc(v_mask, 1)

            def gated(u, h):
                v.wait_ge(pe_av, u * 4 + 2 * h + 2)
                v.scalar_tensor_tensor(yf[h][:], gT[:, h, :], 1.0, ot[h][:], ALU.add, ALU.mult).then_inc(v_y, 1)

            def y_low(u, h):
                v.wait_ge(a_yh, u * 2 + h + 1)
                v.scalar_tensor_tensor(yl[h][:], yf[h][:], nwcur[:, h:h + 1], yh[h][:].bitcast(F32),
                                       ALU.mult, ALU.subtract).then_inc(v_yl, 1)

            def run(p, g, attend, project, more):
                u = p * NG + g
                if not attend:
                    decays(0)
                    return
                for h in range(2):
                    mask(p, u, 2 * h)
                    mask(p, u, 2 * h + 1)
                    gated(u, h)
                    y_low(u, h)
                if more and g == NG - 1:
                    v.wait_ge(v_yl, u * 2 + 2)
                    decays(p + 1)
                for t in range(TPG):
                    tile = acc[:, g * TPG + t, :]
                    v.wait_ge(pe_out, u * TPG + t + 1)
                    if t == 0 and g == 0:
                        v.wait_ge(p_zero, 2)
                    v.tensor_tensor(tile, op[t % 2][:], tile, ALU.add).then_inc(v_acc, 1)

            all_steps(v, run)

        @block.gpsimd
        def _(pool):
            pool.memset(acc[:], 0.0).then_inc(p_zero, 1)
            pool.memset(sqacc[:], 0.0).then_inc(p_zero, 1)
            pool.sem_inc(p_sq, 2)
            pool.wait_ge(p_zero, 2)

            def add_squares(g, u, h):
                pool.wait_ge(a_sq, u * 2 + h + 1)
                pool.wait_ge(p_sq, u * 2 + h + 2)
                c = slice(g * GT, (g + 1) * GT)
                pool.tensor_tensor(sqacc[:, c], sqacc[:, c], sq[h][:], ALU.add).then_inc(p_sq, 1)

            def split_low(pn, j):
                pool.wait_ge(w_hi, pn * FILLS + j + 1)
                c = section(j)
                pool.tensor_tensor(wl[:, c], wraw[:, c], wh[:, c].bitcast(F32), ALU.subtract).then_inc(w_lo, 1)

            def run(p, g, attend, project, more):
                u = p * NG + g
                if not attend:
                    return
                for j in range(FILLS):
                    if more and g == 2:
                        split_low(p + 1, j)
                    if j in (0, 2):
                        add_squares(g, u, j // 2)
                if more and g == NG - 1:
                    for h in range(2):
                        pool.wait_ge(o_hi, p * 2 + 3 + h)
                        c = slice(h * D, (h + 1) * D)
                        pool.tensor_tensor(ol[:, c], oraw[:, c], oh[:, c].bitcast(F32),
                                           ALU.subtract).then_inc(o_lo, 1)

            all_steps(pool, run)


def rsqrt(v, a_sem, n, chain, var, root, rstd):
    v.wait_ge(a_sem, n)
    chain.link(v.reciprocal(rstd, root))
    chain.link(v.tensor_tensor(rstd, rstd, var, ALU.mult))
    chain.link(v.tensor_tensor(root, root, rstd, ALU.add))
    chain.link(v.tensor_scalar(root, root, 0.5, None, ALU.mult))
    chain.link(v.reciprocal(rstd, root))


def experts(nc, ctx, x_tiles, router_w, router_b, router_bias, earlier, ex, b3, ident, xh, xl, acc, sqacc):
    def sb(name, shape, dt=F32):
        return ctx.enter_context(nc.sbuf_tensor(name, shape, dt))

    def sem(name):
        return ctx.enter_context(nc.semaphore(name))

    xs = sb("xs", [P, NT, D])
    eraw = [sb(f"eraw{i}", [P, XCOLS]) for i in range(2)]
    eh = [sb(f"eh{i}", [P, 3 * SEC], F32R) for i in range(2)]
    el = [sb(f"el{i}", [P, 3 * SEC], F32R) for i in range(2)]
    bias = [sb(f"ebias{i}", [P, 2]) for i in range(2)]
    gcur = [sb(f"gcur{i}", [P, NT]) for i in range(2)]
    gate = sb("gate", [P, NT, NE])
    dma_e, dma_xs, dma_r = [sem(f"dma_e{i}") for i in range(2)], sem("dma_xs"), sem("dma_r")
    e_hi, e_lo = sem("e_hi"), sem("e_lo")

    with ExitStack() as inner:
        def isb(name, shape, dt=F32):
            return inner.enter_context(nc.sbuf_tensor(name, shape, dt))

        rw = isb("rw", [P, KC, E])
        rwh = isb("rwh", [P, KC, E], F32R)
        rwl = isb("rwl", [P, KC, E], F32R)
        rb = isb("rb", [P, E])
        rbias = isb("rbias", [P, E])
        early = isb("early", [P, E * E])
        b3s = isb("b3s", [E + 1, D])
        ones = isb("ones", [P, 2])
        ms = isb("meansq", [P, NT])
        root = isb("rms_root", [P, NT])
        rs = isb("rms_factor", [P, NT])
        lg = isb("logits", [P, NT, E])
        sc = isb("rscores", [P, NT, E])
        red = isb("red", [P, NT])
        gm = isb("gmax", [P, NT, GROUPS])
        rank4 = isb("rank4", [P, NT, GROUPS])
        cmp4 = [isb(f"cmp4{i}", [P, NT, GROUPS, GROUPS]) for i in range(2)]
        cmp16 = [isb(f"cmp16{i}", [P, NT // 4, E, E]) for i in range(2)]
        gate_rank = isb("gate_rank", [P, NT, E])
        gt_s = isb("gate_t", [E + 1, T])
        ps_r = inner.enter_context(nc.psum_tensor("ps_router", [P, NT, E], F32))
        ps_m = inner.enter_context(nc.psum_tensor("ps_meansq", [P, NT], F32))
        ps_g = [inner.enter_context(nc.psum_tensor(f"ps_gt{i}", [P, GT], F32)) for i in range(2)]
        ps_b = [inner.enter_context(nc.psum_tensor(f"ps_b3{i}", [P, D], F32)) for i in range(2)]
        rw_split, v_ones, pe_sums, pe_logits, v_var, a_root, v_shift, a_exp, v_chain, v_gate, pe_gt, a_gt, pe_b3, \
            v_b3 = (sem(n) for n in ("rw_split", "v_ones", "pe_sums", "pe_logits", "v_var2", "a_root2", "v_shift",
                                     "a_exp", "v_chain2", "v_gate", "pe_gt", "a_gt", "pe_b3", "v_b3"))
        block = inner.enter_context(nc.Block())

        @block.sync
        def _(sp):
            sp.dma_start(rw[:], router_w).then_inc(dma_r, 16)
            sp.dma_start(rb[:], router_b.partition_broadcast(P)).then_inc(dma_r, 16)
            sp.dma_start(rbias[:], router_bias.partition_broadcast(P)).then_inc(dma_r, 16)
            sp.dma_start(early[:], earlier.partition_broadcast(P)).then_inc(dma_r, 16)
            sp.dma_start(b3s[:], b3).then_inc(dma_r, 16)
            for i in range(2):
                sp.dma_start(eraw[i][:], ex[i]).then_inc(dma_e[i], 16)
            for t in range(NT):
                sp.dma_start(xs[:, t, :], x_tiles[t]).then_inc(dma_xs, 16)

        @block.gpsimd
        def _(pool):
            pool.wait_ge(dma_r, 80)
            pool.tensor_copy(rwh[:], rw[:]).then_inc(rw_split, 1)
            pool.wait_ge(rw_split, 1)
            pool.tensor_tensor(rwl[:], rw[:], rwh[:].bitcast(F32), ALU.subtract).then_inc(rw_split, 1)
            pool.wait_ge(dma_e[0], 16)
            pool.tensor_copy(bias[0][:], eraw[0][:, 3 * SEC:])
            for j in range(3):
                c = slice(j * SEC, (j + 1) * SEC)
                pool.tensor_copy(eh[0][:, c], eraw[0][:, c]).then_inc(e_hi, 1)
                pool.wait_ge(e_hi, j + 1)
                pool.tensor_tensor(el[0][:, c], eraw[0][:, c], eh[0][:, c].bitcast(F32),
                                   ALU.subtract).then_inc(e_lo, 1)

        @block.tensor
        def _(pe):
            pe.wait_ge(v_ones, 1)
            for t in range(NT):
                ins = pe.matmul(ps_m[:, t:t + 1], sqacc[:, t * P:(t + 1) * P], ones[:, 0:1], start=True, stop=True)
            ins.then_inc(pe_sums, 1)
            pe.wait_ge(rw_split, 2)
            for t in range(NT):
                m = slice(t * P, (t + 1) * P)
                parts = [(xh[:, k, m], xl[:, k, m], rwh[:, k, :], rwl[:, k, :]) for k in range(KC)]
                ins = three_passes(pe, ps_r[:, t, :], parts, True, True)
            ins.then_inc(pe_logits, 1)
            pe.wait_ge(v_gate, 1)
            for g in range(NG):
                if g >= 2:
                    pe.wait_ge(a_gt, g - 1)
                for t in range(TPG):
                    ins = pe.transpose(ps_g[g % 2][0:E + 1, t * P:(t + 1) * P], gate[:, g * TPG + t, 0:E + 1],
                                       ident[:])
                ins.then_inc(pe_gt, 1)
            pe.wait_ge(dma_r, 80)
            for t in range(NT):
                if t % TPG == 0:
                    pe.wait_ge(a_gt, t // TPG + 1)
                if t >= 2:
                    pe.wait_ge(v_b3, t - 1)
                pe.matmul(ps_b[t % 2][:], gt_s[:, t * P:(t + 1) * P], b3s[:], start=True,
                          stop=True).then_inc(pe_b3, 1)

        @block.scalar
        def _(a):
            a.wait_ge(v_var, 1)
            a.activation(root[:], ms[:], ACT.Sqrt).then_inc(a_root, 1)
            a.wait_ge(v_shift, 1)
            a.activation(lg[:], lg[:], ACT.Exp).then_inc(a_exp, 1)
            for g in range(NG):
                a.wait_ge(pe_gt, g + 1)
                a.copy(gt_s[:, g * GT:(g + 1) * GT], ps_g[g % 2][0:E + 1, :]).then_inc(a_gt, 1)

        @block.vector
        def _(v):
            c = Chain(v, v_chain)
            v.memset(ones[:], 1.0).then_inc(v_ones, 1)
            c.link(v.memset(gate[:], 1.0))
            v.wait_ge(pe_sums, 1)
            v.tensor_scalar(ms[:], ps_m[:], 1.0 / (H * DH), EPS, ALU.mult, ALU.add).then_inc(v_var, 1)
            v.wait_ge(dma_r, 80)
            v.wait_ge(pe_logits, 1)
            over_e = [P, NT, E]
            c.link(v.tensor_tensor(lg[:], ps_r[:], rb[:].unsqueeze(1).to_broadcast(over_e), ALU.add))
            c.link(v.tensor_reduce(red[:], lg[:], AX_X, ALU.max))
            v.tensor_tensor(lg[:], lg[:], red[:].unsqueeze(2).to_broadcast(over_e), ALU.subtract).then_inc(v_shift, 1)
            v.wait_ge(v_var, 1)
            rsqrt(v, a_root, 1, c, ms[:], root[:], rs[:])
            v.wait_ge(a_exp, 1)
            c.link(v.tensor_reduce(red[:], lg[:], AX_X, ALU.add))
            c.link(v.reciprocal(red[:], red[:]))
            c.link(v.tensor_tensor(sc[:], lg[:], red[:].unsqueeze(2).to_broadcast(over_e), ALU.mult))
            c.link(v.tensor_tensor(sc[:], sc[:], rbias[:].unsqueeze(1).to_broadcast(over_e), ALU.add))
            sc4 = sc[:].rearrange("p t (g e) -> p t g e", g=GROUPS)
            c.link(v.tensor_reduce(gm[:], sc4, AX_X, ALU.max))

            def rank(val, cmps, out, n, t0, nt, lower):
                full = [P, nt, n, n]
                vj = val[:, t0:t0 + nt, :].unsqueeze(2).to_broadcast(full)
                vi = val[:, t0:t0 + nt, :].unsqueeze(3).to_broadcast(full)
                gt, ge = cmps[0][:, 0:nt], cmps[1][:, 0:nt]
                c.link(v.tensor_tensor(gt, vj, vi, ALU.is_gt))
                c.link(v.tensor_tensor(ge, vj, vi, ALU.is_ge))
                c.link(v.tensor_tensor(ge, ge, gt, ALU.subtract))
                c.link(v.tensor_tensor(ge, ge, lower.unsqueeze(1).to_broadcast(full), ALU.mult))
                c.link(v.tensor_tensor(gt, gt, ge, ALU.add))
                c.link(v.tensor_reduce(out[:, t0:t0 + nt, :], gt, AX_X, ALU.add))

            lower16 = early[:].rearrange("p (i j) -> p i j", i=E)
            lower4 = lower16[:, 0:GROUPS, 0:GROUPS]
            rank(gm, cmp4, rank4, GROUPS, 0, NT, lower4)
            c.link(v.tensor_scalar(rank4[:], rank4[:], 2.0, None, ALU.is_lt))
            lg4 = lg[:].rearrange("p t (g e) -> p t g e", g=GROUPS)
            keep = rank4[:].unsqueeze(3).to_broadcast([P, NT, GROUPS, E // GROUPS])
            c.link(v.tensor_tensor(lg4, sc4, keep, ALU.mult))
            c.link(v.tensor_scalar(rank4[:], rank4[:], 1.0, -NEG, ALU.subtract, ALU.mult))
            c.link(v.tensor_tensor(lg4, lg4, keep, ALU.add))
            for quarter in range(4):
                rank(lg, cmp16, gate_rank, E, quarter * NT // 4, NT // 4, lower16)
            c.link(v.tensor_scalar(gate_rank[:], gate_rank[:], 2.0, None, ALU.is_lt))
            v.tensor_tensor(gate[:, :, 0:E], gate_rank[:], sc[:], ALU.mult).then_inc(v_gate, 1)
            v.wait_ge(dma_xs, 16 * NT)
            for t in range(NT):
                ins = v.scalar_tensor_tensor(acc[:, t, :], acc[:, t, :], rs[:, t:t + 1], xs[:, t, :], ALU.mult,
                                             ALU.add)
            c.link(ins)
            for t in range(NT):
                v.wait_ge(pe_b3, t + 1)
                v.tensor_tensor(acc[:, t, :], ps_b[t % 2][:], acc[:, t, :], ALU.add).then_inc(v_b3, 1)

    with ExitStack() as inner:
        hf = [inner.enter_context(nc.sbuf_tensor(f"hf{i}", [P, GT], F32)) for i in range(2)]
        s1 = [inner.enter_context(nc.sbuf_tensor(f"s1{i}", [P, GT], F32)) for i in range(2)]
        hh = [inner.enter_context(nc.sbuf_tensor(f"hh{i}", [P, GT], F32R)) for i in range(2)]
        hl = [inner.enter_context(nc.sbuf_tensor(f"hl{i}", [P, GT], F32R)) for i in range(2)]
        hp = [[inner.enter_context(nc.psum_tensor(f"hp{i}{j}", [P, GT], F32)) for j in range(2)] for i in range(2)]
        op = [inner.enter_context(nc.psum_tensor(f"eout{i}", [P, D], F32)) for i in range(TPG)]
        pe_h1, pe_h2, pe_out, a_s1, a_hh, v_hf, v_hl, v_acc, v_gc = (
            sem(n) for n in ("pe_h1", "pe_h2", "pe_eout", "a_s1", "a_hh", "v_hf", "v_hl", "v_eacc", "v_gc"))
        block = inner.enter_context(nc.Block())
        last = NE // 2 - 1

        def all_steps(run):
            def with_eng(eng):
                run(-1, 1, NG - 1, False, True, False)
                with eng.Fori(0, last) as q:
                    for i in range(2):
                        for g in range(NG):
                            run(q, i, g, True, True, True)
                for i in range(2):
                    for g in range(NG):
                        run(last, i, g, True, i == 0 or g + 1 < NG, i == 0)
            return with_eng

        @block.sync
        def _(sp):
            with sp.Fori(1, last + 1) as q:
                for i in range(2):
                    sp.wait_ge(e_lo, q * 6 + 3 * i - 3)
                    sp.dma_start(eraw[i][:], ex[q * 2 + i]).then_inc(dma_e[i], 16)

        @block.tensor
        def _(pe):
            def run(q, i, g, finish, start, more):
                u = (q * 2 + i) * NG + g
                if start:
                    en, ni, gn = (q * 2 + i, i, g + 1) if g + 1 < NG else (q * 2 + i + 1, 1 - i, 0)
                    m = slice(gn * GT, (gn + 1) * GT)
                    b = (g + 1) % 2
                    for j, done in ((0, pe_h1), (1, pe_h2)):
                        if gn == 0:
                            pe.wait_ge(e_lo, en * 3 + j + 1)
                        parts = []
                        for k in range(KC):
                            c = slice(j * SEC + k * P, j * SEC + (k + 1) * P)
                            parts.append((eh[ni][:, c], el[ni][:, c], xh[:, k, m], xl[:, k, m]))
                        three_passes(pe, hp[b][j][:], parts, True, True).then_inc(done, 1)
                if finish:
                    b = g % 2
                    if g == 0:
                        pe.wait_ge(e_lo, (q * 2 + i) * 3 + 3)
                    pe.wait_ge(v_hl, u + 1)
                    c = slice(2 * SEC, 3 * SEC)
                    for t in range(TPG):
                        m = slice(t * P, (t + 1) * P)
                        three_passes(pe, op[t][:], [(hh[b][:, m], hl[b][:, m], eh[i][:, c], el[i][:, c])],
                                     True, True).then_inc(pe_out, 1)

            all_steps(run)(pe)

        @block.scalar
        def _(a):
            def run(q, i, g, finish, start, more):
                u = (q * 2 + i) * NG + g
                if start:
                    en, ni = (q * 2 + i, i) if g + 1 < NG else (q * 2 + i + 1, 1 - i)
                    b = (g + 1) % 2
                    if g + 1 == NG:
                        a.wait_ge(e_hi, en * 3 + 3)
                    a.wait_ge(pe_h1, u + 2)
                    a.activation(s1[b][:], hp[b][0][:], ACT.Silu, bias=bias[ni][:, 0:1]).then_inc(a_s1, 1)
                if finish and more and g < 3:
                    if g == 0:
                        a.wait_ge(dma_e[1 - i], (q + 1 + i) * 16)
                    if g == 2:
                        a.copy(bias[1 - i][:], eraw[1 - i][:, 3 * SEC:])
                    c = slice(g * SEC, (g + 1) * SEC)
                    a.copy(eh[1 - i][:, c], eraw[1 - i][:, c]).then_inc(e_hi, 1)
                if start:
                    a.wait_ge(v_hf, u + 2)
                    a.copy(hh[b][:], hf[b][:]).then_inc(a_hh, 1)

            all_steps(run)(a)

        @block.gpsimd
        def _(pool):
            def run(q, i, g, finish, start, more):
                if finish and more and g < 3:
                    pool.wait_ge(e_hi, (q * 2 + i + 1) * 3 + g + 1)
                    c = slice(g * SEC, (g + 1) * SEC)
                    pool.tensor_tensor(el[1 - i][:, c], eraw[1 - i][:, c], eh[1 - i][:, c].bitcast(F32),
                                       ALU.subtract).then_inc(e_lo, 1)

            all_steps(run)(pool)

        @block.vector
        def _(v):
            def run(q, i, g, finish, start, more):
                u = (q * 2 + i) * NG + g
                if finish:
                    if g == 0:
                        v.tensor_copy(gcur[i][:], gate[:, :, bass.ds(q * 2 + i, 1)].rearrange("p t o -> p (t o)")
                                      ).then_inc(v_gc, 1)
                        v.wait_ge(v_gc, q * 2 + i + 1)
                    for t in range(TPG):
                        tile = g * TPG + t
                        v.wait_ge(pe_out, u * TPG + t + 1)
                        v.scalar_tensor_tensor(acc[:, tile, :], op[t][:], gcur[i][:, tile:tile + 1], acc[:, tile, :],
                                               ALU.mult, ALU.add).then_inc(v_acc, 1)
                if start:
                    ni, b = (i, (g + 1) % 2) if g + 1 < NG else (1 - i, 0)
                    v.wait_ge(a_s1, u + 2)
                    v.wait_ge(pe_h2, u + 2)
                    v.scalar_tensor_tensor(hf[b][:], hp[b][1][:], bias[ni][:, 1:2], s1[b][:], ALU.add,
                                           ALU.mult).then_inc(v_hf, 1)
                    v.wait_ge(a_hh, u + 2)
                    v.tensor_tensor(hl[b][:], hf[b][:], hh[b][:].bitcast(F32), ALU.subtract).then_inc(v_hl, 1)

            all_steps(run)(v)


def layer_one(nc, ctx, w_qkv, b_qkv, w_o, b_o, w_r, w_a, w_b, sel_in, ident, acc, out_tiles):
    def sb(name, shape, dt=F32):
        return ctx.enter_context(nc.sbuf_tensor(name, shape, dt))

    def sem(name):
        return ctx.enter_context(nc.semaphore(name))

    QK = 3 * SEC
    RAWS = 3
    wq = [sb("l1_wqh", [P, QK], F32R), sb("l1_wql", [P, QK], F32R)]
    wo = [sb("l1_woh", [P, D], F32R), sb("l1_wol", [P, D], F32R)]
    wr = [sb("l1_wrh", [P, KC * K1], F32R), sb("l1_wrl", [P, KC * K1], F32R)]
    wa = [sb("l1_wah", [P, NR * KC * P], F32R), sb("l1_wal", [P, NR * KC * P], F32R)]
    wb = [sb("l1_wbh", [P, NR * D], F32R), sb("l1_wbl", [P, NR * D], F32R)]
    sel = sb("l1_sel", [K1, NR * P], F32R)
    bq = sb("l1_bq", [P, 3])
    bo = sb("l1_bo", [P, D])
    xh = [sb(f"x1h{i}", [P, KC, GT], F32R) for i in range(2)]
    xl = [sb(f"x1l{i}", [P, KC, GT], F32R) for i in range(2)]
    dma_c = sem("l1_dma_c")
    dma_s = [sem(f"l1_dma_s{i}") for i in range(RAWS)]
    s_hi, s_lo, s_bo = sem("l1_hi"), sem("l1_lo"), sem("l1_bo_added")

    pieces = [(w_qkv, wq, j * SEC, SEC) for j in range(3)] + [(w_r, wr, 0, KC * K1), (w_o, wo, 0, D)]
    n_sel = NR * P // D
    pieces += [(sel_in, None, j * D, D) for j in range(n_sel)]
    for j in range(NR):
        pieces += [(w_a, wa, j * SEC, SEC), (w_b, wb, j * D, D)]
    with ExitStack() as inner:
        def isb(name, shape, dt=F32):
            return inner.enter_context(nc.sbuf_tensor(name, shape, dt))

        raw = [isb(f"l1_raw{i}", [P, D]) for i in range(RAWS)]
        stage = isb("l1_stage", [P, TPG, D])
        stat = isb("l1_stat", [P, TPG, 6])
        mv = isb("l1_mv", [P, TPG, 2])
        var = isb("l1_var", [P, TPG])
        root = isb("l1_root", [P, TPG])
        rstd = isb("l1_rstd", [P, TPG])
        qkv = isb("l1_qkv", [P, 3, GT])
        vt = isb("l1_v", [P, TPG, DH])
        pr = isb("l1_p", [P, TPG, S])
        pt = [isb(f"l1_pt{i}", [P, 2 * S]) for i in range(2)]
        mx = isb("l1_mx", [P, TPG])
        sm = isb("l1_sum", [P, TPG])
        oh = isb("l1_oh", [P, GT], F32R)
        ol = isb("l1_ol", [P, GT], F32R)
        sr = isb("l1_sr", [P, TPG, K1])
        left = [isb(f"l1_left{i}", [P, TPG, K1]) for i in range(2)]
        top8 = isb("l1_top8", [P, 2, TPG, 8])
        nm = isb("l1_nm", [P, TPG])
        rz = isb("l1_rz", [P, TPG])
        gg = isb("l1_g", [P, TPG, K1])
        gh = isb("l1_gh", [K1, GT], F32R)
        gl = isb("l1_gl", [K1, GT], F32R)
        gs = isb("l1_gs", [P, GT])
        hf = isb("l1_hf", [P, GT])
        hh = [isb(f"l1_hh{i}", [P, GT], F32R) for i in range(2)]
        hl = [isb(f"l1_hl{i}", [P, GT], F32R) for i in range(2)]
        ob = [inner.enter_context(nc.psum_tensor(f"l1_ob{i}", [P, D], F32)) for i in range(TPG)]
        hb = [inner.enter_context(nc.psum_tensor(f"l1_hb{i}", [P, GT], F32)) for i in range(2)]
        mb = [inner.enter_context(nc.psum_tensor(f"l1_mb{i}", [P, GT], F32)) for i in range(2)]
        SCALE = float(np.float32(1.0) / np.sqrt(np.float32(DH)))
        names = ("pe_h", "pe_m", "pe_out", "a_qkv", "a_vt", "a_exp", "a_rexp", "a_gh", "a_pt", "a_oh", "a_ge", "a_hh",
                 "v_chain", "v_r", "v_nm", "v_max", "v_prob", "v_g", "v_gl", "v_ol", "v_hf", "v_hl", "v_fin",
                 "v_var", "a_root", "v_xn", "a_xh", "v_xl", "p_bo", "dma_out")
        q = {n: sem(f"l1_{n}") for n in names}
        block = inner.enter_context(nc.Block())

        events = [("norm", 0, 0)] + [("xt", 0, k) for k in range(KC)]
        for g in range(NG + 1):
            mix = [("mix", g - 1, j) for j in range(NR)] if g else []
            if g < NG:
                events += [("qkv", g, 0), ("qkv", g, 1), ("qkv", g, 2), ("route", g, 0), ("vt", g, 0),
                           ("score", g, 0), ("score", g, 1)]
            events += mix[:NR // 2]
            if g < NG:
                events += [("probs", g, 0), ("probs", g, 1)]
            if g + 1 < NG:
                events += [("norm", g + 1, 0)]
            events += mix[NR // 2:]
            if g + 1 < NG:
                events += [("xt", g + 1, k) for k in range(KC)]
            if g < NG:
                events += [("gates", g, 0), ("attend", g, 0)]
        h_fill, h_taken, m_fill, m_taken = {}, [], {}, []
        for what, g, i in events:
            if what in ("qkv", "mix"):
                h_fill[what, g, i] = len(h_taken)
                h_taken.append((q["a_qkv"], 3 * g + i + 1) if what == "qkv" else (q["v_hf"], NR * g + i + 1))
            if what not in ("qkv", "norm"):
                m_fill[what, g, i] = len(m_taken)
                m_taken.append({"route": (q["v_r"], g + 1), "vt": (q["a_vt"], g + 1),
                                "score": (q["a_exp"], 2 * g + i + 1), "gates": (q["v_gl"], g + 1),
                                "probs": (q["a_pt"], 2 * g + i + 1), "attend": (q["v_ol"], g + 1),
                                "mix": (q["a_ge"], NR * g + i + 1), "xt": (q["v_xl"], KC * g + i + 1)}[what])

        @block.tensor
        def _(pe):
            def fill(banks, fills, taken, key):
                n = fills[key]
                if n >= 2:
                    pe.wait_ge(*taken[n - 2])
                return banks[n % 2]

            def outputs(g, i):
                pe.wait_ge(q["v_hl"], NR * g + i + 1)
                c = slice(i * D, (i + 1) * D)
                for t in range(TPG):
                    m = slice(t * P, (t + 1) * P)
                    ins = three_passes(pe, ob[t][:], [(hh[i % 2][:, m], hl[i % 2][:, m], wb[0][:, c], wb[1][:, c])],
                                       False, i == NR - 1)
                    if i == NR - 1:
                        ins.then_inc(q["pe_out"], 1)

            for what, g, i in events:
                if what == "norm":
                    continue
                if what == "qkv":
                    if i == 0:
                        pe.wait_ge(q["v_xl"], KC * (g + 1))
                    if g == 0:
                        pe.wait_ge(s_lo, i + 1)
                    bank = fill(hb, h_fill, h_taken, (what, g, i))
                    parts = []
                    for k in range(KC):
                        c = slice(i * SEC + k * P, i * SEC + (k + 1) * P)
                        parts.append((wq[0][:, c], wq[1][:, c], xh[g % 2][:, k, :], xl[g % 2][:, k, :]))
                    three_passes(pe, bank[:], parts, True, True).then_inc(q["pe_h"], 1)
                    continue
                if what != "mix":
                    bank = fill(mb, m_fill, m_taken, (what, g, i))
                if what == "route":
                    if g == 0:
                        pe.wait_ge(s_lo, 4)
                    for t in range(TPG):
                        tok = slice(t * P, (t + 1) * P)
                        parts = [(xh[g % 2][:, k, tok], xl[g % 2][:, k, tok], wr[0][:, k * K1:(k + 1) * K1],
                                  wr[1][:, k * K1:(k + 1) * K1]) for k in range(KC)]
                        ins = three_passes(pe, bank[:, t * K1:(t + 1) * K1], parts, True, True)
                elif what == "xt":
                    if i == 0:
                        pe.wait_ge(q["v_xn"], g + 1)
                    for t in range(TPG):
                        ins = pe.transpose(bank[:, t * P:(t + 1) * P], stage[:, t, i * P:(i + 1) * P], ident[:])
                elif what == "vt":
                    pe.wait_ge(q["a_qkv"], 3 * g + 3)
                    for t in range(TPG):
                        ins = pe.transpose(bank[:, t * P:(t + 1) * P], qkv[:, 2, t * P:(t + 1) * P], ident[:])
                elif what == "score":
                    for t in range(2):
                        ins = pe.matmul(bank[:, t * S:(t + 1) * S], qkv[:, 0, i * S + t * P:i * S + (t + 1) * P],
                                        qkv[:, 1, i * S:(i + 1) * S], start=True, stop=True)
                elif what == "gates":
                    pe.wait_ge(q["v_g"], g + 1)
                    for t in range(TPG):
                        ins = pe.transpose(bank[0:K1, t * P:(t + 1) * P], gg[:, t, :], ident[:])
                elif what == "probs":
                    pe.wait_ge(q["v_prob"], 2 * g + i + 1)
                    for kt in range(2):
                        for t in range(2):
                            ins = pe.transpose(bank[:, kt * S + t * P:kt * S + (t + 1) * P],
                                               pr[:, 2 * i + t, kt * P:(kt + 1) * P], ident[:])
                elif what == "attend":
                    pe.wait_ge(q["a_pt"], 2 * g + 2)
                    for b in range(2):
                        for kt in range(2):
                            ins = pe.matmul(bank[:, b * S:(b + 1) * S], vt[:, 2 * b + kt, :],
                                            pt[b][:, kt * S:(kt + 1) * S], start=kt == 0, stop=kt == 1)
                elif what == "mix":
                    if i == 0:
                        pe.wait_ge(q["v_ol"], g + 1)
                        if g == 0:
                            pe.wait_ge(s_lo, 5)
                        for t in range(TPG):
                            if g:
                                pe.wait_ge(q["v_fin"], TPG * (g - 1) + t + 1)
                            tt = slice(t * P, (t + 1) * P)
                            three_passes(pe, ob[t][:], [(oh[:, tt], ol[:, tt], wo[0][:], wo[1][:])], True, False)
                    bank = fill(hb, h_fill, h_taken, (what, g, i))
                    if g == 0:
                        pe.wait_ge(s_lo, 5 + n_sel + 2 * i + 2)
                    parts = []
                    for k in range(KC):
                        c = slice(i * SEC + k * P, i * SEC + (k + 1) * P)
                        parts.append((wa[0][:, c], wa[1][:, c], xh[g % 2][:, k, :], xl[g % 2][:, k, :]))
                    three_passes(pe, bank[:], parts, True, True).then_inc(q["pe_h"], 1)
                    bank = fill(mb, m_fill, m_taken, (what, g, i))
                    if i == 0:
                        pe.wait_ge(q["v_gl"], g + 1)
                    s = sel[:, i * P:(i + 1) * P]
                    pe.matmul(bank[:], s, gh[:], start=True, stop=False)
                    ins = pe.matmul(bank[:], s, gl[:], start=False, stop=True)
                ins.then_inc(q["pe_m"], 1)
                if what == "mix" and i:
                    outputs(g, i - 1)
                if what == "mix" and i == NR - 1:
                    outputs(g, i)

        @block.scalar
        def _(a):
            for what, g, i in events:
                if what == "norm":
                    a.wait_ge(q["v_var"], g + 1)
                    a.activation(root[:], var[:], ACT.Sqrt).then_inc(q["a_root"], 1)
                    continue
                if what == "qkv":
                    n = h_fill[what, g, i]
                    if g == i == 0:
                        a.wait_ge(dma_c, 32)
                    a.wait_ge(q["pe_h"], n + 1)
                    if g:
                        a.wait_ge(q["pe_m"], m_fill["attend", g - 1, 0] + 1)
                    a.activation(qkv[:, i, :], hb[n % 2][:], ACT.Identity, bias=bq[:, i:i + 1]).then_inc(q["a_qkv"], 1)
                    continue
                n = m_fill[what, g, i]
                bank = mb[n % 2]
                if what == "route":
                    a.wait_ge(q["v_nm"], g + 1)
                    for t in range(TPG):
                        ins = a.activation(gg[:, t, :], sr[:, t, :], ACT.Exp, bias=nm[:, t:t + 1])
                    ins.then_inc(q["a_rexp"], 1)
                    continue
                if what == "score":
                    a.wait_ge(q["v_max"], 2 * g + i + 1)
                    for t in range(2):
                        ins = a.activation(pr[:, 2 * i + t, :], bank[:, t * S:(t + 1) * S], ACT.Exp,
                                           bias=mx[:, 2 * i + t:2 * i + t + 1], scale=SCALE,
                                           accum_out=sm[:, 2 * i + t:2 * i + t + 1])
                    ins.then_inc(q["a_exp"], 1)
                    continue
                a.wait_ge(q["pe_m"], n + 1)
                if what == "xt":
                    a.copy(xh[g % 2][:, i, :], bank[:]).then_inc(q["a_xh"], 1)
                elif what == "vt":
                    a.copy(vt[:].rearrange("p t d -> p (t d)"), bank[:]).then_inc(q["a_vt"], 1)
                elif what == "gates":
                    a.copy(gh[:], bank[0:K1, :]).then_inc(q["a_gh"], 1)
                elif what == "probs":
                    a.copy(pt[i][:], bank[:]).then_inc(q["a_pt"], 1)
                elif what == "attend":
                    a.copy(oh[:], bank[:]).then_inc(q["a_oh"], 1)
                elif what == "mix":
                    a.copy(gs[:], bank[:]).then_inc(q["a_ge"], 1)
                    a.wait_ge(q["v_hf"], NR * g + i + 1)
                    a.copy(hh[i % 2][:], hf[:]).then_inc(q["a_hh"], 1)

        @block.vector
        def _(v):
            c = Chain(v, q["v_chain"])
            for what, g, i in events:
                if what in ("vt", "qkv", "probs"):
                    continue
                if what == "norm":
                    tiles = range(g * TPG, (g + 1) * TPG)
                    for t in tiles:
                        ins = v.bn_stats(stat[:, t % TPG, :], acc[:, t, :])
                    c.link(ins)
                    for t in range(TPG):
                        ins = v.bn_aggr(mv[:, t, :], stat[:, t, :])
                    c.link(ins)
                    v.tensor_scalar(var[:], mv[:, :, 1], EPS, None, ALU.add).then_inc(q["v_var"], 1)
                    v.wait_ge(q["v_var"], g + 1)
                    rsqrt(v, q["a_root"], g + 1, c, var[:], root[:], rstd[:])
                    if g:
                        v.wait_ge(q["pe_m"], m_fill["xt", g - 1, KC - 1] + 1)
                    for t in tiles:
                        ins = v.tensor_scalar(stage[:, t % TPG, :], acc[:, t, :], mv[:, t % TPG, 0:1],
                                              rstd[:, t % TPG:t % TPG + 1], ALU.subtract, ALU.mult)
                    ins.then_inc(q["v_xn"], 1)
                    continue
                n = m_fill[what, g, i]
                bank = mb[n % 2]
                if what == "route":
                    v.wait_ge(q["pe_m"], n + 1)
                    v.tensor_copy(sr[:].rearrange("p t k -> p (t k)"), bank[:, 0:TPG * K1]).then_inc(q["v_r"], 1)
                    v.wait_ge(q["v_r"], g + 1)
                    for t in range(TPG):
                        ins = v.max(top8[:, 0, t, :], sr[:, t, :])
                    c.link(ins)
                    v.tensor_scalar(nm[:], top8[:, 0, :, 0], -1.0, None, ALU.mult).then_inc(q["v_nm"], 1)
                    for t in range(TPG):
                        ins = v.match_replace(left[0][:, t, :], top8[:, 0, t, :], sr[:, t, :], NEG)
                    c.link(ins)
                    for t in range(TPG):
                        ins = v.max(top8[:, 1, t, :], left[0][:, t, :])
                    c.link(ins)
                    for t in range(TPG):
                        ins = v.match_replace(left[1][:, t, :], top8[:, 1, t, :], left[0][:, t, :], NEG)
                    c.link(ins)
                    c.link(v.tensor_tensor(left[0][:], left[1][:], sr[:], ALU.not_equal))
                    v.wait_ge(q["a_rexp"], g + 1)
                    c.link(v.tensor_tensor(gg[:], gg[:], left[0][:], ALU.mult))
                    c.link(v.tensor_reduce(rz[:], gg[:], AX_X, ALU.add))
                    c.link(v.reciprocal(rz[:], rz[:]))
                    for t in range(TPG):
                        ins = v.tensor_scalar(gg[:, t, :], gg[:, t, :], rz[:, t:t + 1], 2.0, ALU.mult, ALU.mult)
                    ins.then_inc(q["v_g"], 1)
                elif what == "score":
                    v.wait_ge(q["pe_m"], n + 1)
                    t2 = slice(2 * i, 2 * i + 2)
                    c.link(v.tensor_reduce(mx[:, t2], bank[:].rearrange("p (t s) -> p t s", t=2), AX_X, ALU.max))
                    v.tensor_scalar(mx[:, t2], mx[:, t2], -SCALE, None, ALU.mult).then_inc(q["v_max"], 1)
                    v.wait_ge(q["a_exp"], 2 * g + i + 1)
                    c.link(v.reciprocal(sm[:, t2], sm[:, t2]))
                    for t in range(2):
                        ins = v.tensor_scalar(pr[:, 2 * i + t, :], pr[:, 2 * i + t, :], sm[:, 2 * i + t:2 * i + t + 1],
                                              None, ALU.mult)
                    ins.then_inc(q["v_prob"], 1)
                elif what == "xt":
                    v.wait_ge(q["a_xh"], KC * g + i + 1)
                    v.tensor_tensor(xl[g % 2][:, i, :], bank[:], xh[g % 2][:, i, :].bitcast(F32),
                                    ALU.subtract).then_inc(q["v_xl"], 1)
                elif what == "gates":
                    v.wait_ge(q["a_gh"], g + 1)
                    v.tensor_tensor(gl[:], bank[0:K1, :], gh[:].bitcast(F32),
                                    ALU.subtract).then_inc(q["v_gl"], 1)
                elif what == "attend":
                    v.wait_ge(q["a_oh"], g + 1)
                    v.tensor_tensor(ol[:], bank[:], oh[:].bitcast(F32), ALU.subtract).then_inc(q["v_ol"], 1)
                elif what == "mix":
                    h = h_fill[what, g, i]
                    v.wait_ge(q["pe_h"], h + 1)
                    v.wait_ge(q["a_ge"], NR * g + i + 1)
                    if NR * g + i:
                        v.wait_ge(q["v_hl"], NR * g + i)
                    v.tensor_tensor(hf[:], hb[h % 2][:], gs[:], ALU.mult).then_inc(q["v_hf"], 1)
                    v.wait_ge(q["a_hh"], NR * g + i + 1)
                    v.tensor_tensor(hl[i % 2][:], hf[:], hh[i % 2][:].bitcast(F32),
                                    ALU.subtract).then_inc(q["v_hl"], 1)
                    if i == NR - 1:
                        for t in range(TPG):
                            tile = acc[:, g * TPG + t, :]
                            v.wait_ge(q["pe_out"], g * TPG + t + 1)
                            v.wait_ge(q["p_bo"], g * TPG + t + 1)
                            v.tensor_tensor(tile, ob[t][:], tile, ALU.add).then_inc(q["v_fin"], 1)

        @block.gpsimd
        def _(pool):
            def split(n):
                _, dst, c0, w = pieces[n]
                c, r = slice(c0, c0 + w), raw[n % RAWS]
                pool.wait_ge(dma_s[n % RAWS], 16 * (n // RAWS + 1))
                if dst is None:
                    pool.tensor_copy(sel[:, c], r[0:K1, :]).then_inc(s_lo, 1)
                    return
                pool.tensor_copy(dst[0][:, c], r[:, 0:w]).then_inc(s_hi, 1)
                pool.wait_ge(s_hi, n + 1 - (n_sel if n > 5 else 0))
                pool.tensor_tensor(dst[1][:, c], r[:, 0:w], dst[0][:, c].bitcast(F32), ALU.subtract).then_inc(s_lo, 1)

            for n in range(len(pieces)):
                split(n)
            pool.wait_ge(dma_c, 32)
            for t in range(NT):
                if t % TPG == 0:
                    pool.wait_ge(q["v_xn"], t // TPG + 1)
                pool.tensor_tensor(acc[:, t, :], acc[:, t, :], bo[:], ALU.add).then_inc(q["p_bo"], 1)

        @block.sync
        def _(sp):
            sp.dma_start(bq[:], b_qkv).then_inc(dma_c, 16)
            sp.dma_start(bo[:], b_o.partition_broadcast(P)).then_inc(dma_c, 16)
            for n, (src, dst, c0, w) in enumerate(pieces):
                if n >= RAWS:
                    sp.wait_ge(s_lo, n - RAWS + 1)
                rows = P if dst else K1
                sp.dma_start(raw[n % RAWS][0:rows, 0:w], src[:, c0:c0 + w]).then_inc(dma_s[n % RAWS], 16)
            for t in range(NT):
                sp.wait_ge(q["v_fin"], t + 1)
                sp.dma_start(out_tiles[t], acc[:, t, :]).then_inc(q["dma_out"], 16)
            sp.wait_ge(q["dma_out"], 16 * NT)


def decay_tables():
    slope = (1.0 / 2.0 ** (8.0 / H)) ** (np.arange(H) + 1.0) * (1.0 - 1.0 / (31 + 1e-5) + 1e-5)
    n_m = np.arange(S)[None, :] - np.arange(P)[:, None]
    d = np.where(n_m >= 0, np.exp(-slope[:, None, None] * np.maximum(n_m, 0)), 0.0).astype(np.float32)
    d = np.concatenate([d, d[:, :, :P]], 2)
    return np.ascontiguousarray(d.reshape(NP_, 2, P, MC).transpose(0, 2, 1, 3))


def chunks(w):
    return w.reshape(KC, P, -1).transpose(1, 0, 2)


def layouts(a):
    qkv = a["L0_attn_qkv_w"].reshape(H, 3, DH, KC, P).transpose(0, 1, 4, 3, 2)
    gate = a["L0_attn_gate_w"].reshape(H, DH, KC, P).transpose(0, 3, 2, 1)
    sections = [w[h::2].reshape(NP_, P, SEC) for h in range(2) for w in (qkv[:, 0], qkv[:, 1], gate)]
    v = np.stack([qkv[0::2, 2], qkv[1::2, 2]], 3).reshape(NP_, P, 2 * SEC)

    def first(w):
        return w.reshape(-1, KC, P, INTER).transpose(0, 2, 1, 3).reshape(-1, P, SEC)

    def inner(w, s):
        return np.concatenate([w, s.reshape(D, 2, INTER).transpose(1, 0, 2)], 0)

    ex = np.concatenate([
        first(inner(a["L0_ffn_ew1"], a["L0_ffn_sw1"])), first(inner(a["L0_ffn_ew2"], a["L0_ffn_sw2"])),
        np.concatenate([a["L0_ffn_ew3"], a["L0_ffn_sw3"].reshape(2, INTER, D)], 0),
        np.concatenate([a["L0_ffn_eb1"], a["L0_ffn_sb1"].reshape(2, INTER)], 0)[:, :, None],
        np.concatenate([a["L0_ffn_eb2"], a["L0_ffn_sb2"].reshape(2, INTER)], 0)[:, :, None]], 2)
    wqkv = a["L1_attn_Wqkv"].reshape(KC, P, 3, DH).transpose(1, 2, 0, 3).reshape(P, 3 * SEC)
    wa = a["L1_ffn_A"].reshape(NR, P, KC, P).transpose(3, 0, 2, 1).reshape(P, NR * SEC)
    wb = a["L1_ffn_B"].transpose(0, 2, 1).reshape(NR, P, D).transpose(1, 0, 2).reshape(P, NR * D)
    return {
        "x": a["L0_attn_hidden_states"],
        "w_pairs": np.concatenate(sections + [v], 2),
        "o_pairs": a["L0_attn_out_w"].T.reshape(NP_, 2, P, D).transpose(0, 2, 1, 3).reshape(NP_, P, OCOLS),
        "decay": decay_tables(),
        "norm_w": a["L0_attn_norm_w"].reshape(H, DH).T,
        "router_w": chunks(a["L0_ffn_router_w"]),
        "router_b": a["L0_ffn_router_b"],
        "router_bias": a["L0_ffn_router_bias"],
        "earlier": np.tril(np.ones((E, E), np.float32), -1).reshape(E * E),
        "ex": ex,
        "b3": np.concatenate([a["L0_ffn_eb3"], a["L0_ffn_sb3"][None]], 0),
        "w_qkv": wqkv,
        "b_qkv": a["L1_attn_bqkv"].reshape(3, DH).T,
        "w_o": a["L1_attn_Wo"],
        "b_o": a["L1_attn_bo"],
        "w_r": chunks(a["L1_ffn_Wr"].T).reshape(P, KC * K1),
        "w_a": wa,
        "w_b": wb,
        "sel": np.repeat(np.eye(K1, dtype=np.float32), RANK, axis=1),
        "ident_in": np.eye(P, dtype=np.float32),
    }


def kernel(**inputs):
    import concourse.bacc as bacc
    from concourse.bass_utils import run_bass_kernel_spmd

    nc = bacc.Bacc("TRN2", target_bir_lowering=False, num_devices=1)
    arrays, aps = {}, {}
    for name, a in layouts({k: np.asarray(v) for k, v in inputs.items()}).items():
        a = np.ascontiguousarray(a)
        arrays[f"in_{name}_dram"] = a
        aps[name] = nc.dram_tensor(f"in_{name}_dram", a.shape, mybir.dt.from_np(a.dtype), kind="ExternalInput").ap()
    aps["out"] = nc.dram_tensor("out_dram", (B, S, D), F32, kind="ExternalOutput").ap()
    two_layers(nc, **aps)
    return run_bass_kernel_spmd(nc, [arrays], core_ids=[0]).results[0]["out_dram"]
```

```python
from contextlib import ExitStack

import numpy as np

import concourse.bass as bass
from concourse import mybir

F32 = mybir.dt.float32
F32R = mybir.dt.float32r
I32 = mybir.dt.int32
ALU = mybir.AluOpType
ACT = mybir.ActivationFunctionType
AX_X = mybir.AxisListType.X

P = 128
B, S, D = 8, 256, 512
T = B * S
NT = T // P
KC = D // P
GT = 512
NG = T // GT
TPG = GT // P
EPS = 1e-5
H, DH, BLOCK = 32, 128, 32
NP_ = H // 2
SEC = KC * P
NSEC = 6
WCOLS = NSEC * SEC + 2 * SEC
OCOLS = 2 * D
FILLS = 8
MC = S + P
E, INTER, GROUPS = 16, 128, 4
NE = E + 2
XCOLS = 3 * SEC + 2
K1, RANK, TOPK = 64, 16, 16
NR = K1 * RANK // P
NEG = -3.0e38
SLOT_T = 256
CHOSEN = 2
NTILES = -(-(CHOSEN * T + E * (SLOT_T - 1)) // SLOT_T)
SLOTS = NTILES * SLOT_T
TABLES = 4
NTHR = T // SLOT_T
C_TRI, C_ONES, C_EARLY, C_THR, C_TILE = 0, P, 2 * P, 2 * P + E * E, 2 * P + E * E + NTHR
C_ALL = C_TILE + NTILES


class Chain:

    def __init__(self, eng, sem):
        self.eng, self.sem, self.n = eng, sem, 0

    def link(self, ins):
        self.n += 1
        ins.then_inc(self.sem, 1)
        self.eng.wait_ge(self.sem, self.n)


def rsqrt(v, a_sem, n, chain, var, root, rstd):
    v.wait_ge(a_sem, n)
    chain.link(v.reciprocal(rstd, root))
    chain.link(v.tensor_tensor(rstd, rstd, var, ALU.mult))
    chain.link(v.tensor_tensor(root, root, rstd, ALU.add))
    chain.link(v.tensor_scalar(root, root, 0.5, None, ALU.mult))
    chain.link(v.reciprocal(rstd, root))


def normalise_and_route(nc, acc, x_ready, xh, xl, ident, loads, xn_dram, dma_xn, split, rwh, rwl, r_lo, logits):
    name = "ln0"
    with ExitStack() as ctx:
        def sem(n):
            return ctx.enter_context(nc.semaphore(f"{name}_{n}"))

        stat = ctx.enter_context(nc.sbuf_tensor(f"{name}_stat", [P, TPG, 6], F32))
        mv = ctx.enter_context(nc.sbuf_tensor(f"{name}_mv", [P, NG, TPG, 2], F32))
        var = ctx.enter_context(nc.sbuf_tensor(f"{name}_var", [P, NG, TPG], F32))
        root = ctx.enter_context(nc.sbuf_tensor(f"{name}_root", [P, NG, TPG], F32))
        rstd = ctx.enter_context(nc.sbuf_tensor(f"{name}_rstd", [P, NG, TPG], F32))
        ps = [ctx.enter_context(nc.psum_tensor(f"{name}_ps{i}", [P, GT], F32)) for i in range(8)]
        v_chain, v_var, a_root, v_xn, pe_xt, a_hi, v_lo, pe_route, v_route = (
            sem(n) for n in ("v_chain", "v_var", "a_root", "v_xn", "pe_xt", "a_hi", "v_lo", "pe_route", "v_route"))
        block = ctx.enter_context(nc.Block())

        @block.sync
        def _(sp):
            loads(sp)
            for g in range(NG):
                sp.wait_ge(v_xn, g + 1)
                for t in range(g * TPG, (g + 1) * TPG):
                    sp.dma_start(xn_dram[t * P:(t + 1) * P, :], acc[:, t, :]).then_inc(dma_xn, 16)

        block.gpsimd(split)

        @block.vector
        def _(v):
            c = Chain(v, v_chain)

            def normalise(g):
                x_ready(v, g)
                for t in range(TPG):
                    ins = v.bn_stats(stat[:, t, :], acc[:, g * TPG + t, :])
                c.link(ins)
                for t in range(TPG):
                    ins = v.bn_aggr(mv[:, g, t, :], stat[:, t, :])
                c.link(ins)
                v.tensor_scalar(var[:, g, :], mv[:, g, :, 1], EPS, None, ALU.add).then_inc(v_var, 1)
                rsqrt(v, a_root, g + 1, c, var[:, g, :], root[:, g, :], rstd[:, g, :])
                for t in range(TPG):
                    ins = v.tensor_scalar(acc[:, g * TPG + t, :], acc[:, g * TPG + t, :], mv[:, g, t, 0:1],
                                          rstd[:, g, t:t + 1], ALU.subtract, ALU.mult)
                ins.then_inc(v_xn, 1)

            def low(g):
                for k in range(KC):
                    n = g * KC + k
                    v.wait_ge(a_hi, n + 1)
                    v.tensor_tensor(xl[:, k, g * GT:(g + 1) * GT], ps[n % 8][:],
                                    xh[:, k, g * GT:(g + 1) * GT].bitcast(F32), ALU.subtract).then_inc(v_lo, 1)

            for g in range(NG):
                normalise(g)
                if g:
                    low(g - 1)
            low(NG - 1)
            v.wait_ge(pe_route, 1)
            v.tensor_copy(logits[:], ps[0][:, 0:NT * E]).then_inc(v_route, 1)

        @block.scalar
        def _(a):
            def roots(g):
                a.wait_ge(v_var, g + 1)
                a.activation(root[:, g, :], var[:, g, :], ACT.Sqrt).then_inc(a_root, 1)

            roots(0)
            for g in range(NG):
                if g + 1 < NG:
                    roots(g + 1)
                for k in range(KC):
                    a.wait_ge(pe_xt, g * KC + k + 1)
                    a.copy(xh[:, k, g * GT:(g + 1) * GT], ps[(g * KC + k) % 8][:]).then_inc(a_hi, 1)

        @block.tensor
        def _(pe):
            for g in range(NG):
                pe.wait_ge(v_xn, g + 1)
                for k in range(KC):
                    n = g * KC + k
                    if n >= 8:
                        pe.wait_ge(v_lo, n - 7)
                    for t in range(TPG):
                        ins = pe.transpose(ps[n % 8][:, t * P:(t + 1) * P],
                                           acc[:, g * TPG + t, k * P:(k + 1) * P], ident[:])
                    ins.then_inc(pe_xt, 1)
            pe.wait_ge(v_lo, NG * KC)
            pe.wait_ge(r_lo, 1)
            for t in range(NT):
                m = slice(t * P, (t + 1) * P)
                parts = [(xh[:, k, m], xl[:, k, m], rwh[:, k, :], rwl[:, k, :]) for k in range(KC)]
                ins = three_passes(pe, ps[0][:, t * E:(t + 1) * E], parts, True, True)
            ins.then_inc(pe_route, 1)


def three_passes(pe, out, parts, start, stop):
    n = len(parts)
    for i, (wh, wl, mh, ml) in enumerate(parts):
        pe.matmul(out, wh, mh, start=start and i == 0, stop=False)
        pe.matmul(out, wh, ml, start=False, stop=False)
        ins = pe.matmul(out, wl, mh, start=False, stop=stop and i == n - 1)
    return ins


def two_layers(nc, x, w_pairs, o_pairs, decay, norm_w, router_w, router_rows, route_consts, token_ids, zeros, shared_w,
               shared_o, shared_b, ex, b3, w_qkv, b_qkv, w_o, b_o, w_r, w_a, w_b, sel, ident_in, out):
    x_tiles = x.rearrange("b (s p) d -> (b s) p d", p=P)
    out_tiles = out.rearrange("b (s p) d -> (b s) p d", p=P)
    xn_dram = nc.dram_tensor("xn_rows", (T, D), F32, kind="Internal").ap()
    token_slots = [nc.dram_tensor(f"token_slots{i}", (SLOTS, 1), I32, kind="Internal").ap() for i in range(TABLES)]
    y_slots = nc.dram_tensor("y_slots", (SLOTS, D), F32, kind="Internal").ap()
    with ExitStack() as top:
        ident = top.enter_context(nc.sbuf_tensor("ident", [P, P], F32))
        acc = top.enter_context(nc.sbuf_tensor("acc", [P, NT, D], F32))
        slot_of = top.enter_context(nc.sbuf_tensor("slot_of", [P, CHOSEN, NT], I32))
        gate_of = top.enter_context(nc.sbuf_tensor("gate_of", [P, CHOSEN, NT], F32))
        expert_of = top.enter_context(nc.sbuf_tensor("expert_of", [P, NTILES], I32))
        token_at = top.enter_context(nc.sbuf_tensor("token_at", [P, SLOTS // P], I32))
        table_in = top.enter_context(nc.semaphore("token_table_in"))
        with ExitStack() as ctx:
            attention_and_shared(nc, ctx, x_tiles, xn_dram, token_slots, w_pairs, o_pairs, decay, norm_w, router_w,
                                 router_rows, route_consts, token_ids, zeros, shared_w, shared_o, shared_b, b3, ident_in,
                                 ident, acc, slot_of, gate_of, expert_of, token_at, table_in)
        with ExitStack() as ctx:
            routed_experts(nc, ctx, ex, xn_dram, y_slots, ident, expert_of, token_at, table_in)
        with ExitStack() as ctx:
            layer_one(nc, ctx, w_qkv, b_qkv, w_o, b_o, w_r, w_a, w_b, sel, ident, acc, slot_of, gate_of, y_slots,
                      out_tiles)


def attention_and_shared(nc, ctx, x_tiles, xn_dram, token_slots, w_pairs, o_pairs, decay, norm_w, router_w,
                         router_rows, route_consts, token_ids, zeros, shared_w, shared_o, shared_b, b3, ident_in,
                         ident, acc, slot_of, gate_of, expert_of, token_at, table_in):
    def sb(name, shape, dt=F32):
        return ctx.enter_context(nc.sbuf_tensor(name, shape, dt))

    def sem(name):
        return ctx.enter_context(nc.semaphore(name))

    xh = sb("xh", [P, KC, T], F32R)
    xl = sb("xl", [P, KC, T], F32R)
    sqacc = sb("sqacc", [P, T])
    logits = sb("logits", [P, NT * E])
    wh = sb("wh", [P, WCOLS], F32R)
    wl = sb("wl", [P, WCOLS], F32R)
    oh = sb("oh", [P, OCOLS], F32R)
    ol = sb("ol", [P, OCOLS], F32R)
    tok_ids = sb("tok_ids", [P, NT], I32)
    wraw = sb("wraw", [P, WCOLS])
    oraw = sb("oraw", [P, OCOLS])
    draw = sb("draw", [P, 2, MC])
    dcur = sb("dcur", [P, 2, MC])
    nw = sb("nw", [P, H])
    nwcur = sb("nwcur", [P, 2])
    qT = sb("qT", [P, 2, GT])
    kT = sb("kT", [P, 2, GT])
    gT = sb("gT", [P, 2, GT])
    vt = sb("vt", [P, TPG, 2 * DH])
    ms = [sb(f"ms{i}", [P, MC]) for i in range(2)]
    yf = [sb(f"yf{i}", [P, GT]) for i in range(2)]
    yh = [sb(f"yh{i}", [P, GT], F32R) for i in range(2)]
    yl = [sb(f"yl{i}", [P, GT], F32R) for i in range(2)]
    sq = [sb(f"sq{i}", [P, GT]) for i in range(2)]

    s_x = [sem(f"dma_x{g}") for g in range(NG)]
    s_c = sem("dma_consts")
    dma_w, dma_o, dma_d = sem("dma_w"), sem("dma_o"), sem("dma_d")
    w_hi, w_lo, o_hi, o_lo = sem("w_hi"), sem("w_lo"), sem("o_hi"), sem("o_lo")
    nw_ready, dma_rw, r_hi, r_lo, dma_xn = (sem(n) for n in ("nw_ready", "dma_rw", "r_hi", "r_lo", "dma_xn"))
    rwh = yh[0][:, 0:KC * E].rearrange("p (k e) -> p k e", k=KC)
    rwl = yl[0][:, 0:KC * E].rearrange("p (k e) -> p k e", k=KC)

    dma_z, dma_side, dma_sh, v_side, v_shift, a_exp = (
        sem(n) for n in ("dma_z", "dma_side", "dma_sh", "v_side", "v_shift", "a_exp"))
    work = wraw[:, 0:4 * NT * E + 4 * E * E]
    spare = draw[:].rearrange("p h c -> p (h c)")
    consts, rrows, sbias = spare[:, 0:C_ALL], spare[:, C_ALL:C_ALL + 2 * E], spare[:, C_ALL + 32:C_ALL + 36]
    small = spare[:, C_ALL + 36:C_ALL + 36 + 2 * NT * GROUPS + NT]

    def section(j):
        return slice(j * SEC, (j + 1) * SEC)

    def load_pair(sp, p):
        sp.dma_start(wraw[:], w_pairs[p]).then_inc(dma_w, 16)
        sp.dma_start(oraw[:], o_pairs[p]).then_inc(dma_o, 16)
        sp.dma_start(draw[:], decay[p]).then_inc(dma_d, 16)

    def load_first(sp):
        sp.dma_start(ident[:], ident_in).then_inc(s_c, 16)
        sp.dma_start(nw[:], norm_w).then_inc(s_c, 16)
        for g in range(NG):
            for t in range(TPG):
                sp.dma_start(acc[:, g * TPG + t, :], x_tiles[g * TPG + t]).then_inc(s_x[g], 16)
        sp.dma_start(yf[0][:, 0:KC * E], router_w).then_inc(dma_rw, 16)
        load_pair(sp, 0)

    def split_first(pool):
        pool.wait_ge(s_c, 32)
        pool.tensor_scalar(nw[:], nw[:], 0.5, None, ALU.mult).then_inc(nw_ready, 1)
        pool.wait_ge(dma_rw, 16)
        pool.tensor_copy(yh[0][:, 0:KC * E], yf[0][:, 0:KC * E]).then_inc(r_hi, 1)
        pool.wait_ge(r_hi, 1)
        pool.tensor_tensor(yl[0][:, 0:KC * E], yf[0][:, 0:KC * E], yh[0][:, 0:KC * E].bitcast(F32),
                           ALU.subtract).then_inc(r_lo, 1)
        pool.wait_ge(dma_w, 16)
        for j in range(FILLS):
            c = section(j)
            pool.tensor_copy(wh[:, c], wraw[:, c]).then_inc(w_hi, 1)
            pool.wait_ge(w_hi, j + 1)
            pool.tensor_tensor(wl[:, c], wraw[:, c], wh[:, c].bitcast(F32), ALU.subtract).then_inc(w_lo, 1)
        pool.wait_ge(dma_o, 16)
        for j in range(2):
            c = slice(j * D, (j + 1) * D)
            pool.tensor_copy(oh[:, c], oraw[:, c]).then_inc(o_hi, 1)
            pool.wait_ge(o_hi, j + 1)
            pool.tensor_tensor(ol[:, c], oraw[:, c], oh[:, c].bitcast(F32), ALU.subtract).then_inc(o_lo, 1)

    def x_ready(v, g):
        if g == 0:
            v.wait_ge(s_c, 32)
        v.wait_ge(s_x[g], 16 * TPG)

    normalise_and_route(nc, acc, x_ready, xh, xl, ident, load_first, xn_dram, dma_xn, split_first, rwh, rwl, r_lo,
                        logits)

    with ExitStack() as inner:
        def ps(name):
            return inner.enter_context(nc.psum_tensor(name, [P, GT], F32))

        pj = [ps(f"proj{i}") for i in range(2)]
        sc = [ps(f"score{i}") for i in range(2)]
        ot = [ps(f"attnout{i}") for i in range(2)]
        op = [ps(f"outproj{i}") for i in range(2)]
        pe_proj, pe_s, pe_av, pe_out = sem("pe_proj"), sem("pe_s"), sem("pe_av"), sem("pe_out")
        a_ev, a_sq, a_yh = sem("a_ev"), sem("a_sq"), sem("a_yh")
        v_dec, v_mask, v_y, v_yl, v_acc, p_zero, p_sq = (
            sem(n) for n in ("v_dec", "v_mask", "v_y", "v_yl", "v_acc", "p_zero", "p_sq"))
        block = inner.enter_context(nc.Block())
        router = Routing(logits, rrows, consts, work, small, v_side, dma_side, v_shift, a_exp, (w_lo, NP_ * FILLS))

        def all_steps(eng, run):
            run(-1, NG - 1, False, True, False)
            with eng.Fori(0, NP_ - 1) as p:
                for g in range(NG):
                    run(p, g, True, True, True)
            for g in range(NG):
                run(NP_ - 1, g, True, g + 1 < NG, False)

        @block.sync
        def _(sp):
            sp.dma_start(tok_ids[:], token_ids).then_inc(dma_z, 16)
            for table in token_slots:
                cells = table.rearrange("(c n) o -> c (n o)", c=P // 8)
                sp.dma_start(cells, zeros.rearrange("(c n) -> c n", c=P // 8)).then_inc(dma_z, 16)
            with sp.Fori(1, NP_) as p:
                sp.wait_ge(w_lo, p * FILLS)
                sp.dma_start(wraw[:], w_pairs[p]).then_inc(dma_w, 16)
                sp.wait_ge(v_dec, p)
                sp.dma_start(draw[:], decay[p]).then_inc(dma_d, 16)
                sp.wait_ge(o_lo, p * 2)
                sp.dma_start(oraw[:], o_pairs[p]).then_inc(dma_o, 16)
            sp.wait_ge(v_dec, NP_)
            sp.dma_start(consts[:], route_consts).then_inc(dma_side, 16)
            sp.dma_start(rrows[:], router_rows.partition_broadcast(P)).then_inc(dma_side, 16)
            sp.dma_start(sbias[:], shared_b).then_inc(dma_side, 16)
            sp.wait_ge(w_lo, NP_ * FILLS)
            sp.dma_start(wraw[:, WCOLS - 4 * SEC:], shared_w).then_inc(dma_sh, 16)
            sp.wait_ge(o_lo, NP_ * 2)
            sp.dma_start(oraw[:], shared_o).then_inc(dma_sh, 16)

        @block.tensor
        def _(pe):
            def project_head(pn, gn, fill, j):
                if gn == 0:
                    pe.wait_ge(w_lo, pn * FILLS + j + 1)
                if not isinstance(fill, int) or fill > 1:
                    pe.wait_ge(a_ev, fill - 1)
                parts = []
                m = slice(gn * GT, (gn + 1) * GT)
                for k in range(KC):
                    c = slice(j * SEC + k * P, j * SEC + (k + 1) * P)
                    parts.append((wh[:, c], wl[:, c], xh[:, k, m], xl[:, k, m]))
                three_passes(pe, pj[j % 2][:], parts, True, True).then_inc(pe_proj, 1)

            def project_v(pn, gn, fill, j):
                if gn == 0:
                    pe.wait_ge(w_lo, pn * FILLS + FILLS)
                pe.wait_ge(a_ev, fill - 1)
                for i in range(2):
                    tok = gn * GT + ((j - NSEC) * 2 + i) * P
                    parts = []
                    for k in range(KC):
                        c = slice(NSEC * SEC + k * 2 * P, NSEC * SEC + (k + 1) * 2 * P)
                        parts.append((xh[:, k, tok:tok + P], xl[:, k, tok:tok + P], wh[:, c], wl[:, c]))
                    ins = three_passes(pe, pj[j % 2][:, i * 2 * P:(i + 1) * 2 * P], parts, True, True)
                ins.then_inc(pe_proj, 1)

            def scores(u, i):
                h, s0 = i // 2, (i % 2) * S
                if i == 0:
                    pe.wait_ge(a_ev, u * FILLS + FILLS)
                pe.matmul(sc[i % 2][:, 0:S], kT[:, h, s0:s0 + P], qT[:, h, s0:s0 + S], start=True, stop=True)
                pe.matmul(sc[i % 2][:, S:MC], kT[:, h, s0 + P:s0 + S], qT[:, h, s0 + P:s0 + S],
                          start=True, stop=True).then_inc(pe_s, 1)

            def values(u, i):
                h, b = i // 2, i % 2
                pe.wait_ge(v_mask, u * 4 + i + 1)
                c = slice(h * DH, (h + 1) * DH)
                pe.matmul(ot[h][:, b * S:(b + 1) * S], vt[:, 2 * b, c], ms[i % 2][:, 0:S], start=True, stop=False)
                pe.matmul(ot[h][:, b * S + P:(b + 1) * S], vt[:, 2 * b + 1, c], ms[i % 2][:, S:MC],
                          start=False, stop=True).then_inc(pe_av, 1)

            def project_out(p, g, u):
                if g == 0:
                    pe.wait_ge(o_lo, p * 2 + 2)
                pe.wait_ge(v_yl, u * 2 + 2)
                for t in range(TPG):
                    if t >= 2:
                        pe.wait_ge(v_acc, u * TPG + t - 1)
                    m = slice(t * P, (t + 1) * P)
                    parts = [(yh[h][:, m], yl[h][:, m], oh[:, h * D:(h + 1) * D], ol[:, h * D:(h + 1) * D])
                             for h in range(2)]
                    three_passes(pe, op[t % 2][:], parts, True, True).then_inc(pe_out, 1)

            def run(p, g, attend, project, more):
                u = p * NG + g
                pn, gn = (p, g + 1) if g + 1 < NG else (p + 1, 0)
                for what, i in (("s", 0), ("s", 1), ("p", 0), ("a", 0), ("a", 1), ("p", 1), ("s", 2), ("s", 3),
                                ("p", 2), ("a", 2), ("a", 3), ("p", 3), ("p", 4), ("p", 5), ("v", 6), ("v", 7)):
                    if what == "s" and attend:
                        scores(u, i)
                    if what == "a" and attend:
                        values(u, i)
                    if what == "p" and project:
                        project_head(pn, gn, (u + 1) * FILLS + i, i)
                    if what == "v" and project:
                        project_v(pn, gn, (u + 1) * FILLS + i, i)
                if attend:
                    project_out(p, g, u)

            all_steps(pe, run)

        @block.scalar
        def _(a):
            dst = [qT[:, 0, :], kT[:, 0, :], gT[:, 0, :], qT[:, 1, :], kT[:, 1, :], gT[:, 1, :],
                   vt[:, 0:2, :].rearrange("p t c -> p (t c)"), vt[:, 2:4, :].rearrange("p t c -> p (t c)")]

            def evacuate(u, j, attend):
                a.wait_ge(pe_proj, (u + 1) * FILLS + j + 1)
                gate = j in (2, 5)
                if gate and attend:
                    a.wait_ge(v_y, u * 2 + j // 3 + 1)
                a.activation(dst[j], pj[j % 2][:], ACT.Tanh if gate else ACT.Silu,
                             scale=0.5 if gate else 1.0).then_inc(a_ev, 1)

            def square(u, h):
                a.wait_ge(v_y, u * 2 + h + 1)
                a.wait_ge(p_sq, u * 2 + h + 1)
                a.activation(sq[h][:], ot[h][:], ACT.Square).then_inc(a_sq, 1)

            def y_high(u, h):
                a.wait_ge(v_y, u * 2 + h + 1)
                a.activation(yh[h][:], yf[h][:], ACT.Identity, scale=nwcur[:, h:h + 1]).then_inc(a_yh, 1)

            def split_high(pn, j):
                a.wait_ge(dma_w, pn * 16 + 16)
                a.copy(wh[:, section(j)], wraw[:, section(j)]).then_inc(w_hi, 1)

            def run(p, g, attend, project, more):
                u = p * NG + g
                split = more and g == 2
                for j in range(FILLS):
                    if project:
                        evacuate(u, j, attend)
                        if split and j < NSEC:
                            split_high(p + 1, j)
                    if attend and j in (0, 2):
                        square(u, j // 2)
                    if attend and j in (1, 3):
                        y_high(u, j // 2)
                    if attend and not more and g == 0 and j == 3:
                        router.exponentials(a)
                if split:
                    split_high(p + 1, 6)
                    split_high(p + 1, 7)
                if more and g == NG - 1:
                    a.wait_ge(dma_o, p * 16 + 32)
                    a.wait_ge(pe_out, u * TPG + TPG)
                    for h in range(2):
                        a.copy(oh[:, h * D:(h + 1) * D], oraw[:, h * D:(h + 1) * D]).then_inc(o_hi, 1)

            all_steps(a, run)

        @block.vector
        def _(v):
            def decays(p):
                v.wait_ge(dma_d, p * 16 + 16)
                v.tensor_copy(dcur[:], draw[:])
                v.tensor_copy(nwcur[:], nw[:, bass.ds(p * 2, 2)]).then_inc(v_dec, 1)

            def mask(p, u, i):
                v.wait_ge(pe_s, u * 4 + i + 1)
                if i == 0:
                    v.wait_ge(v_dec, p + 1)
                v.tensor_tensor(ms[i % 2][:], sc[i % 2][:, 0:MC], dcur[:, i // 2, :], ALU.mult).then_inc(v_mask, 1)

            def gated(u, h):
                v.wait_ge(pe_av, u * 4 + 2 * h + 2)
                v.scalar_tensor_tensor(yf[h][:], gT[:, h, :], 1.0, ot[h][:], ALU.add, ALU.mult).then_inc(v_y, 1)

            def y_low(u, h):
                v.wait_ge(a_yh, u * 2 + h + 1)
                v.scalar_tensor_tensor(yl[h][:], yf[h][:], nwcur[:, h:h + 1], yh[h][:].bitcast(F32),
                                       ALU.mult, ALU.subtract).then_inc(v_yl, 1)

            def run(p, g, attend, project, more):
                u = p * NG + g
                if not attend:
                    decays(0)
                    return
                for h in range(2):
                    mask(p, u, 2 * h)
                    mask(p, u, 2 * h + 1)
                    gated(u, h)
                    y_low(u, h)
                if not more:
                    router.choose(v, g)
                if more and g == NG - 1:
                    v.wait_ge(v_yl, u * 2 + 2)
                    decays(p + 1)
                for t in range(TPG):
                    tile = acc[:, g * TPG + t, :]
                    v.wait_ge(pe_out, u * TPG + t + 1)
                    if t == 0 and g == 0:
                        v.wait_ge(p_zero, 2)
                    v.tensor_tensor(tile, op[t % 2][:], tile, ALU.add).then_inc(v_acc, 1)

            all_steps(v, run)

        @block.gpsimd
        def _(pool):
            pool.wait_ge(dma_xn, 16 * NT)
            pool.memset(acc[:], 0.0).then_inc(p_zero, 1)
            pool.memset(sqacc[:], 0.0).then_inc(p_zero, 1)
            pool.sem_inc(p_sq, 2)
            pool.wait_ge(p_zero, 2)

            def add_squares(g, u, h):
                pool.wait_ge(a_sq, u * 2 + h + 1)
                pool.wait_ge(p_sq, u * 2 + h + 2)
                c = slice(g * GT, (g + 1) * GT)
                pool.tensor_tensor(sqacc[:, c], sqacc[:, c], sq[h][:], ALU.add).then_inc(p_sq, 1)

            def split_low(pn, j):
                pool.wait_ge(w_hi, pn * FILLS + j + 1)
                c = section(j)
                pool.tensor_tensor(wl[:, c], wraw[:, c], wh[:, c].bitcast(F32), ALU.subtract).then_inc(w_lo, 1)

            def run(p, g, attend, project, more):
                u = p * NG + g
                if not attend:
                    return
                for j in range(FILLS):
                    if more and g == 2:
                        split_low(p + 1, j)
                    if j in (0, 2):
                        add_squares(g, u, j // 2)
                if more and g == NG - 1:
                    for h in range(2):
                        pool.wait_ge(o_hi, p * 2 + 3 + h)
                        c = slice(h * D, (h + 1) * D)
                        pool.tensor_tensor(ol[:, c], oraw[:, c], oh[:, c].bitcast(F32),
                                           ALU.subtract).then_inc(o_lo, 1)

            all_steps(pool, run)

    with ExitStack() as inner:
        shared_expert(nc, inner, x_tiles, token_slots, b3, router, wraw, oraw, sbias, consts, wh, wl, oh, ol,
                      xh, xl, dcur, qT, kT, gT, yf, yh, yl, sq, acc, sqacc, ident, tok_ids, dma_sh, dma_z, slot_of, gate_of,
                      expert_of, token_at, table_in)


class Routing:

    def __init__(self, logits, rows, consts, work, small, v_side, dma_side, v_shift, a_exp, work_free):
        n = NT * E
        self.logits = logits[:].rearrange("p (t e) -> p t e", e=E)
        self.lg, self.sc, self.m0, self.m1 = (
            work[:, i * n:(i + 1) * n].rearrange("p (t e) -> p t e", e=E) for i in range(4))
        self.cmp = [work[:, 4 * n + i * 2 * E * E:4 * n + (i + 1) * 2 * E * E] for i in range(2)]
        self.b, self.bias = rows[:, 0:E], rows[:, E:2 * E]
        self.early = consts[:, C_EARLY:C_EARLY + E * E].rearrange("p (i j) -> p i j", i=E)
        self.consts = consts
        self.gm = small[:, 0:NT * GROUPS].rearrange("p (t g) -> p t g", g=GROUPS)
        self.keep = small[:, NT * GROUPS:2 * NT * GROUPS].rearrange("p (t g) -> p t g", g=GROUPS)
        self.red = small[:, 2 * NT * GROUPS:2 * NT * GROUPS + NT]
        self.v_side, self.dma_side, self.v_shift, self.a_exp = v_side, dma_side, v_shift, a_exp
        self.work_free, self.chain = work_free, None

    def exponentials(self, a):
        a.wait_ge(self.v_shift, 1)
        a.activation(self.lg, self.lg, ACT.Exp).then_inc(self.a_exp, 1)

    def rank(self, v, val, out, n, lower):
        c, nt = self.chain, val.shape[1]
        full = [P, nt, n, n]
        vj, vi = val.unsqueeze(2).to_broadcast(full), val.unsqueeze(3).to_broadcast(full)
        gt, ge = (x[:, 0:nt * n * n].rearrange("p (t i j) -> p t i j", i=n, j=n) for x in self.cmp)
        c.link(v.tensor_tensor(gt, vj, vi, ALU.is_gt))
        c.link(v.tensor_tensor(ge, vj, vi, ALU.is_equal))
        c.link(v.tensor_tensor(ge, ge, lower.unsqueeze(1).to_broadcast(full), ALU.mult))
        c.link(v.tensor_tensor(gt, gt, ge, ALU.add))
        c.link(v.tensor_reduce(out, gt, AX_X, ALU.add))

    def choose(self, v, g):
        over_e = [P, NT, E]
        if g == 0:
            self.chain = c = Chain(v, self.v_side)
            v.wait_ge(self.dma_side, 48)
            v.wait_ge(*self.work_free)
            c.link(v.tensor_tensor(self.lg, self.logits, self.b.unsqueeze(1).to_broadcast(over_e), ALU.add))
            c.link(v.tensor_reduce(self.red, self.lg, AX_X, ALU.max))
            v.tensor_tensor(self.lg, self.lg, self.red.unsqueeze(2).to_broadcast(over_e),
                            ALU.subtract).then_inc(self.v_shift, 1)
            v.wait_ge(self.a_exp, 1)
            c.link(v.tensor_reduce(self.red, self.lg, AX_X, ALU.add))
            c.link(v.reciprocal(self.red, self.red))
            c.link(v.tensor_tensor(self.sc, self.lg, self.red.unsqueeze(2).to_broadcast(over_e), ALU.mult))
            c.link(v.tensor_tensor(self.sc, self.sc, self.bias.unsqueeze(1).to_broadcast(over_e), ALU.add))
            by_group = [x.rearrange("p t (g e) -> p t g e", g=GROUPS) for x in (self.sc, self.lg)]
            c.link(v.tensor_reduce(self.gm, by_group[0], AX_X, ALU.max))
            self.rank(v, self.gm, self.keep, GROUPS, self.early[:, 0:GROUPS, 0:GROUPS])
            c.link(v.tensor_scalar(self.keep, self.keep, 2.0, None, ALU.is_lt))
            spread = self.keep.unsqueeze(3).to_broadcast([P, NT, GROUPS, E // GROUPS])
            c.link(v.tensor_tensor(by_group[1], by_group[0], spread, ALU.mult))
            c.link(v.tensor_scalar(self.keep, self.keep, 1.0, -NEG, ALU.subtract, ALU.mult))
            c.link(v.tensor_tensor(by_group[1], by_group[1], spread, ALU.add))
        for t in (range(0, 2, 2), range(2, 8, 2), range(8, NT, 2), ())[g]:
            self.rank(v, self.lg[:, t:t + 2, :], self.m0[:, t:t + 2, :], E, self.early)
        if g == NG - 1:
            c = self.chain
            c.link(v.tensor_scalar(self.m1, self.m0, 1.0, None, ALU.is_equal))
            c.link(v.tensor_scalar(self.m0, self.m0, 0.0, None, ALU.is_equal))
            c.link(v.tensor_tensor(self.lg, self.m0, self.m1, ALU.add))

    def place_slots(self, v, prefix, totals, slot_of, ready):
        c = self.chain
        n = NT * E
        ab = [x[:, 0:n] for x in self.cmp]

        def running(cur, other, step, length):
            while step < length:
                v.tensor_copy(other[:, 0:step], cur[:, 0:step])
                c.link(v.tensor_tensor(other[:, step:length], cur[:, step:length], cur[:, 0:length - step], ALU.add))
                cur, other, step = other, cur, 2 * step
            return cur, other

        c.link(v.tensor_copy(ab[0], totals))
        incl, free = running(ab[0], ab[1], E, n)
        above = self.cmp[0][:, n:n + E * NTHR].rearrange("p (e k) -> p e k", k=NTHR)
        tiles, ends, tmp = (self.cmp[1][:, n + i * E:n + (i + 1) * E] for i in range(3))
        thr = self.consts[:, C_THR:C_THR + NTHR].unsqueeze(1).to_broadcast([P, E, NTHR])
        c.link(v.tensor_tensor(above, incl[:, n - E:n].unsqueeze(2).to_broadcast([P, E, NTHR]), thr, ALU.is_gt))
        c.link(v.tensor_reduce(tiles, above, AX_X, ALU.add))
        c.link(v.tensor_copy(ends, tiles))
        self.ends, tmp = running(ends, tmp, 1, E)
        c.link(v.tensor_tensor(tmp, self.ends, tiles, ALU.subtract))
        c.link(v.tensor_scalar(tmp, tmp, float(SLOT_T), None, ALU.mult))
        slot = free.rearrange("p (t e) -> p t e", e=E)
        c.link(v.tensor_tensor(free, incl, totals, ALU.subtract))
        c.link(v.tensor_tensor(free, free, prefix, ALU.add))
        c.link(v.tensor_tensor(slot, slot, tmp.unsqueeze(1).to_broadcast([P, NT, E]), ALU.add))
        self.prod = incl.rearrange("p (t e) -> p t e", e=E)
        s, col = self.red, tmp
        for i, m in enumerate((self.m0, self.m1)):
            c.link(v.tensor_tensor(self.prod, m, slot, ALU.mult))
            c.link(v.tensor_reduce(s, self.prod, AX_X, ALU.add))
            c.link(v.tensor_scalar(col, s, 1.0 / P, (P - 1) / (2.0 * P), ALU.mult, ALU.subtract))
            c.link(v.tensor_scalar(col, col, 1.5 * 2.0 ** 23, None, ALU.add))
            c.link(v.tensor_scalar(col, col, 1.5 * 2.0 ** 23, 1.0 - SLOTS, ALU.subtract, ALU.mult))
            c.link(v.scalar_tensor_tensor(s, s, float(SLOTS // P), col, ALU.mult, ALU.add))
            v.tensor_copy(slot_of[:, i, :], s).then_inc(ready, 1)
            v.wait_ge(ready, i + 1)

    def gates_and_experts(self, v, gate_of, expert_of, gates, ready):
        c = self.chain
        for i, m in enumerate((self.m0, self.m1)):
            c.link(v.tensor_tensor(self.prod, m, self.sc, ALU.mult))
            c.link(v.tensor_reduce(gate_of[:, i, :], self.prod, AX_X, ALU.add))
        c.link(v.tensor_copy(self.red, self.ends))
        full = [P, NTILES, E]
        late = self.cmp[0][:, 0:NTILES * E].rearrange("p (i e) -> p i e", e=E)
        number = self.consts[:, C_TILE:C_TILE + NTILES].unsqueeze(2).to_broadcast(full)
        c.link(v.tensor_tensor(late, self.red.unsqueeze(1).to_broadcast(full), number, ALU.is_le))
        te = self.cmp[1][:, 0:NTILES]
        c.link(v.tensor_reduce(te, late, AX_X, ALU.add))
        c.link(v.tensor_scalar(te, te, float(E - 1), None, ALU.min))
        v.tensor_copy(expert_of[:], te)
        v.memset(gates[:, :, E:E + 1], 1.0)
        v.tensor_tensor(gates[:, :, 0:E], self.lg, self.sc, ALU.mult).then_inc(ready, 1)


def shared_expert(nc, outer, x_tiles, token_slots, b3, router, wraw, oraw, sbias, consts, wh, wl, oh, ol, xh, xl, dcur,
                  qT, kT, gT, yf, yh, yl, sq, acc, sqacc, ident, tok_ids, dma_sh, dma_z, slot_of, gate_of, expert_of,
                  token_at, table_in):
    def sem(name):
        return outer.enter_context(nc.semaphore(name))

    sraw = wraw[:, WCOLS - 4 * SEC:]
    names = ("sh_hi", "sh_lo", "so_hi", "so_lo", "pe_pre", "pe_sums", "pe_fill", "pe_gt", "pe_out2", "a_root2", "a_s",
             "a_gt", "a_yh2", "v_var2", "v_slots", "v_yf2", "v_yl2", "v_res", "v_acc2", "v_gates", "dma_b3", "dma_parts",
             "p_sum")
    q = {n: sem(n) for n in names}
    ids_out = [sem(f"ids_out{k}") for k in range(TABLES)]
    parts = [dcur[:, k // 2, (k % 2) * P:(k % 2) * P + SLOTS // P].bitcast(I32) for k in range(TABLES)]
    XB = 4
    x_in = [sem(f"x_in{i}") for i in range(XB)]
    xbuf = [x[:, i, :] for x in (qT, kT) for i in range(2)]
    ms = outer.enter_context(nc.sbuf_tensor("meansq", [P, 3, NT], F32))
    mean, root, rs = ms[:, 0, :], ms[:, 1, :], ms[:, 2, :]
    gate_t = sqacc[0:E + 1, :]
    b3s = sq[0][0:E + 1, :]
    gates = sq[1][:, 0:NT * (E + 1)].rearrange("p (t e) -> p t e", e=E + 1)
    fills, misc, op = ([outer.enter_context(nc.psum_tensor(f"sh_{n}{i}", [P, GT], F32)) for i in range(k)]
                       for n, k in (("fill", 4), ("misc", 2), ("out", 2)))
    block = outer.enter_context(nc.Block())

    @block.sync
    def _(sp):
        sp.dma_start(b3s, b3).then_inc(q["dma_b3"], 16)
        for t in range(NT):
            if t >= XB:
                sp.wait_ge(q["v_res"], t - XB + 1)
            sp.dma_start(xbuf[t % XB], x_tiles[t]).then_inc(x_in[t % XB], 16)

    @block.gpsimd
    def _(pool):
        pool.wait_ge(dma_z, 16 * (1 + TABLES))
        pool.wait_ge(q["v_slots"], 2)
        for n in range(NT * CHOSEN):
            t, i, k = n // CHOSEN, n % CHOSEN, n % TABLES
            if n >= TABLES:
                pool.wait_ge(ids_out[k], 16 * (n // TABLES))
            pool.indirect_dma_start(token_slots[k], bass.IndirectOffsetOnAxis(ap=slot_of[:, i, t:t + 1], axis=0),
                                    tok_ids[:, t:t + 1], None).then_inc(ids_out[k], 16)
        for k in range(TABLES):
            pool.wait_ge(ids_out[k], 16 * NT * CHOSEN // TABLES)
            pool.dma_start(parts[k], token_slots[k].rearrange("(p c) o -> p (c o)", p=P)).then_inc(q["dma_parts"], 16)
        pool.wait_ge(q["dma_parts"], 16 * TABLES)
        pool.tensor_tensor(parts[0], parts[0], parts[1], ALU.add).then_inc(q["p_sum"], 1)
        pool.tensor_tensor(parts[2], parts[2], parts[3], ALU.add).then_inc(q["p_sum"], 1)
        pool.wait_ge(q["p_sum"], 2)
        pool.tensor_tensor(token_at[:], parts[0], parts[2], ALU.add).then_inc(table_in, 1)

    @block.tensor
    def _(pe):
        def inner_fill(g, j):
            if g == 0:
                pe.wait_ge(q["sh_lo"], j + 1)
            elif j % 2 == 0:
                pe.wait_ge(q["v_yf2"], 2 * (g - 1) + j // 2 + 1)
            terms = []
            m = slice(g * GT, (g + 1) * GT)
            for k in range(KC):
                c = slice(j * SEC + k * P, j * SEC + (k + 1) * P)
                terms.append((wh[:, c], wl[:, c], xh[:, k, m], xl[:, k, m]))
            three_passes(pe, fills[j][:], terms, True, True).then_inc(q["pe_fill"], 1)

        masks = router.lg.rearrange("p t e -> p (t e)")
        pe.matmul(misc[0][:, 0:NT * E], consts[:, C_TRI:C_TRI + P], masks, start=True, stop=True)
        pe.matmul(misc[1][:, 0:NT * E], consts[:, C_ONES:C_ONES + P], masks, start=True,
                  stop=True).then_inc(q["pe_pre"], 1)
        for t in range(NT):
            ins = pe.matmul(op[0][:, t:t + 1], sqacc[:, t * P:(t + 1) * P], consts[:, C_ONES:C_ONES + 1],
                            start=True, stop=True)
        ins.then_inc(q["pe_sums"], 1)
        for g in range(2):
            for j in range(4):
                inner_fill(g, j)
        pe.wait_ge(q["v_gates"], 1)
        for g in range(NG):
            if g >= 2:
                pe.wait_ge(q["a_gt"], g - 1)
            for t in range(TPG):
                ins = pe.transpose(misc[g % 2][0:E + 1, t * P:(t + 1) * P], gates[:, g * TPG + t, :], ident[:])
            ins.then_inc(q["pe_gt"], 1)
        pe.wait_ge(q["so_lo"], 2)
        pe.wait_ge(q["dma_b3"], 16)
        for g in range(NG):
            if 0 < g < NG - 1:
                for j in range(4):
                    inner_fill(g + 1, j)
            pe.wait_ge(q["v_yl2"], 2 * g + 2)
            if g == 0:
                pe.wait_ge(q["v_var2"], 1)
            pe.wait_ge(q["a_gt"], g + 1)
            for t in range(TPG):
                n = g * TPG + t
                if n >= 2:
                    pe.wait_ge(q["v_acc2"], n - 1)
                m = slice(t * P, (t + 1) * P)
                pe.matmul(op[n % 2][:], gate_t[:, n * P:(n + 1) * P], b3s, start=True, stop=False)
                parts = [(yh[h][:, m], yl[h][:, m], oh[:, h * D:(h + 1) * D], ol[:, h * D:(h + 1) * D])
                         for h in range(2)]
                three_passes(pe, op[n % 2][:], parts, False, True).then_inc(q["pe_out2"], 1)

    @block.scalar
    def _(a):
        a.wait_ge(dma_sh, 32)
        for j in range(4):
            c = slice(j * SEC, (j + 1) * SEC)
            a.copy(wh[:, c], sraw[:, c]).then_inc(q["sh_hi"], 1)
        for h in range(2):
            c = slice(h * D, (h + 1) * D)
            a.copy(oh[:, c], oraw[:, c]).then_inc(q["so_hi"], 1)

        def half(g, h):
            a.wait_ge(q["pe_fill"], 4 * g + 2 * h + 1)
            if g:
                a.wait_ge(q["v_yf2"], 2 * (g - 1) + h + 1)
            a.activation(gT[:, h, :], fills[2 * h][:], ACT.Silu, bias=sbias[:, h:h + 1]).then_inc(q["a_s"], 1)

        def high(g, h):
            a.wait_ge(q["v_yf2"], 2 * g + h + 1)
            if g:
                a.wait_ge(q["pe_out2"], TPG * g)
            a.copy(yh[h][:], yf[h][:]).then_inc(q["a_yh2"], 1)

        a.wait_ge(q["v_var2"], 1)
        a.activation(root, mean, ACT.Sqrt).then_inc(q["a_root2"], 1)
        for g in range(NG):
            for h in range(2):
                half(g, h)
            if g == 1:
                a.wait_ge(q["pe_sums"], 1)
                for i in range(NG):
                    a.wait_ge(q["pe_gt"], i + 1)
                    a.copy(gate_t[:, i * GT:(i + 1) * GT], misc[i % 2][0:E + 1, :]).then_inc(q["a_gt"], 1)
            for h in range(2):
                high(g, h)

    @block.vector
    def _(v):
        for j in range(4):
            v.wait_ge(q["sh_hi"], j + 1)
            c = slice(j * SEC, (j + 1) * SEC)
            v.tensor_tensor(wl[:, c], sraw[:, c], wh[:, c].bitcast(F32), ALU.subtract).then_inc(q["sh_lo"], 1)
        v.wait_ge(q["pe_sums"], 1)
        v.tensor_scalar(mean, op[0][:, 0:NT], 1.0 / (H * DH), EPS, ALU.mult, ALU.add).then_inc(q["v_var2"], 1)
        v.wait_ge(q["pe_pre"], 1)
        router.place_slots(v, misc[0][:, 0:NT * E], misc[1][:, 0:NT * E], slot_of, q["v_slots"])

        def product(g, h):
            v.wait_ge(q["a_s"], 2 * g + h + 1)
            v.wait_ge(q["pe_fill"], 4 * g + 2 * h + 2)
            if g:
                v.wait_ge(q["v_yl2"], 2 * (g - 1) + h + 1)
            v.scalar_tensor_tensor(yf[h][:], fills[2 * h + 1][:], sbias[:, 2 + h:3 + h], gT[:, h, :], ALU.add,
                                   ALU.mult).then_inc(q["v_yf2"], 1)

        def low(g, h):
            v.wait_ge(q["a_yh2"], 2 * g + h + 1)
            v.tensor_tensor(yl[h][:], yf[h][:], yh[h][:].bitcast(F32), ALU.subtract).then_inc(q["v_yl2"], 1)

        for g in range(NG):
            for h in range(2):
                product(g, h)
            if g == 0:
                router.gates_and_experts(v, gate_of, expert_of, gates, q["v_gates"])
                for h in range(2):
                    v.wait_ge(q["so_hi"], h + 1)
                    cc = slice(h * D, (h + 1) * D)
                    v.tensor_tensor(ol[:, cc], oraw[:, cc], oh[:, cc].bitcast(F32), ALU.subtract).then_inc(q["so_lo"], 1)
                rsqrt(v, q["a_root2"], 1, router.chain, mean, root, rs)
            for h in range(2):
                low(g, h)
            tiles = range(g * TPG, (g + 1) * TPG)
            for t in tiles:
                v.wait_ge(x_in[t % XB], 16 * (t // XB + 1))
                v.scalar_tensor_tensor(acc[:, t, :], acc[:, t, :], rs[:, t:t + 1], xbuf[t % XB], ALU.mult,
                                       ALU.add).then_inc(q["v_res"], 1)
            for t in tiles:
                v.wait_ge(q["v_res"], t + 1)
                v.wait_ge(q["pe_out2"], t + 1)
                v.tensor_tensor(acc[:, t, :], op[t % 2][:], acc[:, t, :], ALU.add).then_inc(q["v_acc2"], 1)


def routed_experts(nc, ctx, ex, xn_dram, y_slots, ident, expert_of, token_at, table_in):
    def sb(name, shape, dt=F32):
        return ctx.enter_context(nc.sbuf_tensor(name, shape, dt))

    def pair(name, shape, dt=F32):
        return [sb(f"{name}{i}", shape, dt) for i in range(2)]

    def sem(name):
        return ctx.enter_context(nc.semaphore("e_" + name))

    W12 = 2 * SEC + 2
    raw12, raw3 = pair("eraw12", [P, W12]), pair("eraw3", [P, SEC])
    xin, cur = pair("exin", [P, 2, D]), pair("ecur", [P, 2], I32)
    eh, el, bias = pair("eh", [P, 3 * SEC], F32R), pair("el", [P, 3 * SEC], F32R), pair("ebias", [P, 2])
    xth, xtl = pair("exth", [P, KC, SLOT_T], F32R), pair("extl", [P, KC, SLOT_T], F32R)
    s1, hf = pair("es", [P, SLOT_T]), pair("ehf", [P, SLOT_T])
    hh, hl = pair("ehh", [P, SLOT_T], F32R), pair("ehl", [P, SLOT_T], F32R)
    yb = pair("ey", [P, 2, D])
    xt = [[ctx.enter_context(nc.psum_tensor(f"ext{i}{j}", [P, 2, SLOT_T], F32)) for j in range(2)] for i in range(2)]
    hp = [ctx.enter_context(nc.psum_tensor(f"ehp{i}", [P, 2, SLOT_T], F32)) for i in range(2)]
    op = [ctx.enter_context(nc.psum_tensor(f"eop{i}", [P, D], F32)) for i in range(2)]
    dma_w, dma_w3, dma_x, dma_y = ([sem(f"{n}{i}") for i in range(2)] for n in ("dma_w", "dma_w3", "dma_x", "dma_y"))
    pe_xt, pe_h, pe_o, a_hi, a_hi3, a_xh, a_s, a_hh, a_y, v_lo, v_xl, v_hf, v_hl, v_y, p_lo3, p_cur = (
        sem(n) for n in ("pe_xt", "pe_h", "pe_o", "a_hi", "a_hi3", "a_xh", "a_s", "a_hh", "a_y", "v_lo", "v_xl",
                         "v_hf", "v_hl", "v_y", "p_lo3", "p_cur"))
    y_tiles = y_slots.rearrange("(p i s) d -> i p s d", p=P, s=2)
    block = ctx.enter_context(nc.Block())

    def w(j):
        return slice(j * SEC, (j + 1) * SEC)

    def all_steps(eng, run):
        for r in (-1, 0):
            for b in range(2):
                run(r, b)
        with eng.Fori(1, NTILES // 2 - 2) as r:
            for b in range(2):
                run(r, b)
        for r in (NTILES // 2 - 2, NTILES // 2 - 1):
            for b in range(2):
                run(r, b)

    def tile(r, b, ahead):
        r, b = r + (b + ahead) // 2, (b + ahead) % 2
        i = r * 2 + b
        return not isinstance(i, int) or 0 <= i < NTILES, i, r, b

    def wait(eng, sem_, n):
        if not isinstance(n, int) or n > 0:
            eng.wait_ge(sem_, n)

    @block.sync
    def _(sp):
        def expert(i):
            return sp.value_load(expert_of[0:1, bass.ds(i, 1)], min_val=0, max_val=E - 1)

        def load12(i, b):
            e = expert(i)
            wait(sp, v_lo, i * 2 - 2)
            sp.dma_start(raw12[b][:], ex[e, :, 0:W12]).then_inc(dma_w[b], 16)

        def load3(i, b):
            e = expert(i)
            wait(sp, p_lo3, i - 1)
            sp.dma_start(raw3[b][:], ex[e, :, W12:W12 + SEC]).then_inc(dma_w3[b], 16)

        load12(0, 0)
        load12(1, 1)
        load3(0, 0)

        def run(r, b):
            is_tile, i, _, n = tile(r, b, 4)
            if is_tile:
                load12(i, n)
            is_tile, i, _, n = tile(r, b, 3)
            if is_tile:
                load3(i, n)
            is_tile, i, _, n = tile(r, b, 0)
            if is_tile:
                sp.wait_ge(a_y, i + 1)
                sp.wait_ge(v_y, i + 1)
                sp.dma_start(y_tiles[i], yb[n][:]).then_inc(dma_y[n], 16)

        all_steps(sp, run)
        for b in range(2):
            sp.wait_ge(dma_y[b], 16 * NTILES // 2)

    @block.tensor
    def _(pe):
        def rows_transposed(r, b):
            is_tile, i, half, n = tile(r, b, 2)
            if not is_tile:
                return
            pe.wait_ge(dma_x[n], half * 32 + 32)
            for h in range(2):
                wait(pe, v_xl, i * 2 - 3 + h)
                for k in range(2):
                    c = slice((2 * h + k) * P, (2 * h + k + 1) * P)
                    for s in range(2):
                        ins = pe.transpose(xt[n][h][:, k, s * P:(s + 1) * P], xin[n][:, s, c], ident[:])
                ins.then_inc(pe_xt, 1)

        def inner(r, b):
            is_tile, i, _, n = tile(r, b, 1)
            if not is_tile:
                return
            pe.wait_ge(v_xl, i * 2 + 2)
            wait(pe, v_hf, i - 1)
            for j in range(2):
                pe.wait_ge(v_lo, i * 2 + j + 1)
                parts = []
                for k in range(KC):
                    c = slice(j * SEC + k * P, j * SEC + (k + 1) * P)
                    parts.append((eh[n][:, c], el[n][:, c], xth[n][:, k, :], xtl[n][:, k, :]))
                ins = three_passes(pe, hp[n][:, j, :], parts, True, True)
            ins.then_inc(pe_h, 1)

        def outputs(r, b):
            is_tile, i, _, n = tile(r, b, 0)
            if not is_tile:
                return
            pe.wait_ge(p_lo3, i + 1)
            pe.wait_ge(v_hl, i + 1)
            for s in range(2):
                wait(pe, (a_y, v_y)[s], i)
                m = slice(s * P, (s + 1) * P)
                three_passes(pe, op[s][:], [(hh[n][:, m], hl[n][:, m], eh[n][:, w(2)], el[n][:, w(2)])], True,
                             True).then_inc(pe_o, 1)

        def run(r, b):
            rows_transposed(r, b)
            inner(r, b)
            outputs(r, b)

        all_steps(pe, run)

    @block.scalar
    def _(a):
        def run(r, b):
            is_tile, i, half, n = tile(r, b, 2)
            if is_tile:
                wait(a, pe_h, i - 1)
                for h in range(2):
                    a.wait_ge(pe_xt, i * 2 + h + 1)
                    a.copy(xth[n][:, 2 * h:2 * h + 2, :], xt[n][h][:]).then_inc(a_xh, 1)
            is_3, i3, half3, n3 = tile(r, b, 1)
            if is_3:
                wait(a, pe_o, i3 * 2 - 2)
                a.wait_ge(dma_w3[n3], half3 * 16 + 16)
                a.copy(eh[n3][:, w(2)], raw3[n3][:]).then_inc(a_hi3, 1)
            if is_tile:
                a.wait_ge(dma_w[n], half * 16 + 16)
                for j in range(2):
                    a.copy(eh[n][:, w(j)], raw12[n][:, w(j)]).then_inc(a_hi, 1)
            if is_3:
                a.wait_ge(pe_h, i3 + 1)
                wait(a, v_hf, i3 - 1)
                a.activation(s1[n3][:], hp[n3][:, 0, :], ACT.Silu, bias=bias[n3][:, 0:1]).then_inc(a_s, 1)
                a.wait_ge(v_hf, i3 + 1)
                a.copy(hh[n3][:], hf[n3][:]).then_inc(a_hh, 1)
            is_tile, i, half, n = tile(r, b, 0)
            if is_tile:
                a.wait_ge(pe_o, i * 2 + 1)
                wait(a, dma_y[n], half * 16)
                a.copy(yb[n][:, 0, :], op[0][:]).then_inc(a_y, 1)

        all_steps(a, run)

    @block.vector
    def _(v):
        def run(r, b):
            is_tile, i, half, n = tile(r, b, 2)
            if is_tile:
                for h in range(2):
                    v.wait_ge(a_xh, i * 2 + h + 1)
                    v.tensor_tensor(xtl[n][:, 2 * h:2 * h + 2, :], xt[n][h][:], xth[n][:, 2 * h:2 * h + 2, :].bitcast(F32),
                                    ALU.subtract).then_inc(v_xl, 1)
                for j in range(2):
                    v.wait_ge(a_hi, i * 2 + j + 1)
                    if j == 0:
                        wait(v, v_hf, i - 1)
                        v.tensor_copy(bias[n][:], raw12[n][:, 2 * SEC:W12])
                    v.tensor_tensor(el[n][:, w(j)], raw12[n][:, w(j)], eh[n][:, w(j)].bitcast(F32),
                                    ALU.subtract).then_inc(v_lo, 1)
            is_tile, i, half, n = tile(r, b, 1)
            if is_tile:
                v.wait_ge(a_s, i + 1)
                wait(v, v_hl, i - 1)
                v.scalar_tensor_tensor(hf[n][:], hp[n][:, 1, :], bias[n][:, 1:2], s1[n][:], ALU.add,
                                       ALU.mult).then_inc(v_hf, 1)
                v.wait_ge(a_hh, i + 1)
                v.tensor_tensor(hl[n][:], hf[n][:], hh[n][:].bitcast(F32), ALU.subtract).then_inc(v_hl, 1)
            is_tile, i, half, n = tile(r, b, 0)
            if is_tile:
                v.wait_ge(pe_o, i * 2 + 2)
                wait(v, dma_y[n], half * 16)
                v.tensor_copy(yb[n][:, 1, :], op[1][:]).then_inc(v_y, 1)

        all_steps(v, run)

    @block.gpsimd
    def _(pool):
        def indices(i, n):
            pool.wait_ge(table_in, 1)
            pool.tensor_copy(cur[n][:], token_at[:, bass.ds(i * 2, 2)]).then_inc(p_cur, 1)
            pool.wait_ge(p_cur, i + 1)

        def gather(n):
            for s in range(2):
                pool.indirect_dma_start(xin[n][:, s, :], None, xn_dram,
                                        bass.IndirectOffsetOnAxis(ap=cur[n][:, s:s + 1], axis=0)).then_inc(dma_x[n], 16)

        for b in range(2):
            indices(b, b)
            gather(b)

        def run(r, b):
            is_tile, i, half, n = tile(r, b, 4)
            if is_tile:
                wait(pool, dma_x[n], half * 32)
                indices(i, n)
                pool.wait_ge(pe_xt, i * 2 - 2)
            is_3, i3, _, n3 = tile(r, b, 1)
            if is_3:
                pool.wait_ge(a_hi3, i3 + 1)
                pool.tensor_tensor(el[n3][:, w(2)], raw3[n3][:], eh[n3][:, w(2)].bitcast(F32),
                                   ALU.subtract).then_inc(p_lo3, 1)
            if is_tile:
                gather(n)

        all_steps(pool, run)


def layer_one(nc, ctx, w_qkv, b_qkv, w_o, b_o, w_r, w_a, w_b, sel_in, ident, acc, slot_of, gate_of, y_slots, out_tiles):
    def sb(name, shape, dt=F32):
        return ctx.enter_context(nc.sbuf_tensor(name, shape, dt))

    def sem(name):
        return ctx.enter_context(nc.semaphore(name))

    QK = 3 * SEC
    RAWS = 3
    wq = [sb("l1_wqh", [P, QK], F32R), sb("l1_wql", [P, QK], F32R)]
    wo = [sb("l1_woh", [P, D], F32R), sb("l1_wol", [P, D], F32R)]
    wr = [sb("l1_wrh", [P, KC * K1], F32R), sb("l1_wrl", [P, KC * K1], F32R)]
    wa = [sb("l1_wah", [P, NR * KC * P], F32R), sb("l1_wal", [P, NR * KC * P], F32R)]
    wb = [sb("l1_wbh", [P, NR * D], F32R), sb("l1_wbl", [P, NR * D], F32R)]
    sel = sb("l1_sel", [K1, NR * P], F32R)
    bq = sb("l1_bq", [P, 3])
    bo = sb("l1_bo", [P, D])
    xh = [sb(f"x1h{i}", [P, KC, GT], F32R) for i in range(2)]
    xl = [sb(f"x1l{i}", [P, KC, GT], F32R) for i in range(2)]
    dma_c = sem("l1_dma_c")
    dma_s = [sem(f"l1_dma_s{i}") for i in range(RAWS)]
    s_hi, s_lo, s_bo = sem("l1_hi"), sem("l1_lo"), sem("l1_bo_added")

    pieces = [(w_qkv, wq, j * SEC, SEC) for j in range(3)] + [(w_r, wr, 0, KC * K1), (w_o, wo, 0, D)]
    n_sel = NR * P // D
    pieces += [(sel_in, None, j * D, D) for j in range(n_sel)]
    for j in range(NR):
        pieces += [(w_a, wa, j * SEC, SEC), (w_b, wb, j * D, D)]
    with ExitStack() as inner:
        def isb(name, shape, dt=F32):
            return inner.enter_context(nc.sbuf_tensor(name, shape, dt))

        raw = [isb(f"l1_raw{i}", [P, D]) for i in range(RAWS)]
        stage = isb("l1_stage", [P, TPG, D])
        stat = isb("l1_stat", [P, TPG, 6])
        mv = isb("l1_mv", [P, TPG, 2])
        var = isb("l1_var", [P, TPG])
        root = isb("l1_root", [P, TPG])
        rstd = isb("l1_rstd", [P, TPG])
        qkv = isb("l1_qkv", [P, 3, GT])
        vt = isb("l1_v", [P, TPG, DH])
        pr = isb("l1_p", [P, TPG, S])
        pt = [isb(f"l1_pt{i}", [P, 2 * S]) for i in range(2)]
        mx = isb("l1_mx", [P, TPG])
        sm = isb("l1_sum", [P, TPG])
        oh = isb("l1_oh", [P, GT], F32R)
        ol = isb("l1_ol", [P, GT], F32R)
        sr = isb("l1_sr", [P, TPG, K1])
        left = [isb(f"l1_left{i}", [P, TPG, K1]) for i in range(2)]
        top8 = isb("l1_top8", [P, 2, TPG, 8])
        nm = isb("l1_nm", [P, TPG])
        rz = isb("l1_rz", [P, TPG])
        gg = isb("l1_g", [P, TPG, K1])
        gh = isb("l1_gh", [K1, GT], F32R)
        gl = isb("l1_gl", [K1, GT], F32R)
        gs = isb("l1_gs", [P, GT])
        hf = isb("l1_hf", [P, GT])
        hh = [isb(f"l1_hh{i}", [P, GT], F32R) for i in range(2)]
        hl = [isb(f"l1_hl{i}", [P, GT], F32R) for i in range(2)]
        ob = [inner.enter_context(nc.psum_tensor(f"l1_ob{i}", [P, D], F32)) for i in range(TPG)]
        hb = [inner.enter_context(nc.psum_tensor(f"l1_hb{i}", [P, GT], F32)) for i in range(2)]
        mb = [inner.enter_context(nc.psum_tensor(f"l1_mb{i}", [P, GT], F32)) for i in range(2)]
        SCALE = float(np.float32(1.0) / np.sqrt(np.float32(DH)))
        names = ("pe_h", "pe_m", "pe_out", "a_qkv", "a_vt", "a_exp", "a_rexp", "a_gh", "a_pt", "a_oh", "a_ge", "a_hh",
                 "v_chain", "v_r", "v_nm", "v_max", "v_prob", "v_g", "v_gl", "v_ol", "v_hf", "v_hl", "v_fin",
                 "v_var", "a_root", "v_xn", "a_xh", "v_xl", "p_bo", "dma_y", "v_comb", "dma_out")
        q = {n: sem(f"l1_{n}") for n in names}
        block = inner.enter_context(nc.Block())

        def combine(g):
            return [("gather", g, 0), ("combine", g, 0), ("gather", g, 1), ("combine", g, 1), ("norm", g, 0)]

        events = combine(0) + [("xt", 0, k) for k in range(KC)]
        for g in range(NG + 1):
            mix = [("mix", g - 1, j) for j in range(NR)] if g else []
            if g < NG:
                events += [("qkv", g, 0), ("qkv", g, 1), ("qkv", g, 2), ("route", g, 0), ("vt", g, 0),
                           ("score", g, 0), ("score", g, 1)]
            events += mix[:NR // 2]
            if g < NG:
                events += [("probs", g, 0), ("probs", g, 1)]
            if g + 1 < NG:
                events += combine(g + 1)
            events += mix[NR // 2:]
            if g + 1 < NG:
                events += [("xt", g + 1, k) for k in range(KC)]
            if g < NG:
                events += [("gates", g, 0), ("attend", g, 0)]
        h_fill, h_taken, m_fill, m_taken = {}, [], {}, []
        for what, g, i in events:
            if what in ("qkv", "mix"):
                h_fill[what, g, i] = len(h_taken)
                h_taken.append((q["a_qkv"], 3 * g + i + 1) if what == "qkv" else (q["v_hf"], NR * g + i + 1))
            if what not in ("qkv", "norm", "gather", "combine"):
                m_fill[what, g, i] = len(m_taken)
                m_taken.append({"route": (q["v_r"], g + 1), "vt": (q["a_vt"], g + 1),
                                "score": (q["a_exp"], 2 * g + i + 1), "gates": (q["v_gl"], g + 1),
                                "probs": (q["a_pt"], 2 * g + i + 1), "attend": (q["v_ol"], g + 1),
                                "mix": (q["a_ge"], NR * g + i + 1), "xt": (q["v_xl"], KC * g + i + 1)}[what])

        @block.tensor
        def _(pe):
            def fill(banks, fills, taken, key):
                n = fills[key]
                if n >= 2:
                    pe.wait_ge(*taken[n - 2])
                return banks[n % 2]

            def outputs(g, i):
                pe.wait_ge(q["v_hl"], NR * g + i + 1)
                c = slice(i * D, (i + 1) * D)
                for t in range(TPG):
                    m = slice(t * P, (t + 1) * P)
                    ins = three_passes(pe, ob[t][:], [(hh[i % 2][:, m], hl[i % 2][:, m], wb[0][:, c], wb[1][:, c])],
                                       False, i == NR - 1)
                    if i == NR - 1:
                        ins.then_inc(q["pe_out"], 1)

            for what, g, i in events:
                if what in ("gather", "combine", "norm"):
                    continue
                if what == "qkv":
                    if i == 0:
                        pe.wait_ge(q["v_xl"], KC * (g + 1))
                    if g == 0:
                        pe.wait_ge(s_lo, i + 1)
                    bank = fill(hb, h_fill, h_taken, (what, g, i))
                    parts = []
                    for k in range(KC):
                        c = slice(i * SEC + k * P, i * SEC + (k + 1) * P)
                        parts.append((wq[0][:, c], wq[1][:, c], xh[g % 2][:, k, :], xl[g % 2][:, k, :]))
                    three_passes(pe, bank[:], parts, True, True).then_inc(q["pe_h"], 1)
                    continue
                if what != "mix":
                    bank = fill(mb, m_fill, m_taken, (what, g, i))
                if what == "route":
                    if g == 0:
                        pe.wait_ge(s_lo, 4)
                    for t in range(TPG):
                        tok = slice(t * P, (t + 1) * P)
                        parts = [(xh[g % 2][:, k, tok], xl[g % 2][:, k, tok], wr[0][:, k * K1:(k + 1) * K1],
                                  wr[1][:, k * K1:(k + 1) * K1]) for k in range(KC)]
                        ins = three_passes(pe, bank[:, t * K1:(t + 1) * K1], parts, True, True)
                elif what == "xt":
                    if i == 0:
                        pe.wait_ge(q["v_xn"], g + 1)
                    for t in range(TPG):
                        ins = pe.transpose(bank[:, t * P:(t + 1) * P], stage[:, t, i * P:(i + 1) * P], ident[:])
                elif what == "vt":
                    pe.wait_ge(q["a_qkv"], 3 * g + 3)
                    for t in range(TPG):
                        ins = pe.transpose(bank[:, t * P:(t + 1) * P], qkv[:, 2, t * P:(t + 1) * P], ident[:])
                elif what == "score":
                    for t in range(2):
                        ins = pe.matmul(bank[:, t * S:(t + 1) * S], qkv[:, 0, i * S + t * P:i * S + (t + 1) * P],
                                        qkv[:, 1, i * S:(i + 1) * S], start=True, stop=True)
                elif what == "gates":
                    pe.wait_ge(q["v_g"], g + 1)
                    for t in range(TPG):
                        ins = pe.transpose(bank[0:K1, t * P:(t + 1) * P], gg[:, t, :], ident[:])
                elif what == "probs":
                    pe.wait_ge(q["v_prob"], 2 * g + i + 1)
                    for kt in range(2):
                        for t in range(2):
                            ins = pe.transpose(bank[:, kt * S + t * P:kt * S + (t + 1) * P],
                                               pr[:, 2 * i + t, kt * P:(kt + 1) * P], ident[:])
                elif what == "attend":
                    pe.wait_ge(q["a_pt"], 2 * g + 2)
                    for b in range(2):
                        for kt in range(2):
                            ins = pe.matmul(bank[:, b * S:(b + 1) * S], vt[:, 2 * b + kt, :],
                                            pt[b][:, kt * S:(kt + 1) * S], start=kt == 0, stop=kt == 1)
                elif what == "mix":
                    if i == 0:
                        pe.wait_ge(q["v_ol"], g + 1)
                        if g == 0:
                            pe.wait_ge(s_lo, 5)
                        for t in range(TPG):
                            if g:
                                pe.wait_ge(q["v_fin"], TPG * (g - 1) + t + 1)
                            tt = slice(t * P, (t + 1) * P)
                            three_passes(pe, ob[t][:], [(oh[:, tt], ol[:, tt], wo[0][:], wo[1][:])], True, False)
                    bank = fill(hb, h_fill, h_taken, (what, g, i))
                    if g == 0:
                        pe.wait_ge(s_lo, 5 + n_sel + 2 * i + 2)
                    parts = []
                    for k in range(KC):
                        c = slice(i * SEC + k * P, i * SEC + (k + 1) * P)
                        parts.append((wa[0][:, c], wa[1][:, c], xh[g % 2][:, k, :], xl[g % 2][:, k, :]))
                    three_passes(pe, bank[:], parts, True, True).then_inc(q["pe_h"], 1)
                    bank = fill(mb, m_fill, m_taken, (what, g, i))
                    if i == 0:
                        pe.wait_ge(q["v_gl"], g + 1)
                    s = sel[:, i * P:(i + 1) * P]
                    pe.matmul(bank[:], s, gh[:], start=True, stop=False)
                    ins = pe.matmul(bank[:], s, gl[:], start=False, stop=True)
                ins.then_inc(q["pe_m"], 1)
                if what == "mix" and i:
                    outputs(g, i - 1)
                if what == "mix" and i == NR - 1:
                    outputs(g, i)

        @block.scalar
        def _(a):
            for what, g, i in events:
                if what in ("gather", "combine"):
                    continue
                if what == "norm":
                    a.wait_ge(q["v_var"], g + 1)
                    a.activation(root[:], var[:], ACT.Sqrt).then_inc(q["a_root"], 1)
                    continue
                if what == "qkv":
                    n = h_fill[what, g, i]
                    if g == i == 0:
                        a.wait_ge(dma_c, 32)
                    a.wait_ge(q["pe_h"], n + 1)
                    if g:
                        a.wait_ge(q["pe_m"], m_fill["attend", g - 1, 0] + 1)
                    a.activation(qkv[:, i, :], hb[n % 2][:], ACT.Identity, bias=bq[:, i:i + 1]).then_inc(q["a_qkv"], 1)
                    continue
                n = m_fill[what, g, i]
                bank = mb[n % 2]
                if what == "route":
                    a.wait_ge(q["v_nm"], g + 1)
                    for t in range(TPG):
                        ins = a.activation(gg[:, t, :], sr[:, t, :], ACT.Exp, bias=nm[:, t:t + 1])
                    ins.then_inc(q["a_rexp"], 1)
                    continue
                if what == "score":
                    a.wait_ge(q["v_max"], 2 * g + i + 1)
                    for t in range(2):
                        ins = a.activation(pr[:, 2 * i + t, :], bank[:, t * S:(t + 1) * S], ACT.Exp,
                                           bias=mx[:, 2 * i + t:2 * i + t + 1], scale=SCALE,
                                           accum_out=sm[:, 2 * i + t:2 * i + t + 1])
                    ins.then_inc(q["a_exp"], 1)
                    continue
                a.wait_ge(q["pe_m"], n + 1)
                if what == "xt":
                    a.copy(xh[g % 2][:, i, :], bank[:]).then_inc(q["a_xh"], 1)
                elif what == "vt":
                    a.copy(vt[:].rearrange("p t d -> p (t d)"), bank[:]).then_inc(q["a_vt"], 1)
                elif what == "gates":
                    a.copy(gh[:], bank[0:K1, :]).then_inc(q["a_gh"], 1)
                elif what == "probs":
                    a.copy(pt[i][:], bank[:]).then_inc(q["a_pt"], 1)
                elif what == "attend":
                    a.copy(oh[:], bank[:]).then_inc(q["a_oh"], 1)
                elif what == "mix":
                    a.copy(gs[:], bank[:]).then_inc(q["a_ge"], 1)
                    a.wait_ge(q["v_hf"], NR * g + i + 1)
                    a.copy(hh[i % 2][:], hf[:]).then_inc(q["a_hh"], 1)

        @block.vector
        def _(v):
            c = Chain(v, q["v_chain"])
            for what, g, i in events:
                if what in ("vt", "qkv", "probs", "gather"):
                    continue
                if what == "combine":
                    v.wait_ge(q["dma_y"], 16 * TPG * (2 * g + i + 1))
                    if i:
                        v.wait_ge(q["v_comb"], TPG * (2 * g + 1))
                    for t in range(TPG):
                        tt = g * TPG + t
                        v.scalar_tensor_tensor(acc[:, tt, :], stage[:, t, :], gate_of[:, i, tt:tt + 1], acc[:, tt, :],
                                               ALU.mult, ALU.add).then_inc(q["v_comb"], 1)
                    continue
                if what == "norm":
                    tiles = range(g * TPG, (g + 1) * TPG)
                    v.wait_ge(q["v_comb"], 2 * TPG * (g + 1))
                    for t in tiles:
                        ins = v.bn_stats(stat[:, t % TPG, :], acc[:, t, :])
                    c.link(ins)
                    for t in range(TPG):
                        ins = v.bn_aggr(mv[:, t, :], stat[:, t, :])
                    c.link(ins)
                    v.tensor_scalar(var[:], mv[:, :, 1], EPS, None, ALU.add).then_inc(q["v_var"], 1)
                    v.wait_ge(q["v_var"], g + 1)
                    rsqrt(v, q["a_root"], g + 1, c, var[:], root[:], rstd[:])
                    for t in tiles:
                        ins = v.tensor_scalar(stage[:, t % TPG, :], acc[:, t, :], mv[:, t % TPG, 0:1],
                                              rstd[:, t % TPG:t % TPG + 1], ALU.subtract, ALU.mult)
                    ins.then_inc(q["v_xn"], 1)
                    continue
                n = m_fill[what, g, i]
                bank = mb[n % 2]
                if what == "route":
                    v.wait_ge(q["pe_m"], n + 1)
                    v.tensor_copy(sr[:].rearrange("p t k -> p (t k)"), bank[:, 0:TPG * K1]).then_inc(q["v_r"], 1)
                    v.wait_ge(q["v_r"], g + 1)
                    for t in range(TPG):
                        ins = v.max(top8[:, 0, t, :], sr[:, t, :])
                    c.link(ins)
                    v.tensor_scalar(nm[:], top8[:, 0, :, 0], -1.0, None, ALU.mult).then_inc(q["v_nm"], 1)
                    for t in range(TPG):
                        ins = v.match_replace(left[0][:, t, :], top8[:, 0, t, :], sr[:, t, :], NEG)
                    c.link(ins)
                    for t in range(TPG):
                        ins = v.max(top8[:, 1, t, :], left[0][:, t, :])
                    c.link(ins)
                    for t in range(TPG):
                        ins = v.match_replace(left[1][:, t, :], top8[:, 1, t, :], left[0][:, t, :], NEG)
                    c.link(ins)
                    c.link(v.tensor_tensor(left[0][:], left[1][:], sr[:], ALU.not_equal))
                    v.wait_ge(q["a_rexp"], g + 1)
                    c.link(v.tensor_tensor(gg[:], gg[:], left[0][:], ALU.mult))
                    c.link(v.tensor_reduce(rz[:], gg[:], AX_X, ALU.add))
                    c.link(v.reciprocal(rz[:], rz[:]))
                    for t in range(TPG):
                        ins = v.tensor_scalar(gg[:, t, :], gg[:, t, :], rz[:, t:t + 1], 2.0, ALU.mult, ALU.mult)
                    ins.then_inc(q["v_g"], 1)
                elif what == "score":
                    v.wait_ge(q["pe_m"], n + 1)
                    t2 = slice(2 * i, 2 * i + 2)
                    c.link(v.tensor_reduce(mx[:, t2], bank[:].rearrange("p (t s) -> p t s", t=2), AX_X, ALU.max))
                    v.tensor_scalar(mx[:, t2], mx[:, t2], -SCALE, None, ALU.mult).then_inc(q["v_max"], 1)
                    v.wait_ge(q["a_exp"], 2 * g + i + 1)
                    c.link(v.reciprocal(sm[:, t2], sm[:, t2]))
                    for t in range(2):
                        ins = v.tensor_scalar(pr[:, 2 * i + t, :], pr[:, 2 * i + t, :], sm[:, 2 * i + t:2 * i + t + 1],
                                              None, ALU.mult)
                    ins.then_inc(q["v_prob"], 1)
                elif what == "xt":
                    v.wait_ge(q["a_xh"], KC * g + i + 1)
                    v.tensor_tensor(xl[g % 2][:, i, :], bank[:], xh[g % 2][:, i, :].bitcast(F32),
                                    ALU.subtract).then_inc(q["v_xl"], 1)
                elif what == "gates":
                    v.wait_ge(q["a_gh"], g + 1)
                    v.tensor_tensor(gl[:], bank[0:K1, :], gh[:].bitcast(F32),
                                    ALU.subtract).then_inc(q["v_gl"], 1)
                elif what == "attend":
                    v.wait_ge(q["a_oh"], g + 1)
                    v.tensor_tensor(ol[:], bank[:], oh[:].bitcast(F32), ALU.subtract).then_inc(q["v_ol"], 1)
                elif what == "mix":
                    h = h_fill[what, g, i]
                    v.wait_ge(q["pe_h"], h + 1)
                    v.wait_ge(q["a_ge"], NR * g + i + 1)
                    if NR * g + i:
                        v.wait_ge(q["v_hl"], NR * g + i)
                    v.tensor_tensor(hf[:], hb[h % 2][:], gs[:], ALU.mult).then_inc(q["v_hf"], 1)
                    v.wait_ge(q["a_hh"], NR * g + i + 1)
                    v.tensor_tensor(hl[i % 2][:], hf[:], hh[i % 2][:].bitcast(F32),
                                    ALU.subtract).then_inc(q["v_hl"], 1)
                    if i == NR - 1:
                        for t in range(TPG):
                            tile = acc[:, g * TPG + t, :]
                            v.wait_ge(q["pe_out"], g * TPG + t + 1)
                            v.wait_ge(q["p_bo"], g * TPG + t + 1)
                            v.tensor_tensor(tile, ob[t][:], tile, ALU.add).then_inc(q["v_fin"], 1)

        @block.gpsimd
        def _(pool):
            def split(n):
                _, dst, c0, w = pieces[n]
                c, r = slice(c0, c0 + w), raw[n % RAWS]
                pool.wait_ge(dma_s[n % RAWS], 16 * (n // RAWS + 1))
                if dst is None:
                    pool.tensor_copy(sel[:, c], r[0:K1, :]).then_inc(s_lo, 1)
                    return
                pool.tensor_copy(dst[0][:, c], r[:, 0:w]).then_inc(s_hi, 1)
                pool.wait_ge(s_hi, n + 1 - (n_sel if n > 5 else 0))
                pool.tensor_tensor(dst[1][:, c], r[:, 0:w], dst[0][:, c].bitcast(F32), ALU.subtract).then_inc(s_lo, 1)

            def gather(g, i):
                if i:
                    pool.wait_ge(q["v_comb"], TPG * (2 * g + 1))
                elif g:
                    pool.wait_ge(q["pe_m"], m_fill["xt", g - 1, KC - 1] + 1)
                for t in range(TPG):
                    tt = g * TPG + t
                    pool.indirect_dma_start(
                        stage[:, t, :], None, y_slots,
                        bass.IndirectOffsetOnAxis(ap=slot_of[:, i, tt:tt + 1], axis=0)).then_inc(q["dma_y"], 16)

            gather(0, 0)
            for n in range(2):
                split(n)
            gather(0, 1)
            for n in range(2, len(pieces)):
                split(n)
            pool.wait_ge(dma_c, 32)
            for g in range(NG):
                for t in range(g * TPG, (g + 1) * TPG):
                    if t % TPG == 0:
                        pool.wait_ge(q["v_xn"], g + 1)
                    pool.tensor_tensor(acc[:, t, :], acc[:, t, :], bo[:], ALU.add).then_inc(q["p_bo"], 1)
                if g + 1 < NG:
                    gather(g + 1, 0)
                    gather(g + 1, 1)

        @block.sync
        def _(sp):
            sp.dma_start(bq[:], b_qkv).then_inc(dma_c, 16)
            sp.dma_start(bo[:], b_o.partition_broadcast(P)).then_inc(dma_c, 16)
            for n, (src, dst, c0, w) in enumerate(pieces):
                if n >= RAWS:
                    sp.wait_ge(s_lo, n - RAWS + 1)
                rows = P if dst else K1
                sp.dma_start(raw[n % RAWS][0:rows, 0:w], src[:, c0:c0 + w]).then_inc(dma_s[n % RAWS], 16)
            for t in range(NT):
                sp.wait_ge(q["v_fin"], t + 1)
                sp.dma_start(out_tiles[t], acc[:, t, :]).then_inc(q["dma_out"], 16)
            sp.wait_ge(q["dma_out"], 16 * NT)


def decay_tables():
    slope = (1.0 / 2.0 ** (8.0 / H)) ** (np.arange(H) + 1.0) * (1.0 - 1.0 / (31 + 1e-5) + 1e-5)
    n_m = np.arange(S)[None, :] - np.arange(P)[:, None]
    d = np.where(n_m >= 0, np.exp(-slope[:, None, None] * np.maximum(n_m, 0)), 0.0).astype(np.float32)
    d = np.concatenate([d, d[:, :, :P]], 2)
    return np.ascontiguousarray(d.reshape(NP_, 2, P, MC).transpose(0, 2, 1, 3))


def route_consts():
    def rows(x):
        return np.broadcast_to(np.asarray(x, np.float32), (P, len(x)))

    return np.concatenate([
        np.triu(np.ones((P, P), np.float32), 1), np.ones((P, P), np.float32),
        rows(np.tril(np.ones((E, E)), -1).reshape(E * E)), rows(np.arange(NTHR) * SLOT_T),
        rows(np.arange(NTILES))], 1)


def chunks(w):
    return w.reshape(KC, P, -1).transpose(1, 0, 2)


def layouts(a):
    qkv = a["L0_attn_qkv_w"].reshape(H, 3, DH, KC, P).transpose(0, 1, 4, 3, 2)
    gate = a["L0_attn_gate_w"].reshape(H, DH, KC, P).transpose(0, 3, 2, 1)
    sections = [w[h::2].reshape(NP_, P, SEC) for h in range(2) for w in (qkv[:, 0], qkv[:, 1], gate)]
    v = np.stack([qkv[0::2, 2], qkv[1::2, 2]], 3).reshape(NP_, P, 2 * SEC)

    def first(w):
        return w.reshape(-1, KC, P, INTER).transpose(0, 2, 1, 3).reshape(-1, P, SEC)

    biases = [a[f"L0_ffn_eb{i}"][:, :, None] for i in (1, 2)]
    ex = np.concatenate([first(a["L0_ffn_ew1"]), first(a["L0_ffn_ew2"])] + biases + [a["L0_ffn_ew3"]], 2)
    halves = [a[n].reshape(KC, P, 2, INTER).transpose(2, 1, 0, 3).reshape(2, P, SEC) for n in ("L0_ffn_sw1", "L0_ffn_sw2")]
    wqkv = a["L1_attn_Wqkv"].reshape(KC, P, 3, DH).transpose(1, 2, 0, 3).reshape(P, 3 * SEC)
    wa = a["L1_ffn_A"].reshape(NR, P, KC, P).transpose(3, 0, 2, 1).reshape(P, NR * SEC)
    wb = a["L1_ffn_B"].transpose(0, 2, 1).reshape(NR, P, D).transpose(1, 0, 2).reshape(P, NR * D)
    return {
        "x": a["L0_attn_hidden_states"],
        "w_pairs": np.concatenate(sections + [v], 2),
        "o_pairs": a["L0_attn_out_w"].T.reshape(NP_, 2, P, D).transpose(0, 2, 1, 3).reshape(NP_, P, OCOLS),
        "decay": decay_tables(),
        "norm_w": a["L0_attn_norm_w"].reshape(H, DH).T,
        "router_w": chunks(a["L0_ffn_router_w"]).reshape(P, KC * E),
        "router_rows": np.concatenate([a["L0_ffn_router_b"], a["L0_ffn_router_bias"]]),
        "route_consts": route_consts(),
        "zeros": np.zeros(SLOTS, np.int32),
        "token_ids": np.arange(T, dtype=np.int32).reshape(NT, P).T,
        "shared_w": np.concatenate([halves[0][0], halves[1][0], halves[0][1], halves[1][1]], 1),
        "shared_o": a["L0_ffn_sw3"].reshape(2, INTER, D).transpose(1, 0, 2).reshape(P, OCOLS),
        "shared_b": np.concatenate([a["L0_ffn_sb1"].reshape(2, INTER), a["L0_ffn_sb2"].reshape(2, INTER)]).T,
        "ex": ex,
        "b3": np.concatenate([a["L0_ffn_eb3"], a["L0_ffn_sb3"][None]], 0),
        "w_qkv": wqkv,
        "b_qkv": a["L1_attn_bqkv"].reshape(3, DH).T,
        "w_o": a["L1_attn_Wo"],
        "b_o": a["L1_attn_bo"],
        "w_r": chunks(a["L1_ffn_Wr"].T).reshape(P, KC * K1),
        "w_a": wa,
        "w_b": wb,
        "sel": np.repeat(np.eye(K1, dtype=np.float32), RANK, axis=1),
        "ident_in": np.eye(P, dtype=np.float32),
    }


def kernel(**inputs):
    import concourse.bacc as bacc
    from concourse.bass_utils import run_bass_kernel_spmd

    nc = bacc.Bacc("TRN2", target_bir_lowering=False, num_devices=1)
    arrays, aps = {}, {}
    for name, a in layouts({k: np.asarray(v) for k, v in inputs.items()}).items():
        a = np.ascontiguousarray(a)
        arrays[f"in_{name}_dram"] = a
        aps[name] = nc.dram_tensor(f"in_{name}_dram", a.shape, mybir.dt.from_np(a.dtype), kind="ExternalInput").ap()
    aps["out"] = nc.dram_tensor("out_dram", (B, S, D), F32, kind="ExternalOutput").ap()
    two_layers(nc, **aps)
    return run_bass_kernel_spmd(nc, [arrays], core_ids=[0]).results[0]["out_dram"]
```

```python
from contextlib import ExitStack

import numpy as np

import concourse.bass as bass
from concourse import mybir

F32 = mybir.dt.float32
F32R = mybir.dt.float32r
I32 = mybir.dt.int32
ALU = mybir.AluOpType
ACT = mybir.ActivationFunctionType
AX_X = mybir.AxisListType.X

P = 128
B, S, D = 8, 256, 512
T = B * S
NT = T // P
KC = D // P
GT = 512
NG = T // GT
TPG = GT // P
EPS = 1e-5
H, DH = 32, 128
NP_ = H // 2
SEC = KC * P
NSEC = 6
WCOLS = NSEC * SEC + 2 * SEC
OCOLS = 2 * D
FILLS = 8
MC = S + P
E, INTER, GROUPS = 16, 128, 4
K1, RANK = 64, 16
NR = K1 * RANK // P
NEG = -3.0e38
L_R = 3 * SEC
L_O = L_R + KC * K1
L_A = L_O + D
L_B = L_A + NR * SEC
L_USED = L_B + NR * D
PIECE = 384
PIECES = -(-L_USED // PIECE)
L_ALL = PIECES * PIECE
SLOT_T = 256
CHOSEN = 2
NTILES = E + (CHOSEN * T - E) // SLOT_T
SLOTS = NTILES * SLOT_T
TABLES = 4
NTHR = T // SLOT_T
C_TRI, C_ONES, C_EARLY, C_THR, C_TILE = 0, P, 2 * P, 2 * P + E * E, 2 * P + E * E + NTHR
C_ALL = C_TILE + NTILES


class Chain:

    def __init__(self, eng, sem):
        self.eng, self.sem, self.n = eng, sem, 0

    def link(self, ins):
        self.n += 1
        ins.then_inc(self.sem, 1)
        self.eng.wait_ge(self.sem, self.n)


def rsqrt(v, a_sem, n, chain, var, root, rstd):
    v.wait_ge(a_sem, n)
    chain.link(v.reciprocal(rstd, root))
    chain.link(v.tensor_tensor(rstd, rstd, var, ALU.mult))
    chain.link(v.tensor_tensor(root, root, rstd, ALU.add))
    chain.link(v.tensor_scalar(root, root, 0.5, None, ALU.mult))
    chain.link(v.reciprocal(rstd, root))


def normalise_and_route(nc, acc, x_ready, xh, xl, ident, loads, xn_dram, dma_xn, split_high, split_low, rwh,
                        rwl, r_lo, lt, logits):
    name = "ln0"
    with ExitStack() as ctx:
        def sem(n):
            return ctx.enter_context(nc.semaphore(f"{name}_{n}"))

        stat = ctx.enter_context(nc.sbuf_tensor(f"{name}_stat", [P, TPG, 6], F32))
        mv = ctx.enter_context(nc.sbuf_tensor(f"{name}_mv", [P, NG, TPG, 2], F32))
        var = ctx.enter_context(nc.sbuf_tensor(f"{name}_var", [P, NG, TPG], F32))
        root = ctx.enter_context(nc.sbuf_tensor(f"{name}_root", [P, NG, TPG], F32))
        rstd = ctx.enter_context(nc.sbuf_tensor(f"{name}_rstd", [P, NG, TPG], F32))
        ps = [ctx.enter_context(nc.psum_tensor(f"{name}_ps{i}", [P, GT], F32)) for i in range(8)]
        xt, rt, ps_l = ps[:6], ps[6], ps[7]
        v_chain, v_var, a_root, v_xn, pe_xt, a_hi, v_lo, pe_rt, a_rt, pe_route, v_route = (
            sem(n) for n in ("v_chain", "v_var", "a_root", "v_xn", "pe_xt", "a_hi", "v_lo", "pe_rt", "a_rt",
                             "pe_route", "v_route"))
        block = ctx.enter_context(nc.Block())

        @block.sync
        def _(sp):
            loads(sp)
            for g in range(NG):
                sp.wait_ge(v_xn, g + 1)
                for t in range(g * TPG, (g + 1) * TPG):
                    sp.dma_start(xn_dram[t * P:(t + 1) * P, :], acc[:, t, :]).then_inc(dma_xn, 16)

        block.gpsimd(split_low)

        @block.vector
        def _(v):
            c = Chain(v, v_chain)

            def normalise(g):
                x_ready(v, g)
                for t in range(TPG):
                    ins = v.bn_stats(stat[:, t, :], acc[:, g * TPG + t, :])
                c.link(ins)
                for t in range(TPG):
                    ins = v.bn_aggr(mv[:, g, t, :], stat[:, t, :])
                c.link(ins)
                v.tensor_scalar(var[:, g, :], mv[:, g, :, 1], EPS, None, ALU.add).then_inc(v_var, 1)
                rsqrt(v, a_root, g + 1, c, var[:, g, :], root[:, g, :], rstd[:, g, :])
                for t in range(TPG):
                    ins = v.tensor_scalar(acc[:, g * TPG + t, :], acc[:, g * TPG + t, :], mv[:, g, t, 0:1],
                                          rstd[:, g, t:t + 1], ALU.subtract, ALU.mult)
                ins.then_inc(v_xn, 1)

            def low(g):
                for k in range(KC):
                    n = g * KC + k
                    v.wait_ge(a_hi, n + 1)
                    v.tensor_tensor(xl[:, k, g * GT:(g + 1) * GT], xt[n % 6][:],
                                    xh[:, k, g * GT:(g + 1) * GT].bitcast(F32), ALU.subtract).then_inc(v_lo, 1)

            for g in range(NG):
                normalise(g)
                if g:
                    low(g - 1)
            low(NG - 1)
            v.wait_ge(pe_route, 1)
            v.tensor_copy(logits[:], ps_l[:, 0:NT * E]).then_inc(v_route, 1)

        @block.scalar
        def _(a):
            def roots(g):
                a.wait_ge(v_var, g + 1)
                a.activation(root[:, g, :], var[:, g, :], ACT.Sqrt).then_inc(a_root, 1)

            def route_taken(g):
                a.wait_ge(pe_rt, g + 1)
                a.copy(lt[g], rt[0:E, :]).then_inc(a_rt, 1)

            roots(0)
            for g in range(NG):
                if g + 1 < NG:
                    roots(g + 1)
                for k in range(KC):
                    a.wait_ge(pe_xt, g * KC + k + 1)
                    a.copy(xh[:, k, g * GT:(g + 1) * GT], xt[(g * KC + k) % 6][:]).then_inc(a_hi, 1)
                if g:
                    route_taken(g - 1)
                if g == NG - 2:
                    split_high(a)
            route_taken(NG - 1)

        @block.tensor
        def _(pe):
            def route(g):
                pe.wait_ge(v_lo, KC * (g + 1))
                if g == 0:
                    pe.wait_ge(r_lo, 1)
                else:
                    pe.wait_ge(a_rt, g)
                m = slice(g * GT, (g + 1) * GT)
                parts = [(rwh[:, k, :], rwl[:, k, :], xh[:, k, m], xl[:, k, m]) for k in range(KC)]
                three_passes(pe, rt[0:E, :], parts, True, True).then_inc(pe_rt, 1)

            for g in range(NG):
                pe.wait_ge(v_xn, g + 1)
                for k in range(KC):
                    n = g * KC + k
                    if n >= 6:
                        pe.wait_ge(v_lo, n - 5)
                    for t in range(TPG):
                        ins = pe.transpose(xt[n % 6][:, t * P:(t + 1) * P],
                                           acc[:, g * TPG + t, k * P:(k + 1) * P], ident[:])
                    ins.then_inc(pe_xt, 1)
                if g:
                    route(g - 1)
            route(NG - 1)
            for t in range(NT):
                if t % TPG == 0:
                    pe.wait_ge(a_rt, t // TPG + 1)
                ins = pe.transpose(ps_l[:, t * E:(t + 1) * E], lt[t // TPG][:, t % TPG * P:(t % TPG + 1) * P],
                                   ident[0:E, 0:E])
            ins.then_inc(pe_route, 1)


def three_passes(pe, out, parts, start, stop):
    n = len(parts)
    for i, (wh, wl, mh, ml) in enumerate(parts):
        pe.matmul(out, wh, mh, start=start and i == 0, stop=False)
        pe.matmul(out, wh, ml, start=False, stop=False)
        ins = pe.matmul(out, wl, mh, start=False, stop=stop and i == n - 1)
    return ins


def two_layers(nc, x, w_pairs, o_pairs, decay, norm_w, router_w, router_rows, route_consts, token_ids, zeros, shared_w,
               shared_o, shared_b, ex, b3, l1_w, b_qkv, b_o, sel, ident_in, out):
    x_tiles = x.rearrange("b (s p) d -> (b s) p d", p=P)
    out_tiles = out.rearrange("b (s p) d -> (b s) p d", p=P)
    xn_dram = nc.dram_tensor("xn_rows", (T, D), F32, kind="Internal").ap()
    token_slots = [nc.dram_tensor(f"token_slots{i}", (SLOTS, 1), I32, kind="Internal").ap() for i in range(TABLES)]
    y_slots = nc.dram_tensor("y_slots", (SLOTS, D), F32, kind="Internal").ap()
    with ExitStack() as top:
        ident = top.enter_context(nc.sbuf_tensor("ident", [P, P], F32))
        acc = top.enter_context(nc.sbuf_tensor("acc", [P, NT, D], F32))
        slot_of = top.enter_context(nc.sbuf_tensor("slot_of", [P, CHOSEN, NT], I32))
        gate_of = top.enter_context(nc.sbuf_tensor("gate_of", [P, CHOSEN, NT], F32))
        expert_of = top.enter_context(nc.sbuf_tensor("expert_of", [P, NTILES], I32))
        token_at = top.enter_context(nc.sbuf_tensor("token_at", [P, SLOTS // P], I32))
        table_in = top.enter_context(nc.semaphore("token_table_in"))
        with ExitStack() as ctx:
            attention_and_shared(nc, ctx, x_tiles, xn_dram, token_slots, w_pairs, o_pairs, decay, norm_w, router_w,
                                 router_rows, route_consts, token_ids, zeros, shared_w, shared_o, shared_b, b3, ident_in,
                                 ident, acc, slot_of, gate_of, expert_of, token_at, table_in)
        with ExitStack() as ctx:
            w1h = ctx.enter_context(nc.sbuf_tensor("l1_wh", [P, L_ALL], F32R))
            w1l = ctx.enter_context(nc.sbuf_tensor("l1_wl", [P, L_ALL], F32R))
            with ExitStack() as inner:
                routed_experts(nc, inner, ex, l1_w, xn_dram, y_slots, ident, expert_of, token_at, table_in, w1h, w1l)
            layer_one(nc, ctx, w1h, w1l, b_qkv, b_o, sel, ident, acc, slot_of, gate_of, y_slots, out_tiles)


def attention_and_shared(nc, ctx, x_tiles, xn_dram, token_slots, w_pairs, o_pairs, decay, norm_w, router_w,
                         router_rows, route_consts, token_ids, zeros, shared_w, shared_o, shared_b, b3, ident_in,
                         ident, acc, slot_of, gate_of, expert_of, token_at, table_in):
    def sb(name, shape, dt=F32):
        return ctx.enter_context(nc.sbuf_tensor(name, shape, dt))

    def sem(name):
        return ctx.enter_context(nc.semaphore(name))

    xh = sb("xh", [P, KC, T], F32R)
    xl = sb("xl", [P, KC, T], F32R)
    sqacc = sb("sqacc", [P, T])
    logits = sb("logits", [P, NT * E])
    wh = sb("wh", [P, WCOLS], F32R)
    wl = sb("wl", [P, WCOLS], F32R)
    oh = sb("oh", [P, OCOLS], F32R)
    ol = sb("ol", [P, OCOLS], F32R)
    tok_ids = sb("tok_ids", [P, NT], I32)
    wraw = sb("wraw", [P, WCOLS])
    draw = sb("draw", [P, 2, MC])
    dcur = sb("dcur", [P, 2, MC])
    nw = sb("nw", [P, H])
    nwcur = sb("nwcur", [P, 2])
    qT = sb("qT", [P, 2, GT])
    kT = sb("kT", [P, 2, GT])
    gT = sb("gT", [P, 2, GT])
    vt = sb("vt", [P, TPG, 2 * DH])
    ms = [sb(f"ms{i}", [P, MC]) for i in range(2)]
    yf = sb("yf", [P, GT])
    yh = [sb(f"yh{i}", [P, GT], F32R) for i in range(2)]
    yl = [sb(f"yl{i}", [P, GT], F32R) for i in range(2)]
    sq = sb("sq", [P, GT])
    vh, vl = sb("vh", [P, 2, 2 * DH], F32R), sb("vl", [P, 2, 2 * DH], F32R)
    mh = [sb(f"mh{i}", [P, S], F32R) for i in range(2)]
    ml = [sb(f"ml{i}", [P, S], F32R) for i in range(2)]
    oraw = wraw[:, 0:OCOLS]

    s_x = [sem(f"dma_x{g}") for g in range(NG)]
    s_c = sem("dma_consts")
    dma_w, dma_o, dma_d = sem("dma_w"), sem("dma_o"), sem("dma_d")
    w_hi, w_lo, o_hi, o_lo = sem("w_hi"), sem("w_lo"), sem("o_hi"), sem("o_lo")
    nw_ready, dma_rw, r_hi, r_lo, dma_xn = (sem(n) for n in ("nw_ready", "dma_rw", "r_hi", "r_lo", "dma_xn"))
    rwh = yh[0][:, 0:KC * E].rearrange("p (k e) -> p k e", k=KC)
    rwl = yl[0][:, 0:KC * E].rearrange("p (k e) -> p k e", k=KC)

    sh_hi, sh_lo, pe_fill, dma_so = sem("sh_hi"), sem("sh_lo"), sem("pe_fill"), sem("dma_so")
    dma_z, dma_side, dma_sh, v_side, v_shift, a_exp = (
        sem(n) for n in ("dma_z", "dma_side", "dma_sh", "v_side", "v_shift", "a_exp"))
    work = wraw[:, 0:4 * NT * E + 4 * E * E]
    spare = draw[:].rearrange("p h c -> p (h c)")
    consts, rrows, sbias = spare[:, 0:C_ALL], spare[:, C_ALL:C_ALL + 2 * E], spare[:, C_ALL + 32:C_ALL + 36]
    small = spare[:, C_ALL + 36:C_ALL + 36 + 2 * NT * GROUPS + NT]

    def section(j):
        return slice(j * SEC, (j + 1) * SEC)

    ofirst = gT[:].rearrange("p h t -> p (h t)")

    def load_pair(sp, p):
        sp.dma_start(wraw[:], w_pairs[p]).then_inc(dma_w, 16)
        sp.dma_start(ofirst, o_pairs[p]).then_inc(dma_o, 16)
        sp.dma_start(draw[:], decay[p]).then_inc(dma_d, 16)

    def load_first(sp):
        sp.dma_start(ident[:], ident_in).then_inc(s_c, 16)
        sp.dma_start(nw[:], norm_w).then_inc(s_c, 16)
        for g in range(NG):
            for t in range(TPG):
                sp.dma_start(acc[:, g * TPG + t, :], x_tiles[g * TPG + t]).then_inc(s_x[g], 16)
        sp.dma_start(yf[:, 0:KC * E], router_w).then_inc(dma_rw, 16)
        load_pair(sp, 0)

    def split_first_high(a):
        a.wait_ge(dma_w, 16)
        for j in range(FILLS):
            a.copy(wh[:, section(j)], wraw[:, section(j)]).then_inc(w_hi, 1)
        a.wait_ge(dma_o, 16)
        for j in range(2):
            a.copy(oh[:, j * D:(j + 1) * D], ofirst[:, j * D:(j + 1) * D]).then_inc(o_hi, 1)

    def split_first_low(pool):
        pool.wait_ge(s_c, 32)
        pool.tensor_scalar(nw[:], nw[:], 0.5, None, ALU.mult).then_inc(nw_ready, 1)
        pool.wait_ge(dma_rw, 16)
        pool.tensor_copy(yh[0][:, 0:KC * E], yf[:, 0:KC * E]).then_inc(r_hi, 1)
        pool.wait_ge(r_hi, 1)
        pool.tensor_tensor(yl[0][:, 0:KC * E], yf[:, 0:KC * E], yh[0][:, 0:KC * E].bitcast(F32),
                           ALU.subtract).then_inc(r_lo, 1)
        for j in range(FILLS):
            c = section(j)
            pool.wait_ge(w_hi, j + 1)
            pool.tensor_tensor(wl[:, c], wraw[:, c], wh[:, c].bitcast(F32), ALU.subtract).then_inc(w_lo, 1)
        for j in range(2):
            c = slice(j * D, (j + 1) * D)
            pool.wait_ge(o_hi, j + 1)
            pool.tensor_tensor(ol[:, c], ofirst[:, c], oh[:, c].bitcast(F32), ALU.subtract).then_inc(o_lo, 1)

    def x_ready(v, g):
        if g == 0:
            v.wait_ge(s_c, 32)
        v.wait_ge(s_x[g], 16 * TPG)

    normalise_and_route(nc, acc, x_ready, xh, xl, ident, load_first, xn_dram, dma_xn, split_first_high,
                        split_first_low, rwh, rwl, r_lo, [x[0:E, i, :] for x in (qT, kT) for i in range(2)], logits)

    with ExitStack() as inner:
        def ps(name):
            return inner.enter_context(nc.psum_tensor(name, [P, GT], F32))

        pj = [ps(f"proj{i}") for i in range(2)]
        sc = [ps(f"score{i}") for i in range(2)]
        ot = [ps(f"attnout{i}") for i in range(2)]
        op = [ps(f"outproj{i}") for i in range(2)]
        pe_proj, pe_s, pe_av, pe_out = sem("pe_proj"), sem("pe_s"), sem("pe_av"), sem("pe_out")
        a_ev, a_sq, a_yh = sem("a_ev"), sem("a_sq"), sem("a_yh")
        a_vh, a_mh, v_vl, v_ml = sem("a_vh"), sem("a_mh"), sem("v_vl"), sem("v_ml")
        v_dec, v_mask, v_y, v_yl, v_acc, p_zero, p_sq = (
            sem(n) for n in ("v_dec", "v_mask", "v_y", "v_yl", "v_acc", "p_zero", "p_sq"))
        body = ExitStack()
        block = body.enter_context(nc.Block())
        router = Routing(logits, rrows, consts, work, small, v_side, dma_side, v_shift, a_exp, (o_lo, NP_ * 2))

        def all_steps(eng, run):
            run(-1, NG - 1, False, True, False)
            with eng.Fori(0, NP_ - 1) as p:
                for g in range(NG):
                    run(p, g, True, True, True)
            for g in range(NG):
                run(NP_ - 1, g, True, g + 1 < NG, False)

        @block.sync
        def _(sp):
            sp.dma_start(tok_ids[:], token_ids).then_inc(dma_z, 16)
            for table in token_slots:
                cells = table.rearrange("(c n) o -> c (n o)", c=P // 8)
                sp.dma_start(cells, zeros.rearrange("(c n) -> c n", c=P // 8)).then_inc(dma_z, 16)
            with sp.Fori(1, NP_) as p:
                sp.wait_ge(o_lo, p * 2)
                sp.dma_start(wraw[:], w_pairs[p]).then_inc(dma_w, 16)
                sp.wait_ge(v_dec, p)
                sp.dma_start(draw[:], decay[p]).then_inc(dma_d, 16)
                sp.wait_ge(w_lo, p * FILLS + FILLS)
                sp.dma_start(oraw, o_pairs[p]).then_inc(dma_o, 16)
            sp.wait_ge(v_dec, NP_)
            sp.dma_start(consts[:], route_consts).then_inc(dma_side, 16)
            sp.dma_start(rrows[:], router_rows.partition_broadcast(P)).then_inc(dma_side, 16)
            sp.dma_start(sbias[:], shared_b).then_inc(dma_side, 16)
            sp.wait_ge(w_lo, NP_ * FILLS)
            sp.dma_start(wraw[:, WCOLS - 4 * SEC:], shared_w).then_inc(dma_sh, 16)

        @block.tensor
        def _(pe):
            def project_head(pn, gn, fill, j):
                if gn == 0:
                    pe.wait_ge(w_lo, pn * FILLS + j + 1)
                if not isinstance(fill, int) or fill > 1:
                    pe.wait_ge(a_ev, fill - 1)
                parts = []
                m = slice(gn * GT, (gn + 1) * GT)
                for k in range(KC):
                    c = slice(j * SEC + k * P, j * SEC + (k + 1) * P)
                    parts.append((wh[:, c], wl[:, c], xh[:, k, m], xl[:, k, m]))
                three_passes(pe, pj[j % 2][:], parts, True, True).then_inc(pe_proj, 1)

            def project_v(pn, gn, fill, j):
                if gn == 0:
                    pe.wait_ge(w_lo, pn * FILLS + FILLS)
                pe.wait_ge(a_ev, fill - 1)
                for i in range(2):
                    tok = gn * GT + ((j - NSEC) * 2 + i) * P
                    parts = []
                    for k in range(KC):
                        c = slice(NSEC * SEC + k * 2 * P, NSEC * SEC + (k + 1) * 2 * P)
                        parts.append((xh[:, k, tok:tok + P], xl[:, k, tok:tok + P], wh[:, c], wl[:, c]))
                    ins = three_passes(pe, pj[j % 2][:, i * 2 * P:(i + 1) * 2 * P], parts, True, True)
                ins.then_inc(pe_proj, 1)

            def scores(u, i):
                h, s0 = i // 2, (i % 2) * S
                if i == 0:
                    pe.wait_ge(a_ev, u * FILLS + FILLS)
                pe.matmul(sc[i % 2][:, 0:S], kT[:, h, s0:s0 + P], qT[:, h, s0:s0 + S], start=True, stop=True)
                pe.matmul(sc[i % 2][:, S:MC], kT[:, h, s0 + P:s0 + S], qT[:, h, s0 + P:s0 + S],
                          start=True, stop=True).then_inc(pe_s, 1)

            def values(u, i):
                h, b = i // 2, i % 2
                pe.wait_ge(v_ml, u * 4 + i + 1)
                if i == 0:
                    pe.wait_ge(v_vl, u * 2 + 2)
                c = slice(h * DH, (h + 1) * DH)
                three_passes(pe, ot[h][:, b * S:(b + 1) * S], [(vh[:, b, c], vl[:, b, c], mh[i % 2][:], ml[i % 2][:])],
                             True, False)
                pe.matmul(ot[h][:, b * S + P:(b + 1) * S], vt[:, 2 * b + 1, c], ms[i % 2][:, S:MC],
                          start=False, stop=True).then_inc(pe_av, 1)

            def project_out(p, g, u):
                if g == 0:
                    pe.wait_ge(o_lo, p * 2 + 2)
                pe.wait_ge(v_yl, u * 2 + 2)
                for t in range(TPG):
                    if t >= 2:
                        pe.wait_ge(v_acc, u * TPG + t - 1)
                    m = slice(t * P, (t + 1) * P)
                    parts = [(yh[h][:, m], yl[h][:, m], oh[:, h * D:(h + 1) * D], ol[:, h * D:(h + 1) * D])
                             for h in range(2)]
                    three_passes(pe, op[t % 2][:], parts, True, True).then_inc(pe_out, 1)

            def run(p, g, attend, project, more):
                u = p * NG + g
                pn, gn = (p, g + 1) if g + 1 < NG else (p + 1, 0)
                if attend and not project:
                    pe.wait_ge(a_ev, NP_ * NG * FILLS)

                    def shared(j, some):
                        pe.wait_ge(sh_lo, j + 1)
                        shared_fill(pe, 0, j, pj[j], wh, wl, xh, xl, pe_fill, some)

                    scores(u, 0)
                    scores(u, 1)
                    shared(0, range(KC))
                    values(u, 0)
                    values(u, 1)
                    scores(u, 2)
                    scores(u, 3)
                    shared(1, range(KC // 2))
                    values(u, 2)
                    values(u, 3)
                    shared(1, range(KC // 2, KC))
                    project_out(p, g, u)
                    return
                for what, i in (("s", 0), ("s", 1), ("p", 0), ("a", 0), ("a", 1), ("p", 1), ("s", 2), ("s", 3),
                                ("p", 2), ("a", 2), ("a", 3), ("p", 3), ("p", 4), ("p", 5), ("v", 6), ("v", 7)):
                    if what == "s" and attend:
                        scores(u, i)
                    if what == "a" and attend:
                        values(u, i)
                    if what == "p" and project:
                        project_head(pn, gn, (u + 1) * FILLS + i, i)
                    if what == "v" and project:
                        project_v(pn, gn, (u + 1) * FILLS + i, i)
                if attend:
                    project_out(p, g, u)

            all_steps(pe, run)

        @block.scalar
        def _(a):
            dst = [qT[:, 0, :], kT[:, 0, :], gT[:, 0, :], qT[:, 1, :], kT[:, 1, :], gT[:, 1, :],
                   vt[:, 0:2, :].rearrange("p t c -> p (t c)"), vt[:, 2:4, :].rearrange("p t c -> p (t c)")]

            def evacuate(u, j, attend):
                a.wait_ge(pe_proj, (u + 1) * FILLS + j + 1)
                gate = j in (2, 5)
                if gate and attend:
                    a.wait_ge(v_y, u * 2 + j // 3 + 1)
                a.activation(dst[j], pj[j % 2][:], ACT.Tanh if gate else ACT.Silu,
                             scale=0.5 if gate else 1.0).then_inc(a_ev, 1)

            def v_high(u, b):
                a.wait_ge(a_ev, (u + 1) * FILLS + NSEC + b + 1)
                a.copy(vh[:, b, :], vt[:, 2 * b, :]).then_inc(a_vh, 1)

            def mask_high(u, i):
                a.wait_ge(v_mask, u * 4 + i + 1)
                a.copy(mh[i % 2][:], ms[i % 2][:, 0:S]).then_inc(a_mh, 1)

            def square(u, h):
                a.wait_ge(v_y, u * 2 + h + 1)
                a.wait_ge(p_sq, u * 2 + h + 1)
                a.activation(sq[:], ot[h][:], ACT.Square).then_inc(a_sq, 1)

            def y_high(u, h):
                a.wait_ge(v_y, u * 2 + h + 1)
                a.activation(yh[h][:], yf[:], ACT.Identity, scale=nwcur[:, h:h + 1]).then_inc(a_yh, 1)

            def split_high(pn, j):
                a.wait_ge(dma_w, pn * 16 + 16)
                a.copy(wh[:, section(j)], wraw[:, section(j)]).then_inc(w_hi, 1)

            def run(p, g, attend, project, more):
                u = p * NG + g
                split = more and g == 2
                for j in range(FILLS):
                    if attend and j in (0, 2):
                        mask_high(u, j)
                        mask_high(u, j + 1)
                    if project:
                        evacuate(u, j, attend)
                        if j >= NSEC:
                            v_high(u, j - NSEC)
                        if split and j < NSEC:
                            split_high(p + 1, j)
                    if attend and j in (0, 2):
                        square(u, j // 2)
                        y_high(u, j // 2)
                    if attend and not more and g == 0 and j == 3:
                        router.exponentials(a)
                if split:
                    split_high(p + 1, 6)
                    split_high(p + 1, 7)
                if attend and not more and g == NG - 2:
                    a.wait_ge(dma_sh, 16)
                    for j in range(4):
                        a.copy(wh[:, section(j)], wraw[:, section(4 + j)]).then_inc(sh_hi, 1)
                if more and g == NG - 1:
                    a.wait_ge(dma_o, p * 16 + 32)
                    a.wait_ge(pe_out, u * TPG + TPG)
                    for h in range(2):
                        a.copy(oh[:, h * D:(h + 1) * D], oraw[:, h * D:(h + 1) * D]).then_inc(o_hi, 1)

            all_steps(a, run)

        @block.vector
        def _(v):
            def decays(p):
                v.wait_ge(dma_d, p * 16 + 16)
                v.tensor_copy(dcur[:], draw[:])
                v.tensor_copy(nwcur[:], nw[:, bass.ds(p * 2, 2)]).then_inc(v_dec, 1)

            def mask(p, u, i):
                v.wait_ge(pe_s, u * 4 + i + 1)
                if i == 0:
                    v.wait_ge(v_dec, p + 1)
                v.tensor_tensor(ms[i % 2][:], sc[i % 2][:, 0:MC], dcur[:, i // 2, :], ALU.mult).then_inc(v_mask, 1)

            def gated(u, h):
                v.wait_ge(pe_av, u * 4 + 2 * h + 2)
                if h:
                    v.wait_ge(v_yl, u * 2 + 1)
                v.scalar_tensor_tensor(yf[:], gT[:, h, :], 1.0, ot[h][:], ALU.add, ALU.mult).then_inc(v_y, 1)

            def mask_low(u, i):
                v.wait_ge(a_mh, u * 4 + i + 1)
                v.tensor_tensor(ml[i % 2][:], ms[i % 2][:, 0:S], mh[i % 2][:].bitcast(F32),
                                ALU.subtract).then_inc(v_ml, 1)

            def v_low(u):
                for b in range(2):
                    v.wait_ge(a_vh, (u + 1) * 2 + b + 1)
                    v.tensor_tensor(vl[:, b, :], vt[:, 2 * b, :], vh[:, b, :].bitcast(F32),
                                    ALU.subtract).then_inc(v_vl, 1)

            def y_low(u, h):
                v.wait_ge(a_yh, u * 2 + h + 1)
                v.scalar_tensor_tensor(yl[h][:], yf[:], nwcur[:, h:h + 1], yh[h][:].bitcast(F32),
                                       ALU.mult, ALU.subtract).then_inc(v_yl, 1)

            def run(p, g, attend, project, more):
                u = p * NG + g
                if not attend:
                    decays(0)
                    v_low(u)
                    return
                for h in range(2):
                    mask(p, u, 2 * h)
                    mask(p, u, 2 * h + 1)
                    mask_low(u, 2 * h)
                    mask_low(u, 2 * h + 1)
                    if not more and h == 0:
                        router.rank_experts(v, ((), (1,), (4,), (7,))[g])
                    gated(u, h)
                    y_low(u, h)
                if not more:
                    router.choose(v, g)
                if more and g == NG - 1:
                    v.wait_ge(v_yl, u * 2 + 2)
                    decays(p + 1)
                if project:
                    v_low(u)
                for t in range(TPG):
                    tile = acc[:, g * TPG + t, :]
                    v.wait_ge(pe_out, u * TPG + t + 1)
                    if t == 0 and g == 0:
                        v.wait_ge(p_zero, 2)
                    v.tensor_tensor(tile, op[t % 2][:], tile, ALU.add).then_inc(v_acc, 1)

            all_steps(v, run)

        @block.gpsimd
        def _(pool):
            pool.wait_ge(dma_xn, 16 * NT)
            pool.memset(acc[:], 0.0).then_inc(p_zero, 1)
            pool.memset(sqacc[:], 0.0).then_inc(p_zero, 1)
            pool.sem_inc(p_sq, 1)
            pool.wait_ge(p_zero, 2)

            def add_squares(g, u, h):
                pool.wait_ge(a_sq, u * 2 + h + 1)
                pool.wait_ge(p_sq, u * 2 + h + 1)
                c = slice(g * GT, (g + 1) * GT)
                pool.tensor_tensor(sqacc[:, c], sqacc[:, c], sq[:], ALU.add).then_inc(p_sq, 1)

            def split_low(pn, j):
                pool.wait_ge(w_hi, pn * FILLS + j + 1)
                c = section(j)
                pool.tensor_tensor(wl[:, c], wraw[:, c], wh[:, c].bitcast(F32), ALU.subtract).then_inc(w_lo, 1)

            def run(p, g, attend, project, more):
                u = p * NG + g
                if not attend:
                    return
                for j in range(FILLS):
                    if more and g == 2:
                        split_low(p + 1, j)
                    if j in (0, 2):
                        add_squares(g, u, j // 2)
                if not more and g == NG - 2:
                    for j in range(4):
                        pool.wait_ge(sh_hi, j + 1)
                        pool.tensor_tensor(wl[:, section(j)], wraw[:, section(4 + j)],
                                           wh[:, section(j)].bitcast(F32), ALU.subtract).then_inc(sh_lo, 1)
                if more and g == NG - 1:
                    for h in range(2):
                        pool.wait_ge(o_hi, p * 2 + 3 + h)
                        c = slice(h * D, (h + 1) * D)
                        pool.tensor_tensor(ol[:, c], oraw[:, c], oh[:, c].bitcast(F32),
                                           ALU.subtract).then_inc(o_lo, 1)

            all_steps(pool, run)

        body.close()
        shared_expert(nc, inner, x_tiles, token_slots, b3, router, shared_o, sbias, consts, wh, wl, oh, ol, xh, xl, ms, dcur,
                      qT, kT, gT, vt, yf, yh, yl, sq, acc, sqacc, ident, tok_ids, pj + sc, ot, op, dma_so, dma_z, sh_lo,
                      pe_fill, slot_of, gate_of, expert_of, token_at, table_in)


class Routing:

    def __init__(self, logits, rows, consts, work, small, v_side, dma_side, v_shift, a_exp, work_free):
        n = NT * E
        self.logits = logits[:].rearrange("p (t e) -> p t e", e=E)
        self.lg, self.sc, self.m0, self.m1 = (
            work[:, i * n:(i + 1) * n].rearrange("p (t e) -> p t e", e=E) for i in range(4))
        self.cmp = [work[:, 4 * n + i * 2 * E * E:4 * n + (i + 1) * 2 * E * E] for i in range(2)]
        self.b, self.bias = rows[:, 0:E], rows[:, E:2 * E]
        self.early = consts[:, C_EARLY:C_EARLY + E * E].rearrange("p (i j) -> p i j", i=E)
        self.consts = consts
        self.gm = small[:, 0:NT * GROUPS].rearrange("p (t g) -> p t g", g=GROUPS)
        self.keep = small[:, NT * GROUPS:2 * NT * GROUPS].rearrange("p (t g) -> p t g", g=GROUPS)
        self.red = small[:, 2 * NT * GROUPS:2 * NT * GROUPS + NT]
        self.v_side, self.dma_side, self.v_shift, self.a_exp = v_side, dma_side, v_shift, a_exp
        self.work_free, self.chain = work_free, None

    def exponentials(self, a):
        a.wait_ge(self.v_shift, 1)
        a.activation(self.lg, self.lg, ACT.Exp).then_inc(self.a_exp, 1)

    def rank(self, v, val, out, n, lower):
        c, nt = self.chain, val.shape[1]
        full = [P, nt, n, n]
        vj, vi = val.unsqueeze(2).to_broadcast(full), val.unsqueeze(3).to_broadcast(full)
        gt, ge = (x[:, 0:nt * n * n].rearrange("p (t i j) -> p t i j", i=n, j=n) for x in self.cmp)
        c.link(v.tensor_tensor(gt, vj, vi, ALU.is_gt))
        c.link(v.tensor_tensor(ge, vj, vi, ALU.is_equal))
        c.link(v.tensor_tensor(ge, ge, lower.unsqueeze(1).to_broadcast(full), ALU.mult))
        c.link(v.tensor_tensor(gt, gt, ge, ALU.add))
        c.link(v.tensor_reduce(out, gt, AX_X, ALU.add))

    def rank_experts(self, v, pairs):
        for n in pairs:
            t = slice(2 * n, 2 * n + 2)
            self.rank(v, self.lg[:, t, :], self.m0[:, t, :], E, self.early)

    def choose(self, v, g):
        over_e = [P, NT, E]
        if g == 0:
            self.chain = c = Chain(v, self.v_side)
            v.wait_ge(self.dma_side, 48)
            v.wait_ge(*self.work_free)
            c.link(v.tensor_tensor(self.lg, self.logits, self.b.unsqueeze(1).to_broadcast(over_e), ALU.add))
            c.link(v.tensor_reduce(self.red, self.lg, AX_X, ALU.max))
            v.tensor_tensor(self.lg, self.lg, self.red.unsqueeze(2).to_broadcast(over_e),
                            ALU.subtract).then_inc(self.v_shift, 1)
            v.wait_ge(self.a_exp, 1)
            c.link(v.tensor_reduce(self.red, self.lg, AX_X, ALU.add))
            c.link(v.reciprocal(self.red, self.red))
            c.link(v.tensor_tensor(self.sc, self.lg, self.red.unsqueeze(2).to_broadcast(over_e), ALU.mult))
            c.link(v.tensor_tensor(self.sc, self.sc, self.bias.unsqueeze(1).to_broadcast(over_e), ALU.add))
            by_group = [x.rearrange("p t (g e) -> p t g e", g=GROUPS) for x in (self.sc, self.lg)]
            c.link(v.tensor_reduce(self.gm, by_group[0], AX_X, ALU.max))
            self.rank(v, self.gm, self.keep, GROUPS, self.early[:, 0:GROUPS, 0:GROUPS])
            c.link(v.tensor_scalar(self.keep, self.keep, 2.0, None, ALU.is_lt))
            spread = self.keep.unsqueeze(3).to_broadcast([P, NT, GROUPS, E // GROUPS])
            c.link(v.tensor_tensor(by_group[1], by_group[0], spread, ALU.mult))
            c.link(v.tensor_scalar(self.keep, self.keep, 1.0, -NEG, ALU.subtract, ALU.mult))
            c.link(v.tensor_tensor(by_group[1], by_group[1], spread, ALU.add))
        self.rank_experts(v, ((0,), (2, 3), (5, 6), ())[g])
        if g == NG - 1:
            c = self.chain
            c.link(v.tensor_scalar(self.m1, self.m0, 1.0, None, ALU.is_equal))
            c.link(v.tensor_scalar(self.m0, self.m0, 0.0, None, ALU.is_equal))
            c.link(v.tensor_tensor(self.lg, self.m0, self.m1, ALU.add))

    def place_slots(self, v, prefix, totals, slot_of, ready, between):
        c = self.chain
        n = NT * E
        ab = [x[:, 0:n] for x in self.cmp]

        def running(cur, other, step, length):
            while step < length:
                v.tensor_copy(other[:, 0:step], cur[:, 0:step])
                c.link(v.tensor_tensor(other[:, step:length], cur[:, step:length], cur[:, 0:length - step], ALU.add))
                cur, other, step = other, cur, 2 * step
            return cur, other

        c.link(v.tensor_copy(ab[0], totals))
        incl, free = running(ab[0], ab[1], E, n)
        between()
        above = self.cmp[0][:, n:n + E * NTHR].rearrange("p (e k) -> p e k", k=NTHR)
        tiles, ends, tmp = (self.cmp[1][:, n + i * E:n + (i + 1) * E] for i in range(3))
        thr = self.consts[:, C_THR:C_THR + NTHR].unsqueeze(1).to_broadcast([P, E, NTHR])
        c.link(v.tensor_tensor(above, incl[:, n - E:n].unsqueeze(2).to_broadcast([P, E, NTHR]), thr, ALU.is_gt))
        c.link(v.tensor_reduce(tiles, above, AX_X, ALU.add))
        c.link(v.tensor_copy(ends, tiles))
        self.ends, tmp = running(ends, tmp, 1, E)
        c.link(v.tensor_tensor(tmp, self.ends, tiles, ALU.subtract))
        c.link(v.tensor_scalar(tmp, tmp, float(SLOT_T), None, ALU.mult))
        slot = free.rearrange("p (t e) -> p t e", e=E)
        c.link(v.tensor_tensor(free, incl, totals, ALU.subtract))
        c.link(v.tensor_tensor(free, free, prefix, ALU.add))
        c.link(v.tensor_tensor(slot, slot, tmp.unsqueeze(1).to_broadcast([P, NT, E]), ALU.add))
        self.prod = incl.rearrange("p (t e) -> p t e", e=E)
        s, col = self.red, tmp
        for i, m in enumerate((self.m0, self.m1)):
            c.link(v.tensor_tensor(self.prod, m, slot, ALU.mult))
            c.link(v.tensor_reduce(s, self.prod, AX_X, ALU.add))
            c.link(v.tensor_scalar(col, s, 1.0 / P, (P - 1) / (2.0 * P), ALU.mult, ALU.subtract))
            c.link(v.tensor_scalar(col, col, 1.5 * 2.0 ** 23, None, ALU.add))
            c.link(v.tensor_scalar(col, col, 1.5 * 2.0 ** 23, 1.0 - SLOTS, ALU.subtract, ALU.mult))
            c.link(v.scalar_tensor_tensor(s, s, float(SLOTS // P), col, ALU.mult, ALU.add))
            v.tensor_copy(slot_of[:, i, :], s).then_inc(ready, 1)
            v.wait_ge(ready, i + 1)

    def gates_and_experts(self, v, gate_of, expert_of, gates, ready):
        c = self.chain
        for i, m in enumerate((self.m0, self.m1)):
            c.link(v.tensor_tensor(self.prod, m, self.sc, ALU.mult))
            c.link(v.tensor_reduce(gate_of[:, i, :], self.prod, AX_X, ALU.add))
        c.link(v.tensor_copy(self.red, self.ends))
        full = [P, NTILES, E]
        late = self.cmp[0][:, 0:NTILES * E].rearrange("p (i e) -> p i e", e=E)
        number = self.consts[:, C_TILE:C_TILE + NTILES].unsqueeze(2).to_broadcast(full)
        c.link(v.tensor_tensor(late, self.red.unsqueeze(1).to_broadcast(full), number, ALU.is_le))
        te = self.cmp[1][:, 0:NTILES]
        c.link(v.tensor_reduce(te, late, AX_X, ALU.add))
        c.link(v.tensor_scalar(te, te, float(E - 1), None, ALU.min))
        v.tensor_copy(expert_of[:], te)
        v.memset(gates[:, :, E:E + 1], 1.0)
        v.tensor_tensor(gates[:, :, 0:E], self.lg, self.sc, ALU.mult).then_inc(ready, 1)


def shared_fill(pe, g, j, bank, wh, wl, xh, xl, done, some=range(KC)):
    terms = []
    m = slice(g * GT, (g + 1) * GT)
    first, last = some[0] == 0, some[-1] == KC - 1
    for k in some:
        c = slice(j * SEC + k * P, j * SEC + (k + 1) * P)
        terms.append((wh[:, c], wl[:, c], xh[:, k, m], xl[:, k, m]))
    ins = three_passes(pe, bank[:], terms, first, last)
    if last:
        ins.then_inc(done, 1)


def shared_expert(nc, outer, x_tiles, token_slots, b3, router, shared_o, sbias, consts, wh, wl, oh, ol, xh, xl, ms,
                  dcur, qT, kT, gT, vt, yf, yh, yl, sq, acc, sqacc, ident, tok_ids, fills, misc, op, dma_so, dma_z, sh_lo,
                  pe_fill, slot_of, gate_of, expert_of, token_at, table_in):
    def sem(name):
        return outer.enter_context(nc.semaphore(name))

    names = ("so_hi", "so_lo", "pe_pre", "pe_sums", "pe_gt", "pe_out2", "a_root2", "a_s",
             "a_gt", "a_yh2", "v_var2", "v_slots", "v_yf2", "v_yl2", "v_res", "v_acc2", "v_gates", "dma_b3", "dma_parts",
             "p_sum")
    q = {n: sem(n) for n in names}
    ids_out = [sem(f"ids_out{k}") for k in range(TABLES)]
    parts = [dcur[:, k // 2, (k % 2) * P:(k % 2) * P + SLOTS // P].bitcast(I32) for k in range(TABLES)]
    XB = 3
    x_in = [sem(f"x_in{i}") for i in range(XB)]
    xbuf = [qT[:, 0, :], qT[:, 1, :], kT[:, 0, :]]
    yf = [yf[:], kT[:, 1, :]]
    oraw = vt[:].rearrange("p t c -> p (t c)")
    msq = outer.enter_context(nc.sbuf_tensor("meansq", [P, 3, NT], F32))
    mean, root, rs = msq[:, 0, :], msq[:, 1, :], msq[:, 2, :]
    gate_t = sqacc[0:E + 1, :]
    b3s = sq[0:E + 1, :]
    gates = ms[0][:, 0:NT * (E + 1)].rearrange("p (t e) -> p t e", e=E + 1)
    spare = slice(4 * SEC, 4 * SEC + 2 * GT)
    yh, yl = ([y, [w[:, spare][:, h * GT:(h + 1) * GT] for h in range(2)]]
              for y, w in (([x[:] for x in yh], wh), ([x[:] for x in yl], wl)))
    block = outer.enter_context(nc.Block())

    @block.sync
    def _(sp):
        sp.dma_start(oraw, shared_o).then_inc(dma_so, 16)
        sp.dma_start(b3s, b3).then_inc(q["dma_b3"], 16)
        for t in range(NT):
            if t >= XB:
                sp.wait_ge(q["v_res"], t - XB + 1)
            sp.dma_start(xbuf[t % XB], x_tiles[t]).then_inc(x_in[t % XB], 16)

    @block.gpsimd
    def _(pool):
        pool.wait_ge(dma_z, 16 * (1 + TABLES))
        pool.wait_ge(q["v_slots"], 2)
        for n in range(NT * CHOSEN):
            t, i, k = n // CHOSEN, n % CHOSEN, n % TABLES
            if n >= TABLES:
                pool.wait_ge(ids_out[k], 16 * (n // TABLES))
            pool.indirect_dma_start(token_slots[k], bass.IndirectOffsetOnAxis(ap=slot_of[:, i, t:t + 1], axis=0),
                                    tok_ids[:, t:t + 1], None).then_inc(ids_out[k], 16)
        for k in range(TABLES):
            pool.wait_ge(ids_out[k], 16 * NT * CHOSEN // TABLES)
            pool.dma_start(parts[k], token_slots[k].rearrange("(p c) o -> p (c o)", p=P)).then_inc(q["dma_parts"], 16)
        pool.wait_ge(q["dma_parts"], 16 * TABLES)
        pool.tensor_tensor(parts[0], parts[0], parts[1], ALU.add).then_inc(q["p_sum"], 1)
        pool.tensor_tensor(parts[2], parts[2], parts[3], ALU.add).then_inc(q["p_sum"], 1)
        pool.wait_ge(q["p_sum"], 2)
        pool.tensor_tensor(token_at[:], parts[0], parts[2], ALU.add).then_inc(table_in, 1)

    @block.tensor
    def _(pe):
        def inner_fill(g, j):
            if g == 0:
                pe.wait_ge(sh_lo, j + 1)
            elif j % 2 == 0:
                pe.wait_ge(q["v_yf2"], 2 * (g - 1) + j // 2 + 1)
            shared_fill(pe, g, j, fills[j], wh, wl, xh, xl, pe_fill)

        masks = router.lg.rearrange("p t e -> p (t e)")
        pe.matmul(misc[0][:, 0:NT * E], consts[:, C_TRI:C_TRI + P], masks, start=True, stop=True)
        pe.matmul(misc[1][:, 0:NT * E], consts[:, C_ONES:C_ONES + P], masks, start=True,
                  stop=True).then_inc(q["pe_pre"], 1)
        for t in range(NT):
            ins = pe.matmul(op[0][:, t:t + 1], sqacc[:, t * P:(t + 1) * P], consts[:, C_ONES:C_ONES + 1],
                            start=True, stop=True)
        ins.then_inc(q["pe_sums"], 1)
        for n in range(2, 8):
            inner_fill(n // 4, n % 4)
        pe.wait_ge(q["v_gates"], 1)
        for g in range(NG):
            if g >= 2:
                pe.wait_ge(q["a_gt"], g - 1)
            for t in range(TPG):
                ins = pe.transpose(misc[g % 2][0:E + 1, t * P:(t + 1) * P], gates[:, g * TPG + t, :], ident[:])
            ins.then_inc(q["pe_gt"], 1)
        pe.wait_ge(q["so_lo"], 2)
        pe.wait_ge(q["dma_b3"], 16)
        for g in range(NG):
            if 0 < g < NG - 1:
                for j in range(4):
                    inner_fill(g + 1, j)
            pe.wait_ge(q["v_yl2"], 2 * g + 2)
            if g == 0:
                pe.wait_ge(q["v_var2"], 1)
            pe.wait_ge(q["a_gt"], g + 1)
            for t in range(TPG):
                n = g * TPG + t
                if n >= 2:
                    pe.wait_ge(q["v_acc2"], n - 1)
                m = slice(t * P, (t + 1) * P)
                pe.matmul(op[n % 2][:], gate_t[:, n * P:(n + 1) * P], b3s, start=True, stop=False)
                parts = [(yh[g % 2][h][:, m], yl[g % 2][h][:, m], oh[:, h * D:(h + 1) * D], ol[:, h * D:(h + 1) * D])
                         for h in range(2)]
                three_passes(pe, op[n % 2][:], parts, False, True).then_inc(q["pe_out2"], 1)

    @block.scalar
    def _(a):
        def half(g, h):
            a.wait_ge(pe_fill, 4 * g + 2 * h + 1)
            if g:
                a.wait_ge(q["v_yf2"], 2 * (g - 1) + h + 1)
            a.activation(gT[:, h, :], fills[2 * h][:], ACT.Silu, bias=sbias[:, h:h + 1]).then_inc(q["a_s"], 1)

        def high(g, h):
            a.wait_ge(q["v_yf2"], 2 * g + h + 1)
            if g >= 2:
                a.wait_ge(q["pe_out2"], TPG * (g - 1))
            a.copy(yh[g % 2][h], yf[h]).then_inc(q["a_yh2"], 1)

        a.wait_ge(q["v_var2"], 1)
        a.activation(root, mean, ACT.Sqrt).then_inc(q["a_root2"], 1)
        for g in range(NG):
            for h in range(2):
                half(g, h)
            if g == 0:
                a.wait_ge(dma_so, 16)
                for h in range(2):
                    c = slice(h * D, (h + 1) * D)
                    a.copy(oh[:, c], oraw[:, c]).then_inc(q["so_hi"], 1)
            if g == 1:
                a.wait_ge(q["pe_sums"], 1)
                for i in range(NG):
                    a.wait_ge(q["pe_gt"], i + 1)
                    a.copy(gate_t[:, i * GT:(i + 1) * GT], misc[i % 2][0:E + 1, :]).then_inc(q["a_gt"], 1)
            for h in range(2):
                high(g, h)

    @block.vector
    def _(v):
        v.wait_ge(q["pe_sums"], 1)
        v.tensor_scalar(mean, op[0][:, 0:NT], 1.0 / (H * DH), EPS, ALU.mult, ALU.add).then_inc(q["v_var2"], 1)

        def product(g, h):
            v.wait_ge(q["a_s"], 2 * g + h + 1)
            v.wait_ge(pe_fill, 4 * g + 2 * h + 2)
            if g:
                v.wait_ge(q["v_yl2"], 2 * (g - 1) + h + 1)
            v.scalar_tensor_tensor(yf[h], fills[2 * h + 1][:], sbias[:, 2 + h:3 + h], gT[:, h, :], ALU.add,
                                   ALU.mult).then_inc(q["v_yf2"], 1)

        def low(g, h):
            v.wait_ge(q["a_yh2"], 2 * g + h + 1)
            v.tensor_tensor(yl[g % 2][h], yf[h], yh[g % 2][h].bitcast(F32), ALU.subtract).then_inc(q["v_yl2"], 1)

        product(0, 0)
        v.wait_ge(q["pe_pre"], 1)
        router.place_slots(v, misc[0][:, 0:NT * E], misc[1][:, 0:NT * E], slot_of, q["v_slots"], lambda: product(0, 1))
        router.gates_and_experts(v, gate_of, expert_of, gates, q["v_gates"])
        for h in range(2):
            v.wait_ge(q["so_hi"], h + 1)
            cc = slice(h * D, (h + 1) * D)
            v.tensor_tensor(ol[:, cc], oraw[:, cc], oh[:, cc].bitcast(F32), ALU.subtract).then_inc(q["so_lo"], 1)
        for h in range(2):
            low(0, h)
        rsqrt(v, q["a_root2"], 1, router.chain, mean, root, rs)
        for g in range(NG):
            tiles = range(g * TPG, (g + 1) * TPG)
            for t in tiles:
                v.wait_ge(x_in[t % XB], 16 * (t // XB + 1))
                v.scalar_tensor_tensor(acc[:, t, :], acc[:, t, :], rs[:, t:t + 1], xbuf[t % XB], ALU.mult,
                                       ALU.add).then_inc(q["v_res"], 1)
            if g + 1 < NG:
                for h in range(2):
                    product(g + 1, h)
                for h in range(2):
                    low(g + 1, h)
            for t in tiles:
                v.wait_ge(q["v_res"], t + 1)
                v.wait_ge(q["pe_out2"], t + 1)
                v.tensor_tensor(acc[:, t, :], op[t % 2][:], acc[:, t, :], ALU.add).then_inc(q["v_acc2"], 1)


def routed_experts(nc, ctx, ex, l1_w, xn_dram, y_slots, ident, expert_of, token_at, table_in, w1h, w1l):
    def sb(name, shape, dt=F32):
        return ctx.enter_context(nc.sbuf_tensor(name, shape, dt))

    def pair(name, shape, dt=F32):
        return [sb(f"{name}{i}", shape, dt) for i in range(2)]

    def sem(name):
        return ctx.enter_context(nc.semaphore("e_" + name))

    W12 = 2 * SEC + 2
    raw12, raw3 = pair("eraw12", [P, W12]), pair("eraw3", [P, SEC])
    xin, cur = pair("exin", [P, 2, D]), pair("ecur", [P, 2], I32)
    eh, el, bias = pair("eh", [P, 3 * SEC], F32R), pair("el", [P, 3 * SEC], F32R), pair("ebias", [P, 2])
    xth, xtl = pair("exth", [P, KC, SLOT_T], F32R), pair("extl", [P, KC, SLOT_T], F32R)
    s1, hf = pair("es", [P, SLOT_T]), pair("ehf", [P, SLOT_T])
    hh, hl = pair("ehh", [P, SLOT_T], F32R), pair("ehl", [P, SLOT_T], F32R)
    yb = pair("ey", [P, 2, D])
    l1raw = pair("l1_raw", [P, PIECE])
    xt = [[ctx.enter_context(nc.psum_tensor(f"ext{i}{j}", [P, 2, SLOT_T], F32)) for j in range(2)] for i in range(2)]
    hp = [ctx.enter_context(nc.psum_tensor(f"ehp{i}", [P, 2, SLOT_T], F32)) for i in range(2)]
    op = [ctx.enter_context(nc.psum_tensor(f"eop{i}", [P, D], F32)) for i in range(2)]
    dma_w, dma_w3, dma_x, dma_y, dma_l1 = ([sem(f"{n}{i}") for i in range(2)]
                                           for n in ("dma_w", "dma_w3", "dma_x", "dma_y", "dma_l1"))
    a_l1, p_l1 = sem("a_l1"), sem("p_l1")
    pe_xt, pe_h, pe_o, a_hi, a_hi3, a_xh, a_s, a_hh, a_y, v_lo, v_xl, v_hf, v_hl, v_y, p_lo3, p_cur = (
        sem(n) for n in ("pe_xt", "pe_h", "pe_o", "a_hi", "a_hi3", "a_xh", "a_s", "a_hh", "a_y", "v_lo", "v_xl",
                         "v_hf", "v_hl", "v_y", "p_lo3", "p_cur"))
    y_tiles = y_slots.rearrange("(p i s) d -> i p s d", p=P, s=2)
    block = ctx.enter_context(nc.Block())

    def w(j):
        return slice(j * SEC, (j + 1) * SEC)

    def all_steps(eng, run):
        for r in (-1, 0):
            for b in range(2):
                run(r, b)
        with eng.Fori(1, NTILES // 2 - 2) as r:
            for b in range(2):
                run(r, b)
        for r in range(NTILES // 2 - 2, (NTILES + 1) // 2):
            for b in range(2):
                run(r, b)

    def tile(r, b, ahead, n=NTILES):
        r, b = r + (b + ahead) // 2, (b + ahead) % 2
        i = r * 2 + b
        return not isinstance(i, int) or 0 <= i < n, i, r, b

    def wait(eng, sem_, n):
        if not isinstance(n, int) or n > 0:
            eng.wait_ge(sem_, n)

    @block.sync
    def _(sp):
        def expert(i):
            return sp.value_load(expert_of[0:1, bass.ds(i, 1)], min_val=0, max_val=E - 1)

        def load12(i, b):
            e = expert(i)
            wait(sp, v_lo, i * 2 - 2)
            sp.dma_start(raw12[b][:], ex[e, :, 0:W12]).then_inc(dma_w[b], 16)

        def load3(i, b):
            e = expert(i)
            wait(sp, p_lo3, i - 1)
            sp.dma_start(raw3[b][:], ex[e, :, W12:W12 + SEC]).then_inc(dma_w3[b], 16)

        def load_piece(i, b):
            wait(sp, p_l1, i - 1)
            sp.dma_start(l1raw[b][:], l1_w[:, bass.ds(i * PIECE, PIECE)]).then_inc(dma_l1[b], 16)

        load12(0, 0)
        load3(0, 0)
        load12(1, 1)

        def run(r, b):
            is_tile, i, _, n = tile(r, b, 4)
            if is_tile:
                load12(i, n)
            is_tile, i, _, n = tile(r, b, 3)
            if is_tile:
                load3(i, n)
            is_piece, i, _, n = tile(r, b, 2, PIECES)
            if is_piece:
                load_piece(i, n)
            is_tile, i, _, n = tile(r, b, 0)
            if is_tile:
                sp.wait_ge(a_y, i + 1)
                sp.wait_ge(v_y, i + 1)
                sp.dma_start(y_tiles[i], yb[n][:]).then_inc(dma_y[n], 16)

        all_steps(sp, run)
        for b in range(2):
            sp.wait_ge(dma_y[b], 16 * ((NTILES + 1 - b) // 2))

    @block.tensor
    def _(pe):
        def rows_transposed(r, b):
            is_tile, i, half, n = tile(r, b, 2)
            if not is_tile:
                return
            pe.wait_ge(dma_x[n], half * 32 + 32)
            for h in range(2):
                wait(pe, v_xl, i * 2 - 3 + h)
                for k in range(2):
                    c = slice((2 * h + k) * P, (2 * h + k + 1) * P)
                    for s in range(2):
                        ins = pe.transpose(xt[n][h][:, k, s * P:(s + 1) * P], xin[n][:, s, c], ident[:])
                ins.then_inc(pe_xt, 1)

        def inner(r, b):
            is_tile, i, _, n = tile(r, b, 1)
            if not is_tile:
                return
            pe.wait_ge(v_xl, i * 2 + 2)
            wait(pe, v_hf, i - 1)
            for j in range(2):
                pe.wait_ge(v_lo, i * 2 + j + 1)
                parts = []
                for k in range(KC):
                    c = slice(j * SEC + k * P, j * SEC + (k + 1) * P)
                    parts.append((eh[n][:, c], el[n][:, c], xth[n][:, k, :], xtl[n][:, k, :]))
                ins = three_passes(pe, hp[n][:, j, :], parts, True, True)
            ins.then_inc(pe_h, 1)

        def outputs(r, b):
            is_tile, i, _, n = tile(r, b, 0)
            if not is_tile:
                return
            pe.wait_ge(p_lo3, i + 1)
            pe.wait_ge(v_hl, i + 1)
            for s in range(2):
                wait(pe, (a_y, v_y)[s], i)
                m = slice(s * P, (s + 1) * P)
                three_passes(pe, op[s][:], [(hh[n][:, m], hl[n][:, m], eh[n][:, w(2)], el[n][:, w(2)])], True,
                             True).then_inc(pe_o, 1)

        def run(r, b):
            rows_transposed(r, b)
            inner(r, b)
            outputs(r, b)

        all_steps(pe, run)

    @block.scalar
    def _(a):
        def run(r, b):
            is_tile, i, half, n = tile(r, b, 2)
            if is_tile:
                wait(a, pe_h, i - 1)
                for h in range(2):
                    a.wait_ge(pe_xt, i * 2 + h + 1)
                    a.copy(xth[n][:, 2 * h:2 * h + 2, :], xt[n][h][:]).then_inc(a_xh, 1)
            is_3, i3, half3, n3 = tile(r, b, 1)
            if is_3:
                wait(a, pe_o, i3 * 2 - 2)
                a.wait_ge(dma_w3[n3], half3 * 16 + 16)
                a.copy(eh[n3][:, w(2)], raw3[n3][:]).then_inc(a_hi3, 1)
            if is_tile:
                a.wait_ge(dma_w[n], half * 16 + 16)
                for j in range(2):
                    a.copy(eh[n][:, w(j)], raw12[n][:, w(j)]).then_inc(a_hi, 1)
            is_piece, k, half_k, nk = tile(r, b, 0, PIECES)
            if is_piece:
                a.wait_ge(dma_l1[nk], half_k * 16 + 16)
                a.copy(w1h[:, bass.ds(k * PIECE, PIECE)], l1raw[nk][:]).then_inc(a_l1, 1)
            if is_3:
                a.wait_ge(pe_h, i3 + 1)
                wait(a, v_hf, i3 - 1)
                a.activation(s1[n3][:], hp[n3][:, 0, :], ACT.Silu, bias=bias[n3][:, 0:1]).then_inc(a_s, 1)
                a.wait_ge(v_hf, i3 + 1)
                a.copy(hh[n3][:], hf[n3][:]).then_inc(a_hh, 1)
            is_tile, i, half, n = tile(r, b, 0)
            if is_tile:
                a.wait_ge(pe_o, i * 2 + 1)
                wait(a, dma_y[n], half * 16)
                a.copy(yb[n][:, 0, :], op[0][:]).then_inc(a_y, 1)

        all_steps(a, run)

    @block.vector
    def _(v):
        def run(r, b):
            is_tile, i, half, n = tile(r, b, 2)
            if is_tile:
                for h in range(2):
                    v.wait_ge(a_xh, i * 2 + h + 1)
                    v.tensor_tensor(xtl[n][:, 2 * h:2 * h + 2, :], xt[n][h][:], xth[n][:, 2 * h:2 * h + 2, :].bitcast(F32),
                                    ALU.subtract).then_inc(v_xl, 1)
                for j in range(2):
                    v.wait_ge(a_hi, i * 2 + j + 1)
                    if j == 0:
                        wait(v, v_hf, i - 1)
                        v.tensor_copy(bias[n][:], raw12[n][:, 2 * SEC:W12])
                    v.tensor_tensor(el[n][:, w(j)], raw12[n][:, w(j)], eh[n][:, w(j)].bitcast(F32),
                                    ALU.subtract).then_inc(v_lo, 1)
            is_tile, i, half, n = tile(r, b, 1)
            if is_tile:
                v.wait_ge(a_s, i + 1)
                wait(v, v_hl, i - 1)
                v.scalar_tensor_tensor(hf[n][:], hp[n][:, 1, :], bias[n][:, 1:2], s1[n][:], ALU.add,
                                       ALU.mult).then_inc(v_hf, 1)
                v.wait_ge(a_hh, i + 1)
                v.tensor_tensor(hl[n][:], hf[n][:], hh[n][:].bitcast(F32), ALU.subtract).then_inc(v_hl, 1)
            is_tile, i, half, n = tile(r, b, 0)
            if is_tile:
                v.wait_ge(pe_o, i * 2 + 2)
                wait(v, dma_y[n], half * 16)
                v.tensor_copy(yb[n][:, 1, :], op[1][:]).then_inc(v_y, 1)

        all_steps(v, run)

    @block.gpsimd
    def _(pool):
        def indices(i, n):
            pool.wait_ge(table_in, 1)
            pool.tensor_copy(cur[n][:], token_at[:, bass.ds(i * 2, 2)]).then_inc(p_cur, 1)
            pool.wait_ge(p_cur, i + 1)

        def gather(n):
            for s in range(2):
                pool.indirect_dma_start(xin[n][:, s, :], None, xn_dram,
                                        bass.IndirectOffsetOnAxis(ap=cur[n][:, s:s + 1], axis=0)).then_inc(dma_x[n], 16)

        for b in range(2):
            indices(b, b)
            gather(b)

        def run(r, b):
            is_tile, i, half, n = tile(r, b, 4)
            if is_tile:
                wait(pool, dma_x[n], half * 32)
                indices(i, n)
                pool.wait_ge(pe_xt, i * 2 - 2)
            is_3, i3, _, n3 = tile(r, b, 1)
            if is_3:
                pool.wait_ge(a_hi3, i3 + 1)
                pool.tensor_tensor(el[n3][:, w(2)], raw3[n3][:], eh[n3][:, w(2)].bitcast(F32),
                                   ALU.subtract).then_inc(p_lo3, 1)
            if is_tile:
                gather(n)
            is_piece, k, _, nk = tile(r, b, 0, PIECES)
            if is_piece:
                c = bass.ds(k * PIECE, PIECE)
                pool.wait_ge(a_l1, k + 1)
                pool.tensor_tensor(w1l[:, c], l1raw[nk][:], w1h[:, c].bitcast(F32), ALU.subtract).then_inc(p_l1, 1)

        all_steps(pool, run)


def layer_one(nc, ctx, w1h, w1l, b_qkv, b_o, sel_in, ident, acc, slot_of, gate_of, y_slots, out_tiles):
    def sb(name, shape, dt=F32):
        return ctx.enter_context(nc.sbuf_tensor(name, shape, dt))

    def sem(name):
        return ctx.enter_context(nc.semaphore(name))

    wq, wr, wo, wa, wb = ((w1h[:, a:b], w1l[:, a:b])
                          for a, b in ((0, L_R), (L_R, L_O), (L_O, L_A), (L_A, L_B), (L_B, L_USED)))
    sel = sb("l1_sel", [K1, NR * P], F32R)
    bq = sb("l1_bq", [P, 3])
    bo = sb("l1_bo", [P, D])
    xh = [sb(f"x1h{i}", [P, KC, GT], F32R) for i in range(2)]
    xl = [sb(f"x1l{i}", [P, KC, GT], F32R) for i in range(2)]
    dma_c = sem("l1_dma_c")
    s_sel = sem("l1_sel_ready")
    with ExitStack() as inner:
        def isb(name, shape, dt=F32):
            return inner.enter_context(nc.sbuf_tensor(name, shape, dt))

        stage = isb("l1_stage", [P, TPG, D])
        stat = isb("l1_stat", [P, TPG, 6])
        mv = isb("l1_mv", [P, TPG, 2])
        var = isb("l1_var", [P, TPG])
        root = isb("l1_root", [P, TPG])
        rstd = isb("l1_rstd", [P, TPG])
        qkv = isb("l1_qkv", [P, 3, GT])
        vt = isb("l1_v", [P, TPG, DH])
        pr = isb("l1_p", [P, TPG, S])
        pt = [isb(f"l1_pt{i}", [P, 2 * S]) for i in range(2)]
        mx = isb("l1_mx", [P, TPG])
        sm = isb("l1_sum", [P, TPG])
        oh = isb("l1_oh", [P, GT], F32R)
        ol = isb("l1_ol", [P, GT], F32R)
        sr = isb("l1_sr", [P, TPG, K1])
        left = [isb(f"l1_left{i}", [P, TPG, K1]) for i in range(2)]
        top8 = isb("l1_top8", [P, 2, TPG, 8])
        nm = isb("l1_nm", [P, TPG])
        rz = isb("l1_rz", [P, TPG])
        gg = isb("l1_g", [P, TPG, K1])
        gh = isb("l1_gh", [K1, GT], F32R)
        gl = isb("l1_gl", [K1, GT], F32R)
        st = isb("l1_scores_t", [K1, GT])[:]
        gs = isb("l1_gs", [P, GT])
        hf = isb("l1_hf", [P, GT])
        hh = [isb(f"l1_hh{i}", [P, GT], F32R) for i in range(2)]
        hl = [isb(f"l1_hl{i}", [P, GT], F32R) for i in range(2)]
        ob = [inner.enter_context(nc.psum_tensor(f"l1_ob{i}", [P, D], F32)) for i in range(TPG)]
        hb = [inner.enter_context(nc.psum_tensor(f"l1_hb{i}", [P, GT], F32)) for i in range(2)]
        mb = [inner.enter_context(nc.psum_tensor(f"l1_mb{i}", [P, GT], F32)) for i in range(2)]
        SCALE = float(np.float32(1.0) / np.sqrt(np.float32(DH)))
        names = ("pe_h", "pe_m", "pe_out", "a_qkv", "a_vt", "a_st", "a_exp", "a_rexp", "a_gh", "a_pt", "a_oh", "a_ge", "a_hh",
                 "v_chain", "v_r", "v_nm", "v_max", "v_prob", "v_g", "v_gl", "v_ol", "v_hf", "v_hl", "v_fin",
                 "v_var", "a_root", "v_xn", "a_xh", "v_xl", "p_bo", "v_comb", "dma_out")
        q = {n: sem(f"l1_{n}") for n in names}
        dma_y = [[sem(f"l1_dma_y{i}_{t}") for t in range(TPG)] for i in range(CHOSEN)]
        dma_sel = sem("l1_dma_sel")
        sel_raw = [gs[0:K1, :], hf[0:K1, :]]

        def rows_of(g, i, t):
            if g == 0 and i:
                return pt[t - 2][:] if t >= 2 else pr[:, 2 * t:2 * t + 2, :].rearrange("p a s -> p (a s)")
            return stage[:, t, :]
        block = inner.enter_context(nc.Block())

        events = []
        for g in range(NG + 1):
            mix = [[("mix", g - 1, j)] if g else [] for j in range(NR)]
            if g < NG:
                events += [("combine", g, 0)] + mix[0] + ([("combine", g, 1)] if g else []) + mix[1]
                events += [("stats", g, 0)] + mix[2] + [("norm", g, 0)] + mix[3] + [("xt", g, 0), ("xt", g, 1)]
                events += mix[4] + [("xt", g, 2), ("xt", g, 3)] + mix[5]
                events += [("qkv", g, 0), ("qkv", g, 1), ("qkv", g, 2), ("scores_t", g, 0), ("vt", g, 0)]
                events += [("route", g, 0), ("score", g, 0), ("score", g, 1), ("top", g, 0)]
                events += mix[6] + [("top", g, 1)] + mix[7] + [("top", g, 2)]
                events += [("probs", g, 0), ("probs", g, 1), ("attend", g, 0), ("gates", g, 0)]
            else:
                events += sum(mix, [])
        quiet = ("combine", "stats", "norm", "top")
        h_fill, h_taken, m_fill, m_taken = {}, [], {}, []
        for what, g, i in events:
            if what in ("qkv", "mix"):
                h_fill[what, g, i] = len(h_taken)
                h_taken.append((q["a_qkv"], 3 * g + i + 1) if what == "qkv" else (q["v_hf"], NR * g + i + 1))
            if what != "qkv" and what not in quiet:
                m_fill[what, g, i] = len(m_taken)
                m_taken.append({"route": (q["v_r"], g + 1), "vt": (q["a_vt"], g + 1),
                                "score": (q["a_exp"], 2 * g + i + 1), "scores_t": (q["a_st"], g + 1), "gates": (q["v_gl"], g + 1),
                                "probs": (q["a_pt"], 2 * g + i + 1), "attend": (q["v_ol"], g + 1),
                                "mix": (q["a_ge"], NR * g + i + 1), "xt": (q["v_xl"], KC * g + i + 1)}[what])

        @block.tensor
        def _(pe):
            def fill(banks, fills, taken, key):
                n = fills[key]
                if n >= 2:
                    pe.wait_ge(*taken[n - 2])
                return banks[n % 2]

            def outputs(g, i):
                pe.wait_ge(q["v_hl"], NR * g + i + 1)
                c = slice(i * D, (i + 1) * D)
                for t in range(TPG):
                    m = slice(t * P, (t + 1) * P)
                    ins = three_passes(pe, ob[t][:], [(hh[i % 2][:, m], hl[i % 2][:, m], wb[0][:, c], wb[1][:, c])],
                                       False, i == NR - 1)
                    if i == NR - 1:
                        ins.then_inc(q["pe_out"], 1)

            for what, g, i in events:
                if what in quiet:
                    continue
                if what == "qkv":
                    if i == 0:
                        pe.wait_ge(q["v_xl"], KC * (g + 1))
                    bank = fill(hb, h_fill, h_taken, (what, g, i))
                    parts = []
                    for k in range(KC):
                        c = slice(i * SEC + k * P, i * SEC + (k + 1) * P)
                        parts.append((wq[0][:, c], wq[1][:, c], xh[g % 2][:, k, :], xl[g % 2][:, k, :]))
                    three_passes(pe, bank[:], parts, True, True).then_inc(q["pe_h"], 1)
                    continue
                if what != "mix":
                    bank = fill(mb, m_fill, m_taken, (what, g, i))
                if what == "scores_t":
                    parts = [(wr[0][:, k * K1:(k + 1) * K1], wr[1][:, k * K1:(k + 1) * K1], xh[g % 2][:, k, :],
                              xl[g % 2][:, k, :]) for k in range(KC)]
                    ins = three_passes(pe, bank[0:K1, :], parts, True, True)
                elif what == "route":
                    pe.wait_ge(q["a_st"], g + 1)
                    for t in range(TPG):
                        ins = pe.transpose(bank[:, t * K1:(t + 1) * K1], st[:, t * P:(t + 1) * P], ident[0:K1, 0:K1])
                elif what == "xt":
                    if i == 0:
                        pe.wait_ge(q["v_xn"], g + 1)
                    for t in range(TPG):
                        ins = pe.transpose(bank[:, t * P:(t + 1) * P], stage[:, t, i * P:(i + 1) * P], ident[:])
                elif what == "vt":
                    pe.wait_ge(q["a_qkv"], 3 * g + 3)
                    for t in range(TPG):
                        ins = pe.transpose(bank[:, t * P:(t + 1) * P], qkv[:, 2, t * P:(t + 1) * P], ident[:])
                elif what == "score":
                    for t in range(2):
                        ins = pe.matmul(bank[:, t * S:(t + 1) * S], qkv[:, 0, i * S + t * P:i * S + (t + 1) * P],
                                        qkv[:, 1, i * S:(i + 1) * S], start=True, stop=True)
                elif what == "gates":
                    pe.wait_ge(q["v_g"], g + 1)
                    for t in range(TPG):
                        ins = pe.transpose(bank[0:K1, t * P:(t + 1) * P], gg[:, t, :], ident[:])
                elif what == "probs":
                    pe.wait_ge(q["v_prob"], 2 * g + i + 1)
                    for kt in range(2):
                        for t in range(2):
                            ins = pe.transpose(bank[:, kt * S + t * P:kt * S + (t + 1) * P],
                                               pr[:, 2 * i + t, kt * P:(kt + 1) * P], ident[:])
                elif what == "attend":
                    pe.wait_ge(q["a_pt"], 2 * g + 2)
                    for b in range(2):
                        for kt in range(2):
                            ins = pe.matmul(bank[:, b * S:(b + 1) * S], vt[:, 2 * b + kt, :],
                                            pt[b][:, kt * S:(kt + 1) * S], start=kt == 0, stop=kt == 1)
                elif what == "mix":
                    if i == 0:
                        pe.wait_ge(q["v_ol"], g + 1)
                        for t in range(TPG):
                            if g:
                                pe.wait_ge(q["v_fin"], TPG * (g - 1) + t + 1)
                            tt = slice(t * P, (t + 1) * P)
                            three_passes(pe, ob[t][:], [(oh[:, tt], ol[:, tt], wo[0], wo[1])], True, False)
                    bank = fill(hb, h_fill, h_taken, (what, g, i))
                    parts = []
                    for k in range(KC):
                        c = slice(i * SEC + k * P, i * SEC + (k + 1) * P)
                        parts.append((wa[0][:, c], wa[1][:, c], xh[g % 2][:, k, :], xl[g % 2][:, k, :]))
                    three_passes(pe, bank[:], parts, True, True).then_inc(q["pe_h"], 1)
                    bank = fill(mb, m_fill, m_taken, (what, g, i))
                    if i == 0:
                        pe.wait_ge(q["v_gl"], g + 1)
                        pe.wait_ge(s_sel, 2)
                    s = sel[:, i * P:(i + 1) * P]
                    pe.matmul(bank[:], s, gh[:], start=True, stop=False)
                    ins = pe.matmul(bank[:], s, gl[:], start=False, stop=True)
                ins.then_inc(q["pe_m"], 1)
                if what == "mix" and i:
                    outputs(g, i - 1)
                if what == "mix" and i == NR - 1:
                    outputs(g, i)

        @block.scalar
        def _(a):
            for what, g, i in events:
                if what == "stats":
                    a.wait_ge(q["v_var"], g + 1)
                    a.activation(root[:], var[:], ACT.Sqrt).then_inc(q["a_root"], 1)
                if (what, i) == ("top", 0):
                    a.wait_ge(q["v_nm"], g + 1)
                    for t in range(TPG):
                        ins = a.activation(gg[:, t, :], sr[:, t, :], ACT.Exp, bias=nm[:, t:t + 1])
                    ins.then_inc(q["a_rexp"], 1)
                if what in quiet or what == "route":
                    continue
                if what == "qkv":
                    n = h_fill[what, g, i]
                    if g == i == 0:
                        a.wait_ge(dma_c, 32)
                    a.wait_ge(q["pe_h"], n + 1)
                    if g:
                        a.wait_ge(q["pe_m"], m_fill["attend", g - 1, 0] + 1)
                    a.activation(qkv[:, i, :], hb[n % 2][:], ACT.Identity, bias=bq[:, i:i + 1]).then_inc(q["a_qkv"], 1)
                    continue
                n = m_fill[what, g, i]
                bank = mb[n % 2]
                if what == "score":
                    a.wait_ge(q["v_max"], 2 * g + i + 1)
                    for t in range(2):
                        ins = a.activation(pr[:, 2 * i + t, :], bank[:, t * S:(t + 1) * S], ACT.Exp,
                                           bias=mx[:, 2 * i + t:2 * i + t + 1], scale=SCALE,
                                           accum_out=sm[:, 2 * i + t:2 * i + t + 1])
                    ins.then_inc(q["a_exp"], 1)
                    continue
                a.wait_ge(q["pe_m"], n + 1)
                if what == "xt":
                    a.copy(xh[g % 2][:, i, :], bank[:]).then_inc(q["a_xh"], 1)
                elif what == "scores_t":
                    a.copy(st, bank[0:K1, :]).then_inc(q["a_st"], 1)
                elif what == "vt":
                    a.copy(vt[:].rearrange("p t d -> p (t d)"), bank[:]).then_inc(q["a_vt"], 1)
                elif what == "gates":
                    a.copy(gh[:], bank[0:K1, :]).then_inc(q["a_gh"], 1)
                elif what == "probs":
                    a.copy(pt[i][:], bank[:]).then_inc(q["a_pt"], 1)
                elif what == "attend":
                    a.copy(oh[:], bank[:]).then_inc(q["a_oh"], 1)
                elif what == "mix":
                    a.copy(gs[:], bank[:]).then_inc(q["a_ge"], 1)
                    a.wait_ge(q["v_hf"], NR * g + i + 1)
                    a.copy(hh[i % 2][:], hf[:]).then_inc(q["a_hh"], 1)

        @block.vector
        def _(v):
            c = Chain(v, q["v_chain"])
            for what, g, i in events:
                if what in ("vt", "qkv", "probs", "scores_t"):
                    continue
                if what == "combine":
                    for t in range(TPG):
                        tt = g * TPG + t
                        for choice in (range(CHOSEN) if g == 0 else [i]):
                            v.wait_ge(dma_y[choice][t], 16 * (g + 1))
                            if choice:
                                v.wait_ge(q["v_comb"], 2 * t + 1 if g == 0 else TPG * (2 * g + 1))
                            v.scalar_tensor_tensor(acc[:, tt, :], rows_of(g, choice, t), gate_of[:, choice, tt:tt + 1],
                                                   acc[:, tt, :], ALU.mult, ALU.add).then_inc(q["v_comb"], 1)
                        if g == 0 and t:
                            v.wait_ge(q["v_comb"], 2 * t)
                            v.bn_stats(stat[:, t - 1, :], acc[:, t - 1, :])
                    continue
                if what == "stats":
                    tiles = range(g * TPG, (g + 1) * TPG)
                    v.wait_ge(q["v_comb"], 2 * TPG * (g + 1))
                    for t in tiles if g else [TPG - 1]:
                        ins = v.bn_stats(stat[:, t % TPG, :], acc[:, t, :])
                    c.link(ins)
                    for t in range(TPG):
                        ins = v.bn_aggr(mv[:, t, :], stat[:, t, :])
                    c.link(ins)
                    v.tensor_scalar(var[:], mv[:, :, 1], EPS, None, ALU.add).then_inc(q["v_var"], 1)
                    continue
                if what == "norm":
                    v.wait_ge(q["v_var"], g + 1)
                    rsqrt(v, q["a_root"], g + 1, c, var[:], root[:], rstd[:])
                    for t in range(g * TPG, (g + 1) * TPG):
                        ins = v.tensor_scalar(stage[:, t % TPG, :], acc[:, t, :], mv[:, t % TPG, 0:1],
                                              rstd[:, t % TPG:t % TPG + 1], ALU.subtract, ALU.mult)
                    ins.then_inc(q["v_xn"], 1)
                    continue
                if what == "top" and i == 0:
                    for t in range(TPG):
                        ins = v.max(top8[:, 0, t, :], sr[:, t, :])
                    c.link(ins)
                    v.tensor_scalar(nm[:], top8[:, 0, :, 0], -1.0, None, ALU.mult).then_inc(q["v_nm"], 1)
                    for t in range(TPG):
                        ins = v.match_replace(left[0][:, t, :], top8[:, 0, t, :], sr[:, t, :], NEG)
                    c.link(ins)
                    continue
                if what == "top" and i == 1:
                    for t in range(TPG):
                        ins = v.max(top8[:, 1, t, :], left[0][:, t, :])
                    c.link(ins)
                    for t in range(TPG):
                        ins = v.match_replace(left[1][:, t, :], top8[:, 1, t, :], left[0][:, t, :], NEG)
                    c.link(ins)
                    c.link(v.tensor_tensor(left[0][:], left[1][:], sr[:], ALU.not_equal))
                    continue
                if what == "top":
                    v.wait_ge(q["a_rexp"], g + 1)
                    c.link(v.tensor_tensor(gg[:], gg[:], left[0][:], ALU.mult))
                    c.link(v.tensor_reduce(rz[:], gg[:], AX_X, ALU.add))
                    c.link(v.reciprocal(rz[:], rz[:]))
                    for t in range(TPG):
                        ins = v.tensor_scalar(gg[:, t, :], gg[:, t, :], rz[:, t:t + 1], 2.0, ALU.mult, ALU.mult)
                    ins.then_inc(q["v_g"], 1)
                    continue
                n = m_fill[what, g, i]
                bank = mb[n % 2]
                if what == "route":
                    v.wait_ge(q["pe_m"], n + 1)
                    v.tensor_copy(sr[:].rearrange("p t k -> p (t k)"), bank[:, 0:TPG * K1]).then_inc(q["v_r"], 1)
                    v.wait_ge(q["v_r"], g + 1)
                elif what == "score":
                    v.wait_ge(q["pe_m"], n + 1)
                    t2 = slice(2 * i, 2 * i + 2)
                    c.link(v.tensor_reduce(mx[:, t2], bank[:].rearrange("p (t s) -> p t s", t=2), AX_X, ALU.max))
                    v.tensor_scalar(mx[:, t2], mx[:, t2], -SCALE, None, ALU.mult).then_inc(q["v_max"], 1)
                    v.wait_ge(q["a_exp"], 2 * g + i + 1)
                    c.link(v.reciprocal(sm[:, t2], sm[:, t2]))
                    for t in range(2):
                        ins = v.tensor_scalar(pr[:, 2 * i + t, :], pr[:, 2 * i + t, :], sm[:, 2 * i + t:2 * i + t + 1],
                                              None, ALU.mult)
                    ins.then_inc(q["v_prob"], 1)
                elif what == "xt":
                    v.wait_ge(q["a_xh"], KC * g + i + 1)
                    v.tensor_tensor(xl[g % 2][:, i, :], bank[:], xh[g % 2][:, i, :].bitcast(F32),
                                    ALU.subtract).then_inc(q["v_xl"], 1)
                elif what == "gates":
                    v.wait_ge(q["a_gh"], g + 1)
                    v.tensor_tensor(gl[:], bank[0:K1, :], gh[:].bitcast(F32),
                                    ALU.subtract).then_inc(q["v_gl"], 1)
                elif what == "attend":
                    v.wait_ge(q["a_oh"], g + 1)
                    v.tensor_tensor(ol[:], bank[:], oh[:].bitcast(F32), ALU.subtract).then_inc(q["v_ol"], 1)
                elif what == "mix":
                    h = h_fill[what, g, i]
                    v.wait_ge(q["pe_h"], h + 1)
                    v.wait_ge(q["a_ge"], NR * g + i + 1)
                    if NR * g + i:
                        v.wait_ge(q["v_hl"], NR * g + i)
                    v.tensor_tensor(hf[:], hb[h % 2][:], gs[:], ALU.mult).then_inc(q["v_hf"], 1)
                    v.wait_ge(q["a_hh"], NR * g + i + 1)
                    v.tensor_tensor(hl[i % 2][:], hf[:], hh[i % 2][:].bitcast(F32),
                                    ALU.subtract).then_inc(q["v_hl"], 1)
                    if i == NR - 1:
                        for t in range(TPG):
                            tile = acc[:, g * TPG + t, :]
                            v.wait_ge(q["pe_out"], g * TPG + t + 1)
                            v.wait_ge(q["p_bo"], g * TPG + t + 1)
                            v.tensor_tensor(tile, ob[t][:], tile, ALU.add).then_inc(q["v_fin"], 1)

        @block.gpsimd
        def _(pool):
            def gather(g, i, tiles=range(TPG)):
                if g and i:
                    pool.wait_ge(q["v_comb"], TPG * (2 * g + 1))
                elif g:
                    pool.wait_ge(q["pe_m"], m_fill["xt", g - 1, KC - 1] + 1)
                for t in tiles:
                    tt = g * TPG + t
                    pool.indirect_dma_start(
                        rows_of(g, i, t), None, y_slots,
                        bass.IndirectOffsetOnAxis(ap=slot_of[:, i, tt:tt + 1], axis=0)).then_inc(dma_y[i][t], 16)

            for t in range(TPG):
                for i in range(CHOSEN):
                    gather(0, i, [t])
            pool.wait_ge(dma_sel, 32)
            for j in range(2):
                pool.tensor_copy(sel[:, j * D:(j + 1) * D], sel_raw[j]).then_inc(s_sel, 1)
            pool.wait_ge(dma_c, 32)
            for g in range(NG):
                for t in range(g * TPG, (g + 1) * TPG):
                    if t % TPG == 0:
                        pool.wait_ge(q["v_xn"], g + 1)
                    pool.tensor_tensor(acc[:, t, :], acc[:, t, :], bo[:], ALU.add).then_inc(q["p_bo"], 1)
                if g + 1 < NG:
                    gather(g + 1, 0)
                    gather(g + 1, 1)

        @block.sync
        def _(sp):
            sp.dma_start(bq[:], b_qkv).then_inc(dma_c, 16)
            sp.dma_start(bo[:], b_o.partition_broadcast(P)).then_inc(dma_c, 16)
            for j in range(2):
                sp.dma_start(sel_raw[j], sel_in[:, j * D:(j + 1) * D]).then_inc(dma_sel, 16)
            for t in range(NT):
                sp.wait_ge(q["v_fin"], t + 1)
                sp.dma_start(out_tiles[t], acc[:, t, :]).then_inc(q["dma_out"], 16)
            sp.wait_ge(q["dma_out"], 16 * NT)


def decay_tables():
    slope = (1.0 / 2.0 ** (8.0 / H)) ** (np.arange(H) + 1.0) * (1.0 - 1.0 / (31 + 1e-5) + 1e-5)
    n_m = np.arange(S)[None, :] - np.arange(P)[:, None]
    d = np.where(n_m >= 0, np.exp(-slope[:, None, None] * np.maximum(n_m, 0)), 0.0).astype(np.float32)
    d = np.concatenate([d, d[:, :, :P]], 2)
    return np.ascontiguousarray(d.reshape(NP_, 2, P, MC).transpose(0, 2, 1, 3))


def route_consts():
    def rows(x):
        return np.broadcast_to(np.asarray(x, np.float32), (P, len(x)))

    return np.concatenate([
        np.triu(np.ones((P, P), np.float32), 1), np.ones((P, P), np.float32),
        rows(np.tril(np.ones((E, E)), -1).reshape(E * E)), rows(np.arange(NTHR) * SLOT_T),
        rows(np.arange(NTILES))], 1)


def chunks(w):
    return w.reshape(KC, P, -1).transpose(1, 0, 2)


def layouts(a):
    qkv = a["L0_attn_qkv_w"].reshape(H, 3, DH, KC, P).transpose(0, 1, 4, 3, 2)
    gate = a["L0_attn_gate_w"].reshape(H, DH, KC, P).transpose(0, 3, 2, 1)
    sections = [w[h::2].reshape(NP_, P, SEC) for h in range(2) for w in (qkv[:, 0], qkv[:, 1], gate)]
    v = np.stack([qkv[0::2, 2], qkv[1::2, 2]], 3).reshape(NP_, P, 2 * SEC)

    def first(w):
        return w.reshape(-1, KC, P, INTER).transpose(0, 2, 1, 3).reshape(-1, P, SEC)

    biases = [a[f"L0_ffn_eb{i}"][:, :, None] for i in (1, 2)]
    ex = np.concatenate([first(a["L0_ffn_ew1"]), first(a["L0_ffn_ew2"])] + biases + [a["L0_ffn_ew3"]], 2)
    halves = [a[n].reshape(KC, P, 2, INTER).transpose(2, 1, 0, 3).reshape(2, P, SEC) for n in ("L0_ffn_sw1", "L0_ffn_sw2")]
    wqkv = a["L1_attn_Wqkv"].reshape(KC, P, 3, DH).transpose(1, 2, 0, 3).reshape(P, 3 * SEC)
    wa = a["L1_ffn_A"].reshape(NR, P, KC, P).transpose(3, 0, 2, 1).reshape(P, NR * SEC)
    wb = a["L1_ffn_B"].transpose(0, 2, 1).reshape(NR, P, D).transpose(1, 0, 2).reshape(P, NR * D)
    return {
        "x": a["L0_attn_hidden_states"],
        "w_pairs": np.concatenate(sections + [v], 2),
        "o_pairs": a["L0_attn_out_w"].T.reshape(NP_, 2, P, D).transpose(0, 2, 1, 3).reshape(NP_, P, OCOLS),
        "decay": decay_tables(),
        "norm_w": a["L0_attn_norm_w"].reshape(H, DH).T,
        "router_w": chunks(a["L0_ffn_router_w"]).reshape(P, KC * E),
        "router_rows": np.concatenate([a["L0_ffn_router_b"], a["L0_ffn_router_bias"]]),
        "route_consts": route_consts(),
        "zeros": np.zeros(SLOTS, np.int32),
        "token_ids": np.arange(T, dtype=np.int32).reshape(NT, P).T,
        "shared_w": np.concatenate([halves[0][0], halves[1][0], halves[0][1], halves[1][1]], 1),
        "shared_o": a["L0_ffn_sw3"].reshape(2, INTER, D).transpose(1, 0, 2).reshape(P, OCOLS),
        "shared_b": np.concatenate([a["L0_ffn_sb1"].reshape(2, INTER), a["L0_ffn_sb2"].reshape(2, INTER)]).T,
        "ex": ex,
        "b3": np.concatenate([a["L0_ffn_eb3"], a["L0_ffn_sb3"][None]], 0),
        "l1_w": np.concatenate([wqkv, chunks(a["L1_ffn_Wr"].T).reshape(P, KC * K1), a["L1_attn_Wo"], wa, wb,
                                np.zeros((P, L_ALL - L_USED), np.float32)], 1),
        "b_qkv": a["L1_attn_bqkv"].reshape(3, DH).T,
        "b_o": a["L1_attn_bo"],
        "sel": np.repeat(np.eye(K1, dtype=np.float32), RANK, axis=1),
        "ident_in": np.eye(P, dtype=np.float32),
    }


def kernel(**inputs):
    import concourse.bacc as bacc
    from concourse.bass_utils import run_bass_kernel_spmd

    nc = bacc.Bacc("TRN2", target_bir_lowering=False, num_devices=1)
    arrays, aps = {}, {}
    for name, a in layouts({k: np.asarray(v) for k, v in inputs.items()}).items():
        a = np.ascontiguousarray(a)
        arrays[f"in_{name}_dram"] = a
        aps[name] = nc.dram_tensor(f"in_{name}_dram", a.shape, mybir.dt.from_np(a.dtype), kind="ExternalInput").ap()
    aps["out"] = nc.dram_tensor("out_dram", (B, S, D), F32, kind="ExternalOutput").ap()
    two_layers(nc, **aps)
    return run_bass_kernel_spmd(nc, [arrays], core_ids=[0]).results[0]["out_dram"]
```
